# Optimizing a Trainium2 kernel written in Bass

```python
import numpy as np
import jax
import jax.numpy as jnp

def _softmax(x, axis=-1):
    return jax.nn.softmax(x, axis=axis)

def _gelu(x):
    return jax.nn.gelu(x, approximate=True)

def _silu(x):
    return jax.nn.silu(x)

def _sigmoid(x):
    return jax.nn.sigmoid(x)

def _layernorm(x, axis=-1, eps=1e-05):
    m = jnp.mean(x, axis=axis, keepdims=True)
    v = jnp.var(x, axis=axis, keepdims=True)
    return (x - m) / jnp.sqrt(v + eps)

def _scatter_add(tgt, idx, src, axis=0):
    return tgt.at[idx].add(src)

def _segment_sum(src, seg, n):
    return jax.ops.segment_sum(src, seg, n)
kernel_name = 'mk_seq_preln_d2_jaxref_r4_67122d'

def setup_inputs(seed: int=0):
    np.random.seed(seed)
    _w = jnp.asarray

    def _L0_attn_setup():
        import jax, jax.numpy as jnp
        import numpy as np
        GROUP = 64
        MAX_REL = 32

        def _silu(x):
            return x * jax.nn.sigmoid(x)

        def _ln(x, w, b, eps=1e-05):
            m = x.mean(-1, keepdims=True)
            v = ((x - m) ** 2).mean(-1, keepdims=True)
            return (x - m) / jnp.sqrt(v + eps) * w + b

        def _rope(x):
            n, d = (x.shape[-2], x.shape[-1])
            half = d // 2
            pos = jnp.arange(n, dtype=x.dtype)
            inv_freq = 10000.0 ** (-jnp.arange(half, dtype=x.dtype) / half)
            sinusoid = pos[:, None] * inv_freq[None, :]
            sin, cos = (jnp.sin(sinusoid), jnp.cos(sinusoid))
            x1, x2 = (x[..., :half], x[..., half:])
            return jnp.concatenate([x1 * cos - x2 * sin, x2 * cos + x1 * sin], axis=-1)
        key = jax.random.key(seed)
        ks = jax.random.split(key, 8)
        B, N, D, QK, H = (4, 1024, 256, 64, 512)
        s = 0.02
        return {'x': jax.random.normal(ks[0], (B, N, D), dtype=jnp.float32), 'ln1_w': jnp.ones((D,), jnp.float32), 'ln1_b': jnp.zeros((D,), jnp.float32), 'Wqk': jax.random.normal(ks[1], (QK, D), jnp.float32) * s, 'bqk': jnp.zeros((QK,), jnp.float32), 'Wv': jax.random.normal(ks[2], (H, D), jnp.float32) * s, 'bv': jnp.zeros((H,), jnp.float32), 'Wg': jax.random.normal(ks[3], (H, D), jnp.float32) * s, 'bg': jnp.zeros((H,), jnp.float32), 'Wo': jax.random.normal(ks[4], (D, H), jnp.float32) * s, 'bo': jnp.zeros((D,), jnp.float32), 'ln2_w': jnp.ones((D,), jnp.float32), 'ln2_b': jnp.zeros((D,), jnp.float32), 'gamma': jax.random.normal(ks[5], (4, QK), jnp.float32) * 0.02, 'beta': jnp.zeros((4, QK), jnp.float32), 'pos_emb': jax.random.normal(ks[6], (2 * MAX_REL + 1,), jnp.float32)}
    _L0_attn_in = _L0_attn_setup()

    def _L0_ffn_setup():
        import jax, jax.numpy as jnp
        import numpy as np
        E, K, D, H = (8, 2, 256, 512)
        B, S = (1, 256)

        def _grouped_swiglu(x_sorted, counts, w1, w2, w3):
            if hasattr(jax.lax, 'ragged_dot'):
                gs = counts.astype(jnp.int32)
                h = jax.nn.silu(jax.lax.ragged_dot(x_sorted, w1, gs)) * jax.lax.ragged_dot(x_sorted, w3, gs)
                return jax.lax.ragged_dot(h, w2, gs)
            pos = jnp.arange(x_sorted.shape[0])
            eid = jnp.searchsorted(jnp.cumsum(counts), pos, side='right')
            out = jnp.zeros((x_sorted.shape[0], w2.shape[-1]), x_sorted.dtype)
            for e in range(w1.shape[0]):
                xm = jnp.where((eid == e)[:, None], x_sorted, 0.0)
                he = jax.nn.silu(xm @ w1[e]) * (xm @ w3[e])
                out = out + he @ w2[e]
            return out
        key = jax.random.key(seed)
        k0, k1, k2, k3, k4 = jax.random.split(key, 5)
        sD = 1.0 / np.sqrt(D)
        sH = 1.0 / np.sqrt(H)
        return {'hidden_states': jax.random.normal(k0, (B, S, D), jnp.float32), 'gate_w': jax.random.normal(k1, (E, D), jnp.float32) * sD, 'w1': jax.random.normal(k2, (E, D, H), jnp.float32) * sD, 'w2': jax.random.normal(k3, (E, H, D), jnp.float32) * sH, 'w3': jax.random.normal(k4, (E, D, H), jnp.float32) * sD}
    _L0_ffn_in = _L0_ffn_setup()

    def _L1_attn_setup():
        import jax, jax.numpy as jnp
        import numpy as np
        from math import sqrt
        D_MODEL = 256
        NUM_HEADS = 16
        D_HEAD = D_MODEL // NUM_HEADS
        THETA = 10000.0

        def _rope(x, freqs):
            xr = x[..., ::2]
            xi = x[..., 1::2]
            cos = jnp.cos(freqs)
            sin = jnp.sin(freqs)
            yr = xr * cos - xi * sin
            yi = xr * sin + xi * cos
            return jnp.stack([yr, yi], axis=-1).reshape(x.shape)
        key = jax.random.key(seed)
        k1, k2, k3 = jax.random.split(key, 3)
        X = jax.random.normal(k1, (4, 512, D_MODEL), dtype=jnp.float32)
        std_kqv = sqrt(2.0 / (D_MODEL + 3 * D_MODEL))
        W_KQV = std_kqv * jax.random.truncated_normal(k2, -3.0, 3.0, (3 * D_MODEL, D_MODEL), dtype=jnp.float32)
        std_o = sqrt(2.0 / (D_MODEL + D_MODEL))
        W_O = std_o * jax.random.truncated_normal(k3, -3.0, 3.0, (D_MODEL, D_MODEL), dtype=jnp.float32)
        return {'X': X, 'W_KQV': W_KQV, 'W_O': W_O}
    _L1_attn_in = _L1_attn_setup()

    def _L1_ffn_setup():
        import jax, jax.numpy as jnp
        import numpy as np
        B, S, H, E, K = (2, 256, 256, 8, 2)
        F = 4 * H
        key = jax.random.key(seed)
        ks = jax.random.split(key, 8)
        std = 0.02
        return {'x': jax.random.normal(ks[0], (B, S, H), jnp.float32), 'gate_w': jax.random.normal(ks[1], (E, H), jnp.float32) * (std / np.sqrt(H)), 'gate_bias': jnp.zeros((E,), jnp.float32), 'Wu': jax.random.normal(ks[2], (E, F, H), jnp.float32) * std, 'bu': jnp.zeros((E, F), jnp.float32), 'Wd': jax.random.normal(ks[3], (E, H, F), jnp.float32) * std, 'bd': jnp.zeros((E, H), jnp.float32), 'sWu': jax.random.normal(ks[4], (F, H), jnp.float32) * std, 'sbu': jnp.zeros((F,), jnp.float32), 'sWd': jax.random.normal(ks[5], (H, F), jnp.float32) * std, 'sbd': jnp.zeros((H,), jnp.float32)}
    _L1_ffn_in = _L1_ffn_setup()
    _d = {'L0_attn_x': _L0_attn_in['x'], 'L0_attn_ln1_w': _L0_attn_in['ln1_w'], 'L0_attn_ln1_b': _L0_attn_in['ln1_b'], 'L0_attn_Wqk': _L0_attn_in['Wqk'], 'L0_attn_bqk': _L0_attn_in['bqk'], 'L0_attn_Wv': _L0_attn_in['Wv'], 'L0_attn_bv': _L0_attn_in['bv'], 'L0_attn_Wg': _L0_attn_in['Wg'], 'L0_attn_bg': _L0_attn_in['bg'], 'L0_attn_Wo': _L0_attn_in['Wo'], 'L0_attn_bo': _L0_attn_in['bo'], 'L0_attn_ln2_w': _L0_attn_in['ln2_w'], 'L0_attn_ln2_b': _L0_attn_in['ln2_b'], 'L0_attn_gamma': _L0_attn_in['gamma'], 'L0_attn_beta': _L0_attn_in['beta'], 'L0_attn_pos_emb': _L0_attn_in['pos_emb'], 'L0_ffn_gate_w': _L0_ffn_in['gate_w'], 'L0_ffn_w1': _L0_ffn_in['w1'], 'L0_ffn_w2': _L0_ffn_in['w2'], 'L0_ffn_w3': _L0_ffn_in['w3'], 'L1_attn_W_KQV': _L1_attn_in['W_KQV'], 'L1_attn_W_O': _L1_attn_in['W_O'], 'L1_ffn_gate_w': _L1_ffn_in['gate_w'], 'L1_ffn_gate_bias': _L1_ffn_in['gate_bias'], 'L1_ffn_Wu': _L1_ffn_in['Wu'], 'L1_ffn_bu': _L1_ffn_in['bu'], 'L1_ffn_Wd': _L1_ffn_in['Wd'], 'L1_ffn_bd': _L1_ffn_in['bd'], 'L1_ffn_sWu': _L1_ffn_in['sWu'], 'L1_ffn_sbu': _L1_ffn_in['sbu'], 'L1_ffn_sWd': _L1_ffn_in['sWd'], 'L1_ffn_sbd': _L1_ffn_in['sbd']}
    _x0 = _d['L0_attn_x']
    _d['L0_attn_x'] = jax.random.normal(jax.random.fold_in(jax.random.key(seed), 1), (4, 1024, 256), dtype=_x0.dtype)
    del _x0
    return _d

def reference(L0_attn_x, L0_attn_ln1_w, L0_attn_ln1_b, L0_attn_Wqk, L0_attn_bqk, L0_attn_Wv, L0_attn_bv, L0_attn_Wg, L0_attn_bg, L0_attn_Wo, L0_attn_bo, L0_attn_ln2_w, L0_attn_ln2_b, L0_attn_gamma, L0_attn_beta, L0_attn_pos_emb, L0_ffn_gate_w, L0_ffn_w1, L0_ffn_w2, L0_ffn_w3, L1_attn_W_KQV, L1_attn_W_O, L1_ffn_gate_w, L1_ffn_gate_bias, L1_ffn_Wu, L1_ffn_bu, L1_ffn_Wd, L1_ffn_bd, L1_ffn_sWu, L1_ffn_sbu, L1_ffn_sWd, L1_ffn_sbd):

    def _L0_attn_ref(x, ln1_w, ln1_b, Wqk, bqk, Wv, bv, Wg, bg, Wo, bo, ln2_w, ln2_b, gamma, beta, pos_emb):
        import jax, jax.numpy as jnp
        import numpy as np
        GROUP = 64
        MAX_REL = 32

        def _silu(x):
            return x * jax.nn.sigmoid(x)

        def _ln(x, w, b, eps=1e-05):
            m = x.mean(-1, keepdims=True)
            v = ((x - m) ** 2).mean(-1, keepdims=True)
            return (x - m) / jnp.sqrt(v + eps) * w + b

        def _rope(x):
            n, d = (x.shape[-2], x.shape[-1])
            half = d // 2
            pos = jnp.arange(n, dtype=x.dtype)
            inv_freq = 10000.0 ** (-jnp.arange(half, dtype=x.dtype) / half)
            sinusoid = pos[:, None] * inv_freq[None, :]
            sin, cos = (jnp.sin(sinusoid), jnp.cos(sinusoid))
            x1, x2 = (x[..., :half], x[..., half:])
            return jnp.concatenate([x1 * cos - x2 * sin, x2 * cos + x1 * sin], axis=-1)
        b, n, d = x.shape
        G = GROUP
        x = _ln(x, ln1_w, ln1_b)
        qk = _silu(x @ Wqk.T + bqk)
        v = _silu(x @ Wv.T + bv)
        heads = qk[..., None, :] * gamma + beta
        quad_q, lin_q, quad_k, lin_k = (heads[..., i, :] for i in range(4))
        quad_q, lin_q, quad_k, lin_k = map(_rope, (quad_q, lin_q, quad_k, lin_k))
        g = n // G
        rs = lambda t: t.reshape(b, g, G, t.shape[-1])
        qq, lq, qkk, lk, vg = map(rs, (quad_q, lin_q, quad_k, lin_k, v))
        idx = jnp.arange(G)
        dist = jnp.clip(jnp.abs(idx[:, None] - idx[None, :]), 0, MAX_REL)
        bias = pos_emb[dist]
        quad_att = jnp.einsum('bgid,bgjd->bgij', qq, qkk) / G + bias
        attn = jax.nn.relu(quad_att) ** 2
        quad_out = jnp.einsum('bgij,bgje->bgie', attn, vg)
        lin_kv = jnp.einsum('bgnd,bgne->bde', lk, vg) / n
        lin_out = jnp.einsum('bgnd,bde->bgne', lq, lin_kv)
        qo = quad_out.reshape(b, n, -1)
        lo = lin_out.reshape(b, n, -1)
        gate = _silu(x @ Wg.T + bg)
        out = gate * (qo + lo)
        out = out @ Wo.T + bo
        return _ln(out, ln2_w, ln2_b)

    def _L0_ffn_ref(hidden_states, gate_w, w1, w2, w3):
        import jax, jax.numpy as jnp
        import numpy as np
        E, K, D, H = (8, 2, 256, 512)
        B, S = (1, 256)

        def _grouped_swiglu(x_sorted, counts, w1, w2, w3):
            if hasattr(jax.lax, 'ragged_dot'):
                gs = counts.astype(jnp.int32)
                h = jax.nn.silu(jax.lax.ragged_dot(x_sorted, w1, gs)) * jax.lax.ragged_dot(x_sorted, w3, gs)
                return jax.lax.ragged_dot(h, w2, gs)
            pos = jnp.arange(x_sorted.shape[0])
            eid = jnp.searchsorted(jnp.cumsum(counts), pos, side='right')
            out = jnp.zeros((x_sorted.shape[0], w2.shape[-1]), x_sorted.dtype)
            for e in range(w1.shape[0]):
                xm = jnp.where((eid == e)[:, None], x_sorted, 0.0)
                he = jax.nn.silu(xm @ w1[e]) * (xm @ w3[e])
                out = out + he @ w2[e]
            return out
        x = hidden_states.reshape(-1, D)
        N = x.shape[0]
        scores = jax.nn.softmax(x @ gate_w.T, axis=-1)
        top_scores, sel = jax.lax.top_k(scores, K)
        sel_flat = sel.T.reshape(-1)
        scores_flat = top_scores.T.reshape(-1)
        order = jnp.argsort(sel_flat, stable=True)
        tok_sorted = order % N
        scores_sorted = scores_flat[order]
        counts = jnp.bincount(sel_flat, length=E)
        x_sorted = x[tok_sorted]
        y = _grouped_swiglu(x_sorted, counts, w1, w2, w3)
        weighted = y * scores_sorted[:, None]
        out = jnp.zeros((N, D), x.dtype).at[tok_sorted].add(weighted)
        return out.reshape(hidden_states.shape)

    def _L1_attn_ref(X, W_KQV, W_O):
        import jax, jax.numpy as jnp
        import numpy as np
        from math import sqrt
        D_MODEL = 256
        NUM_HEADS = 16
        D_HEAD = D_MODEL // NUM_HEADS
        THETA = 10000.0

        def _rope(x, freqs):
            xr = x[..., ::2]
            xi = x[..., 1::2]
            cos = jnp.cos(freqs)
            sin = jnp.sin(freqs)
            yr = xr * cos - xi * sin
            yi = xr * sin + xi * cos
            return jnp.stack([yr, yi], axis=-1).reshape(x.shape)
        B, S, D = X.shape
        H, d = (NUM_HEADS, D_HEAD)
        KQV = jnp.einsum('bsd,ed->bse', X, W_KQV)
        K, Q, V = jnp.split(KQV, [D, 2 * D], axis=-1)

        def to_heads(t):
            return t.reshape(B, S, H, d).transpose(0, 2, 1, 3)
        K, Q, V = (to_heads(K), to_heads(Q), to_heads(V))
        inv_freq = 1.0 / THETA ** (jnp.arange(0, d, 2, dtype=jnp.float32) / d)
        pos = jnp.arange(S, dtype=jnp.float32)
        freqs = pos[:, None] * inv_freq[None, :]
        Q = _rope(Q, freqs)
        K = _rope(K, freqs)
        scores = jnp.einsum('bhqd,bhkd->bhqk', Q, K) / sqrt(d)
        causal = jnp.triu(jnp.ones((S, S), dtype=bool), k=1)
        scores = jnp.where(causal, -jnp.inf, scores)
        probs = jax.nn.softmax(scores, axis=-1)
        heads = jnp.einsum('bhqk,bhkd->bhqd', probs, V)
        acts = heads.transpose(0, 2, 1, 3).reshape(B, S, D)
        return jnp.einsum('bsd,ed->bse', acts, W_O)

    def _L1_ffn_ref(x, gate_w, gate_bias, Wu, bu, Wd, bd, sWu, sbu, sWd, sbd):
        import jax, jax.numpy as jnp
        import numpy as np
        B, S, H, E, K = (2, 256, 256, 8, 2)
        F = 4 * H
        b, s, h = x.shape
        x_flat = x.reshape(-1, h)
        T = x_flat.shape[0]
        scores = jax.nn.sigmoid(x_flat @ gate_w.T + gate_bias)
        top_scores, top_idx = jax.lax.top_k(scores, K)
        top_scores = top_scores / (top_scores.sum(-1, keepdims=True) + 1e-06)
        w = jnp.zeros((T, E), x.dtype).at[jnp.arange(T)[:, None], top_idx].add(top_scores)
        h1 = jnp.einsum('th,efh->etf', x_flat, Wu) + bu[:, None, :]
        a1 = jax.nn.gelu(h1, approximate=False)
        y = jnp.einsum('etf,ehf->eth', a1, Wd) + bd[:, None, :]
        combined = jnp.einsum('te,eth->th', w, y)
        sh = jax.nn.gelu(x_flat @ sWu.T + sbu, approximate=False)
        shared = (sh @ sWd.T + sbd) * 0.1
        return (combined + shared).reshape(b, s, h)
    x = L0_attn_x
    x = x + _L0_attn_ref(_layernorm(x, axis=-1), L0_attn_ln1_w, L0_attn_ln1_b, L0_attn_Wqk, L0_attn_bqk, L0_attn_Wv, L0_attn_bv, L0_attn_Wg, L0_attn_bg, L0_attn_Wo, L0_attn_bo, L0_attn_ln2_w, L0_attn_ln2_b, L0_attn_gamma, L0_attn_beta, L0_attn_pos_emb)
    x = x + _L0_ffn_ref(_layernorm(x, axis=-1), L0_ffn_gate_w, L0_ffn_w1, L0_ffn_w2, L0_ffn_w3)
    x = x + _L1_attn_ref(_layernorm(x, axis=-1), L1_attn_W_KQV, L1_attn_W_O)
    x = x + _L1_ffn_ref(_layernorm(x, axis=-1), L1_ffn_gate_w, L1_ffn_gate_bias, L1_ffn_Wu, L1_ffn_bu, L1_ffn_Wd, L1_ffn_bd, L1_ffn_sWu, L1_ffn_sbu, L1_ffn_sWd, L1_ffn_sbd)
    return x

_drawn_inputs = setup_inputs


def setup_inputs(seed=0):
    import zlib

    import numpy as np

    out = dict(_drawn_inputs(seed))
    spreads = {'L0_attn_ln1_w': (1.0, 0.2),
     'L0_attn_ln1_b': (0.0, 0.1),
     'L0_attn_bqk': (0.0, 2.0),
     'L0_attn_bv': (0.0, 0.1),
     'L0_attn_bg': (0.0, 0.1),
     'L0_attn_bo': (0.0, 0.1),
     'L0_attn_ln2_w': (1.0, 0.2),
     'L0_attn_ln2_b': (0.0, 0.1),
     'L0_attn_beta': (0.0, 0.8),
     'L1_ffn_gate_bias': (0.0, 0.1),
     'L1_ffn_bu': (0.0, 0.492),
     'L1_ffn_bd': (0.0, 0.1),
     'L1_ffn_sbu': (0.0, 0.8),
     'L1_ffn_sbd': (0.0, 0.8)}
    factors = {'L0_attn_Wqk': 8.0, 'L0_attn_gamma': 8.0, 'L1_ffn_sWu': 7.755, 'L1_ffn_sWd': 7.3}
    for name, (base, spread) in spreads.items():
        noise = np.random.default_rng([zlib.crc32(name.encode()), seed]).standard_normal(out[name].shape)
        drawn = base * np.exp(spread * noise) if base else spread * noise
        out[name] = jnp.asarray(drawn.astype(out[name].dtype))
    for name, factor in factors.items():
        out[name] = (out[name] * factor).astype(out[name].dtype)
    return out
```

```python
from contextlib import ExitStack

import concourse.bass as bass
import numpy as np
from concourse import mybir

F32 = mybir.dt.float32
BF16 = mybir.dt.bfloat16
U32 = mybir.dt.uint32
I32 = mybir.dt.int32
ALU = mybir.AluOpType
ACT = mybir.ActivationFunctionType
AX = mybir.AxisListType

P = 128
BATCH, SEQ, D = 4, 1024, 256
TILES = SEQ // P
ALL_TILES = BATCH * TILES
DC = D // P
EPS = 1e-5


class Steps:

    def __init__(self, engine, semaphore, base=0):
        self.engine, self.semaphore, self.base, self.n = engine, semaphore, base, 0

    def do(self, instruction):
        self.n += 1
        return instruction.then_inc(self.semaphore, 1)

    def done(self):
        self.engine.wait_ge(self.semaphore, self.base + self.n)


class Memory:

    def __init__(self, nc, stack, tag):
        self.nc, self.stack, self.tag, self.sems = nc, stack, tag, []
        stack.callback(self.clear)

    def clear(self):
        self.nc.clear_and_free_semaphores(self.sems)
        self.nc.all_engine_barrier()

    def sb(self, name, shape, dtype=F32):
        return self.stack.enter_context(self.nc.sbuf_tensor(f"{self.tag}_{name}", shape, dtype))

    def banks(self, n):
        return [self.stack.enter_context(self.nc.psum_tensor(f"{self.tag}_bank{i}", [P, 512], F32)) for i in range(n)]

    def sem(self, name):
        self.sems.append(self.nc.alloc_semaphore(f"{self.tag}_{name}"))
        return self.sems[-1]


def split_bias(steps, rows, left, table):
    v = steps.engine
    for k, p in enumerate((0, 32, 64)):
        row, rest, part = rows[p:p + 1, :], left[p:p + 1, :], table[p:p + 1, :]
        for _ in range(k):
            steps.do(v.tensor_copy(part, row)); steps.done()
            steps.do(v.tensor_tensor(rest, row, part, ALU.subtract)); steps.done()
            steps.do(v.tensor_copy(row, rest)); steps.done()
        steps.do(v.tensor_copy(part, row)); steps.done()


QK, HID, GROUP = 64, 512, 64
HC = HID // P
NVG = 2 * HID + QK


def gated_attention(nc, io, x_in, x_out):
    with ExitStack() as stack:
        m = Memory(nc, stack, "ga")
        sb, sem = m.sb, m.sem
        x = sb("x", [P, ALL_TILES, D])
        w_vgk = sb("w_vgk", [P, DC, NVG])
        w_o = sb("w_o", [P, HC, D])
        ident = sb("ident", [P, P])
        rope = sb("rope", [P, 2, TILES, QK])
        heads_wb = sb("heads_wb", [P, 2, 4, QK])
        group_bias = sb("group_bias", [P, P])
        ln1 = sb("ln1", [P, 2, DC])
        ln2 = sb("ln2", [P, 2, D])
        brow = sb("brow", [P, NVG + D])
        bleft = sb("bleft", [P, NVG + D])
        bparts = sb("bparts", [P, NVG + D], BF16)
        ones = sb("ones", [P, P], BF16)
        stats = sb("stats", [P, ALL_TILES, 6])
        mv = sb("mv", [P, ALL_TILES, 2])
        root = sb("root", [P, ALL_TILES])
        r1 = sb("r1", [P, ALL_TILES])
        var2 = sb("var2", [P, ALL_TILES])
        rstd = sb("rstd", [P, ALL_TILES])
        xn = sb("xn", [P, 2, D])
        xT = sb("xT", [P, 2, DC, P])
        v = sb("v", [P, TILES, HID])
        gate = sb("gate", [P, TILES, HID])
        qk = sb("qk", [P, 2, QK])
        hm = sb("hm", [P, 4, QK])
        hb = sb("hb", [P, 4, QK])
        hc = sb("hc", [P, 4, QK])
        hs = sb("hs", [P, 4, QK])
        heads = sb("heads", [P, 2, 5, QK])
        headsT = sb("headsT", [P, TILES, 2, P])
        z = sb("z", [P, P])
        attnT = sb("attnT", [P, TILES, P])
        kv = sb("kv", [P, HID])
        go = sb("go", [P, 2, HID])
        goT = sb("goT", [P, 2, HC, P])
        y = sb("y", [P, TILES, D])
        ystats = sb("ystats", [P, TILES, 6])
        ymv = sb("ymv", [P, TILES, 2])
        yroot = sb("yroot", [P, TILES])
        yrstd = sb("yrstd", [P, TILES])
        epst = sb("epst", [P, 1])

        bT, bR, bV, bG, bQ, bS, bKV, bY = m.banks(8)
        bO = [bV, bG]
        bGT = [bQ, bS]

        consts_in = sem("consts_in")
        x_loaded = sem("x_loaded")
        dve_step = sem("dve_step")
        ready = sem("ready")
        var_ready, root_ready = sem("var_ready"), sem("root_ready")
        xn_ready, xT_psum, xT_ready = sem("xn_ready"), sem("xT_psum"), sem("xT_ready")
        v_psum, g_psum, q_psum = sem("v_psum"), sem("g_psum"), sem("q_psum")
        v_ready, g_ready, q_ready = sem("v_ready"), sem("g_ready"), sem("q_ready")
        heads_ready, headsT_psum, headsT_ready = sem("heads_ready"), sem("headsT_psum"), sem("headsT_ready")
        s_psum, attn_ready = sem("s_psum"), sem("attn_ready")
        kv_psum, kv_ready = sem("kv_psum"), sem("kv_ready")
        o_psum, go_ready, goT_psum, goT_ready = sem("o_psum"), sem("go_ready"), sem("goT_psum"), sem("goT_ready")
        y_psum, y_ready = sem("y_psum"), sem("y_ready")
        yvar_ready, yroot_ready = sem("yvar_ready"), sem("yroot_ready")
        x_done, stored = sem("x_done"), sem("stored")
        waited = sem("waited")
        N_CONST = 9

        block = stack.enter_context(nc.Block())

        @block.sync
        def _(sp):
            for b in range(BATCH):
                sp.dma_start(x[:, b * TILES:(b + 1) * TILES, :], x_in[b].rearrange("(t p) d -> p t d", p=P)).then_inc(x_loaded, 16)
            with sp.Fori(0, BATCH) as b:
                sp.wait_ge(x_done, b + 1)
                sp.dma_start(x_out[b].rearrange("(t p) d -> p t d", p=P), x[:, bass.ds(b * TILES, TILES), :]).then_inc(stored, 16)
            sp.wait_ge(stored, 16 * BATCH)

        @block.gpsimd
        def _(pool):
            pool.memset(ones[:, :], 1.0).then_inc(ready, 1)
            pool.memset(bparts[:, :], 0.0).then_inc(ready, 1)
            pool.memset(kv[:, :], 0.0).then_inc(ready, 1)
            pool.memset(heads[:, :, :, :], 0.0).then_inc(ready, 1)

        @block.scalar
        def _(act):
            for dst, src in ((w_vgk[:, :, :], io["ga_w"]), (w_o[:, :, :], io["ga_wo"]), (ident[:, :], io["ident"]),
                             (rope[:, :, :, :], io["ga_rope"]), (heads_wb[:, :, :, :], io["ga_heads"]),
                             (group_bias[:, :], io["ga_bias"]), (ln1[:, :, :], io["ga_ln1"]), (ln2[:, :, :], io["ga_ln2"]),
                             (brow[:, :], io["ga_brow"])):
                act.dma_start(dst, src).then_inc(consts_in, 16)
            for k, s in enumerate((mv[:, :, 1], var2[:, :])):
                act.wait_ge(var_ready, k + 1)
                act.activation(root[:, :], s, ACT.Sqrt, bias=epst[:, 0:1]).then_inc(root_ready, 1)
            with act.Fori(0, BATCH) as b:
                n0 = b * TILES
                for t in range(TILES):
                    act.wait_ge(xT_psum, n0 + t + 1)
                    for c in range(DC):
                        i = act.activation(xT[:, t % 2, c, :], bT[:, c * P:(c + 1) * P], ACT.Identity,
                                           bias=ln1[:, 1, c:c + 1], scale=ln1[:, 0, c:c + 1])
                    i.then_inc(xT_ready, 1)
                    act.wait_ge(q_psum, n0 + t + 1)
                    act.activation(qk[:, t % 2, :], bQ[:, 0:QK], ACT.Silu).then_inc(q_ready, 1)
                    if t == 0:
                        act.wait_ge(o_psum, n0 + 1)
                    act.wait_ge(v_psum, n0 + t + 1)
                    act.activation(v[:, t, :], bV[:, :], ACT.Silu).then_inc(v_ready, 1)
                    act.wait_ge(g_psum, n0 + t + 1)
                    act.activation(gate[:, t, :], bG[:, :], ACT.Silu).then_inc(g_ready, 1)
                    act.wait_ge(headsT_psum, n0 + t + 1)
                    act.activation(headsT[:, t, :, :], bR[:, 0:2 * P].rearrange("p (c n) -> p c n", c=2), ACT.Identity).then_inc(headsT_ready, 1)
                act.wait_ge(kv_psum, b + 1)
                act.activation(kv[0:QK, :], bKV[0:QK, :], ACT.Identity, scale=1.0 / SEQ).then_inc(kv_ready, 1)
                for t in range(TILES):
                    act.wait_ge(goT_psum, n0 + t + 1)
                    act.activation(goT[:, t % 2, :, :], bGT[t % 2][:, :].rearrange("p (c n) -> p c n", c=HC), ACT.Identity).then_inc(goT_ready, 1)
                    act.wait_ge(y_psum, n0 + t + 1)
                    act.activation(y[:, t, :], bY[:, 0:D], ACT.Identity).then_inc(y_ready, 1)
                act.wait_ge(yvar_ready, b + 1)
                act.activation(yroot[:, :], ymv[:, :, 1], ACT.Sqrt, bias=epst[:, 0:1]).then_inc(yroot_ready, 1)

        @block.vector
        def _(dve):
            s = Steps(dve, dve_step)
            dve.wait_ge(ready, 4)
            dve.wait_ge(consts_in, 16 * N_CONST)
            s.do(dve.memset(epst[:, :], EPS))
            split_bias(s, brow, bleft, bparts)
            s.done()
            dve.sem_inc(ready, 1)
            dve.wait_ge(x_loaded, 16 * BATCH)
            for n in range(ALL_TILES):
                s.do(dve.bn_stats(stats[:, n, :], x[:, n, :]))
            s.done()
            for n in range(ALL_TILES):
                s.do(dve.bn_aggr(mv[:, n, :], stats[:, n, :]))
            s.done()
            dve.sem_inc(var_ready, 1)
            dve.wait_ge(root_ready, 1)
            s.do(dve.reciprocal(r1[:, :], root[:, :])); s.done()
            s.do(dve.tensor_tensor(var2[:, :], r1[:, :], r1[:, :], ALU.mult)); s.done()
            s.do(dve.tensor_tensor(var2[:, :], var2[:, :], mv[:, :, 1], ALU.mult)); s.done()
            dve.sem_inc(var_ready, 1)
            dve.wait_ge(root_ready, 2)
            s.do(dve.reciprocal(rstd[:, :], root[:, :])); s.done()
            s.do(dve.tensor_tensor(rstd[:, :], rstd[:, :], r1[:, :], ALU.mult)); s.done()
            once = s.n

            def normalise(b, t):
                n = b * TILES + t
                if t >= 2:
                    dve.wait_ge(xT_psum, n - 1)
                dve.tensor_scalar(xn[:, t % 2, :], x[:, bass.ds(n, 1), :].rearrange("p a d -> p (a d)"),
                                  mv[:, bass.ds(n, 1), 0], rstd[:, bass.ds(n, 1)],
                                  ALU.subtract, ALU.mult).then_inc(xn_ready, 1)

            def make_heads(b, t):
                n = b * TILES + t
                dve.wait_ge(q_ready, n + 1)
                if t >= 2:
                    dve.wait_ge(headsT_psum, n - 1)
                    if t >= 3:
                        dve.wait_ge(s_psum, n - 2)
                q4 = qk[:, t % 2, None, :].to_broadcast([P, 4, QK])
                s.do(dve.tensor_tensor(hm[:, :, :], q4, heads_wb[:, 0, :, :], ALU.mult)); s.done()
                s.do(dve.tensor_tensor(hb[:, :, :], hm[:, :, :], heads_wb[:, 1, :, :], ALU.add)); s.done()
                cos = rope[:, 0, t, None, :].to_broadcast([P, 4, QK])
                s.do(dve.tensor_tensor(hc[:, :, :], hb[:, :, :], cos, ALU.mult))
                for a, c in ((0, 1), (1, 0)):
                    half = QK // 2
                    sin = rope[:, 1, t, None, a * half:(a + 1) * half].to_broadcast([P, 4, half])
                    s.do(dve.tensor_tensor(hs[:, :, a * half:(a + 1) * half], hb[:, :, c * half:(c + 1) * half], sin, ALU.mult))
                s.done()
                dve.tensor_tensor(heads[:, t % 2, 0:2, :], hc[:, 0:2, :], hs[:, 0:2, :], ALU.add)
                s.do(dve.tensor_tensor(heads[:, t % 2, 3:5, :], hc[:, 2:4, :], hs[:, 2:4, :], ALU.add)); s.done()
                dve.sem_inc(heads_ready, 1)

            def attention(b, t):
                dve.wait_ge(s_psum, b * TILES + t + 1)
                s.do(dve.scalar_tensor_tensor(out=z[:, :], in0=bS[:, 0:P], scalar=1.0 / GROUP, in1=group_bias[:, :],
                                              op0=ALU.mult, op1=ALU.add)); s.done()
                s.do(dve.scalar_tensor_tensor(out=attnT[:, t, :], in0=z[:, :], scalar=0.0, in1=z[:, :],
                                              op0=ALU.max, op1=ALU.mult)); s.done()
                dve.sem_inc(attn_ready, 1)

            def gated(b, t):
                n = b * TILES + t
                dve.wait_ge(o_psum, n + 2)
                if t >= 2:
                    dve.wait_ge(goT_psum, n - 1)
                dve.wait_ge(g_ready, n + 1)
                dve.tensor_tensor(go[:, t % 2, :], bO[t % 2][:, :], gate[:, t, :], ALU.mult).then_inc(go_ready, 1)

            def row_stats(b, t):
                dve.wait_ge(y_ready, b * TILES + t + 1)
                s.do(dve.bn_stats(ystats[:, t, :], y[:, t, :]))

            with dve.Fori(0, BATCH) as b:
                PER = TILES * (6 + 2 + 1 + 1 + 1) + 4
                s.base, s.n = once + b * PER, 0
                normalise(b, 0)
                normalise(b, 1)
                for t in range(TILES):
                    make_heads(b, t)
                    if t + 2 < TILES:
                        normalise(b, t + 2)
                    if t:
                        attention(b, t - 1)
                attention(b, TILES - 1)
                for t in range(TILES):
                    gated(b, t)
                    if t:
                        row_stats(b, t - 1)
                row_stats(b, TILES - 1)
                s.done()
                dve.sem_inc(waited, 1)
                for t in range(TILES):
                    s.do(dve.bn_aggr(ymv[:, t, :], ystats[:, t, :]))
                s.done()
                dve.sem_inc(yvar_ready, 1)
                dve.wait_ge(yroot_ready, b + 1)
                s.do(dve.reciprocal(yrstd[:, :], yroot[:, :])); s.done()
                for t in range(TILES):
                    s.do(dve.tensor_scalar(y[:, t, :], y[:, t, :], ymv[:, t, 0:1], yrstd[:, t:t + 1], ALU.subtract, ALU.mult))
                s.done()
                wide = [P, TILES, D]
                s.do(dve.tensor_tensor(y[:, :, :], y[:, :, :], ln2[:, 0, None, :].to_broadcast(wide), ALU.mult)); s.done()
                s.do(dve.tensor_tensor(y[:, :, :], y[:, :, :], ln2[:, 1, None, :].to_broadcast(wide), ALU.add)); s.done()
                xs = x[:, bass.ds(b * TILES, TILES), :]
                s.do(dve.tensor_tensor(xs, xs, y[:, :, :], ALU.add)); s.done()
                dve.sem_inc(x_done, 1)
                assert s.n == PER

        @block.tensor
        def _(pe):
            pe.wait_ge(ready, 5)
            pe.sem_inc(o_psum, 1)

            def turn_rows(b, t):
                n = b * TILES + t
                pe.wait_ge(xn_ready, n + 1)
                if t:
                    pe.wait_ge(xT_ready, n)
                for c in range(DC):
                    i = pe.transpose(bT[:, c * P:(c + 1) * P], xn[:, t % 2, c * P:(c + 1) * P], ident[:, :])
                i.then_inc(xT_psum, 1)

            def project(b, t):
                n = b * TILES + t
                pe.wait_ge(xT_ready, n + 1)
                if t:
                    pe.wait_ge(g_ready, n)
                for bank, at, width, signal in ((bQ, 2 * HID, QK, q_psum), (bV, 0, HID, v_psum), (bG, HID, HID, g_psum)):
                    for c in range(DC):
                        pe.matmul(bank[:, 0:width], xT[:, t % 2, c, :], w_vgk[:, c, at:at + width], start=(c == 0), stop=False)
                    pe.matmul(bank[:, 0:width], ones[:, :], bparts[:, at:at + width], start=False, stop=True).then_inc(signal, 1)

            def turn_heads(b, t):
                n = b * TILES + t
                pe.wait_ge(heads_ready, n + 1)
                if t:
                    pe.wait_ge(headsT_ready, n)
                for c in range(2):
                    i = pe.transpose(bR[:, c * P:(c + 1) * P], heads[:, t % 2, 2 * c:2 * c + 2, :].rearrange("p a d -> p (a d)"), ident[:, :])
                i.then_inc(headsT_psum, 1)

            def scores(b, t):
                n = b * TILES + t
                pe.wait_ge(v_ready, n + 1)
                i = pe.matmul(bKV[0:QK, :], heads[:, t % 2, 4, :], v[:, t, :], start=(t == 0), stop=(t == TILES - 1))
                if t == TILES - 1:
                    i.then_inc(kv_psum, 1)
                pe.wait_ge(headsT_ready, n + 1)
                if t:
                    pe.wait_ge(attn_ready, n)
                pe.matmul(bS[:, 0:P], headsT[:, t, 1, :], headsT[:, t, 0, :], start=True, stop=True).then_inc(s_psum, 1)

            def outputs(b, t):
                n = b * TILES + t
                if t == 0:
                    pe.wait_ge(kv_ready, b + 1)
                    pe.wait_ge(g_ready, (b + 1) * TILES)
                    pe.wait_ge(attn_ready, (b + 1) * TILES)
                if t >= 2:
                    pe.wait_ge(go_ready, n - 1)
                pe.matmul(bO[t % 2][:, :], attnT[:, t, :], v[:, t, :], start=True, stop=False)
                pe.matmul(bO[t % 2][:, :], headsT[:, t, 0, :], kv[:, :], start=False, stop=True).then_inc(o_psum, 1)

            def turn_gated(b, t):
                n = b * TILES + t
                pe.wait_ge(go_ready, n + 1)
                if t >= 2:
                    pe.wait_ge(goT_ready, n - 1)
                for c in range(HC):
                    i = pe.transpose(bGT[t % 2][:, c * P:(c + 1) * P], go[:, t % 2, c * P:(c + 1) * P], ident[:, :])
                i.then_inc(goT_psum, 1)

            def project_out(b, t):
                n = b * TILES + t
                pe.wait_ge(goT_ready, n + 1)
                if t:
                    pe.wait_ge(y_ready, n)
                for c in range(HC):
                    pe.matmul(bY[:, 0:D], goT[:, t % 2, c, :], w_o[:, c, :], start=(c == 0), stop=False)
                pe.matmul(bY[:, 0:D], ones[:, :], bparts[:, NVG:NVG + D], start=False, stop=True).then_inc(y_psum, 1)

            with pe.Fori(0, BATCH) as b:
                turn_rows(b, 0)
                for t in range(TILES):
                    project(b, t)
                    if t + 1 < TILES:
                        turn_rows(b, t + 1)
                    if t:
                        scores(b, t - 1)
                    turn_heads(b, t)
                scores(b, TILES - 1)
                for t in range(TILES + 2):
                    if t < TILES:
                        outputs(b, t)
                    if 1 <= t <= TILES:
                        turn_gated(b, t - 1)
                    if t >= 2:
                        project_out(b, t - 2)


EXPERTS, TOPK, UP = 8, 2, 1024
ASSIGNED = TOPK * BATCH * SEQ
ROUTED = (ASSIGNED + EXPERTS * (P - 1)) // P
ROUTED += ROUTED % 2


def experts(nc, io, x_in, x_out, rows, results, layer):
    gated = layer == 0
    shared = 0 if gated else 1
    n_exp = EXPERTS + shared
    hidden = UP // 2 if gated else UP
    hc = hidden // P
    SH = shared * ALL_TILES
    BLOCKS = SH + ROUTED
    with ExitStack() as stack:
        m = Memory(nc, stack, f"moe{layer}")
        sb, sem = m.sb, m.sem
        w_up = sb("w_up", [P, n_exp, DC, UP])
        w_down = sb("w_down", [P, n_exp, hc, D])
        if gated:
            xn_all = sb("xn_all", [P, ALL_TILES, D])
            LATE = n_exp
        else:
            LATE = n_exp - ALL_TILES * D // (DC * UP)
            xn_all = w_up[:, LATE:n_exp, :, :].rearrange("p e c n -> p (e c n)").rearrange("p (t d) -> p t d", d=D)
        spare = None if gated else w_down[:, LATE:n_exp, :, :].rearrange("p e c n -> p (e c n)")
        used = [0]

        def early(name, shape, dtype=F32):
            if gated:
                return sb(name, shape, dtype)
            n = int(np.prod(shape[1:])) * (2 if dtype == BF16 else 4) // 4
            view = spare[0:shape[0], used[0]:used[0] + n]
            used[0] += n
            if dtype != F32:
                view = view.bitcast(dtype)
            if len(shape) == 3:
                view = view.rearrange("p (a b) -> p a b", b=shape[2])
            if len(shape) == 4:
                view = view.rearrange("p (a b c) -> p a b c", b=shape[2], c=shape[3])
            return view

        ident = sb("ident", [P, P])
        misc = early("misc", [P, P + EXPERTS + ALL_TILES + ROUTED])
        w_gate = early("w_gate", [P, DC, EXPERTS])
        gbias = early("gbias", [P, EXPERTS])
        before = early("before", [P, P], BF16)
        ones = sb("ones", [P, P], BF16)
        zero = sb("zero", [P, 4 * D])
        if not gated:
            b_row = early("b_row", [n_exp, UP + D])
            b_parts = early("b_parts", [n_exp, 3, UP + D], BF16)
            b_table = sb("b_table", [P, n_exp, UP + D], BF16)
        stats = early("stats", [P, ALL_TILES, 6])
        mv = early("mv", [P, ALL_TILES, 2])
        root = early("root", [P, ALL_TILES])
        rstd = early("rstd", [P, ALL_TILES])
        epst = sb("epst", [P, 1])
        te = [P, ALL_TILES, EXPERTS]
        logit = early("logit", te)
        prob = early("prob", te)
        top = early("top", te)
        topi = early("topi", te, U32)
        topf = early("topf", te)
        small = early("small", [P, ALL_TILES])
        hot = early("hot", [P, TOPK, ALL_TILES, EXPERTS])
        both = early("both", te)
        both16 = early("both16", te, BF16)
        upto = early("upto", te)
        place = early("place", te)
        picked = early("picked", te)
        over = early("over", [P, EXPERTS, ALL_TILES])
        nblk = early("nblk", [P, EXPERTS])
        blk_end = sb("blk_end", [P, EXPERTS])
        blk_start = early("blk_start", [P, EXPERTS])
        one8 = early("one8", [P, ALL_TILES])
        posf = early("posf", [P, TOPK, ALL_TILES])
        pos = sb("pos", [P, TOPK, ALL_TILES], U32)
        weight = sb("weight", [P, TOPK, ALL_TILES])
        passed = early("passed", [P, ROUTED, EXPERTS])
        ownerf = early("ownerf", [P, BLOCKS])
        owner = sb("owner", [P, BLOCKS], I32)
        xb = sb("xb", [P, 2, D])
        xT = sb("xT", [P, 2, DC, P])
        act_out = sb("act_out", [P, 2, hidden])
        h = sb("h", [P, 2, hidden]) if gated else act_out
        hT = sb("hT", [P, 2, hc, P])
        gT = hT[:, :, 0:2 * DC, :]
        yb = sb("yb", [P, 2, D])
        rest = sb("sums", [P, 2, 4, D]) if gated else act_out.rearrange("p s (k d) -> p s k d", d=D)
        y_in, x_res, part = rest[:, :, 0:TOPK + shared, :], rest[:, :, 3, :], yb

        bX, bU0, bU1, bU2, bU3, bH0, bH1, bY = m.banks(8)
        bU = [(bU0, bU1), (bU2, bU3)]

        consts_in, w_in, x_loaded = sem("consts_in"), sem("w_in"), [sem(f"x_loaded{q}") for q in range(4)]
        late_in = sem("late_in")
        ready, dve_step = sem("ready"), sem("dve_step")
        var_ready, root_ready, xn_ready = sem("var_ready"), sem("root_ready"), sem("xn_ready")
        gT_psum, gT_ready, logit_psum, logit_read = sem("gT_psum"), sem("gT_ready"), sem("logit_psum"), sem("logit_read")
        exp_in, exp_ready = sem("exp_in"), sem("exp_ready")
        both_ready, rank_psum, routed = sem("both_ready"), sem("rank_psum"), sem("routed")
        cleared, sent, copied = sem("cleared"), sem("sent"), sem("copied")
        b_ready, b_in = sem("b_ready"), sem("b_in")
        xb_in, xT_psum, xT_ready = [sem("xb_in0"), sem("xb_in1")], sem("xT_psum"), sem("xT_ready")
        u_psum, a_ready, h_ready = sem("u_psum"), sem("a_ready"), sem("h_ready")
        hT_psum, hT_ready, y_psum, yb_ready, yb_out = sem("hT_psum"), sem("hT_ready"), sem("y_psum"), sem("yb_ready"), [sem("yb_out0"), sem("yb_out1")]
        hT_ready2 = sem("hT_ready2")
        out_ready = sem("out_ready")
        gathered, res_in, stored = [[sem(f"{x}{q}") for q in range(2)] for x in ("gathered", "res_in", "stored")]
        sh_in = sem("sh_in")
        N_CONST = 3 + (2 if not gated else 0)
        HALF_TILES = ALL_TILES // 2

        SHARED_ROWS = ROUTED * P
        routed_rows, routed_results = rows[0:SHARED_ROWS, :], results[0:SHARED_ROWS, :]
        x_tiles = x_in.rearrange("b (t p) d -> p (b t) d", p=P)
        block = stack.enter_context(nc.Block())

        @block.sync
        def _(sp):
            for q in range(4):
                n = ALL_TILES // 4
                sp.dma_start(xn_all[:, q * n:(q + 1) * n, :], x_tiles[:, q * n:(q + 1) * n, :]).then_inc(x_loaded[q], 16)
            if not gated:
                sp.wait_ge(xn_ready, ALL_TILES)
                sp.dma_start(rows[SHARED_ROWS:SHARED_ROWS + SH * P, :].rearrange("(t p) d -> p t d", p=P), xn_all[:, :, :]).then_inc(copied, 16)
                sp.wait_ge(copied, 16)

            def load_block(t, origin):
                if t.n >= 2:
                    sp.wait_ge(xT_psum, t.j - 1)
                sp.dma_start(xb[:, t.side, :], rows[bass.ds(t.j * P + origin, P), :]).then_inc(xb_in[t.side], 16)

            def store_block(t, origin):
                sp.wait_ge(yb_ready, t.j + 1)
                sp.dma_start(results[bass.ds(t.j * P + origin, P), :], yb[:, t.side, :]).then_inc(yb_out[t.side], 16)

            def pass_blocks(first, end, origin):
                for side in range(2):
                    load_block(Turn(first // 2, side, first + side), origin)
                if first:
                    for side in range(2):
                        store_block(at(first - 2 + side), SHARED_ROWS)
                with sp.Fori(first // 2 + 1, end // 2) as pair:
                    for side in range(2):
                        load_block(Turn(pair, side, 2 + side), origin)
                        store_block(Turn(pair - 1, side, 2 + side), origin)

            if SH:
                pass_blocks(0, SH, SHARED_ROWS)
            sp.wait_ge(sent, 16 * TOPK * ALL_TILES)
            pass_blocks(SH, BLOCKS, -SH * P)
            for side in range(2):
                store_block(at(BLOCKS - 2 + side), -SH * P)
            for out in yb_out:
                sp.wait_ge(out, 8 * BLOCKS)
            with sp.Fori(0, ALL_TILES // 2) as i:
                for q in range(2):
                    n = 2 * i + q
                    sp.wait_ge(out_ready, n + 1)
                    sp.dma_start(x_res[:, q, :], x_tiles[:, bass.ds(n, 1), :].rearrange("p a d -> p (a d)")).then_inc(res_in[q], 16)
                    if shared:
                        sp.dma_start(y_in[:, q, TOPK, :], results[bass.ds(n * P + SHARED_ROWS, P), :]).then_inc(res_in[q], 16)

        @block.gpsimd
        def _(pool):
            if gated:
                pool.memset(zero[:, :], 0.0).then_inc(ready, 1)
            pool.memset(ones[:, :], 1.0).then_inc(ready, 1)
            if not gated:
                pool.memset(b_table[:, :, :], 0.0).then_inc(ready, 1)
            if gated:
                pool.wait_ge(ready, 1)
                per = P * 4
                for k in range(rows.shape[0] // per):
                    pool.dma_start(rows[k * per:(k + 1) * per, :].rearrange("(p r) d -> p (r d)", p=P), zero[:, :]).then_inc(cleared, 16)
                pool.wait_ge(cleared, 16 * (rows.shape[0] // per))
            pool.wait_ge(routed, 1)
            pool.wait_ge(xn_ready, ALL_TILES)
            for n in range(ALL_TILES):
                for k in range(TOPK):
                    pool.indirect_dma_start(routed_rows, bass.IndirectOffsetOnAxis(ap=pos_slot(pos, k, n), axis=0),
                                            xn_all[:, n, :], None).then_inc(sent, 16)
            if LATE < n_exp:
                pool.wait_ge(sent, 16 * TOPK * ALL_TILES)
                pool.wait_ge(copied, 16)
                pool.wait_ge(gT_psum, ALL_TILES // 2)
                pool.wait_ge(b_in, 16 * 3 * n_exp)
                for e in range(LATE, n_exp):
                    pool.dma_start(w_up[:, e, :, :], io[f"m{layer}_up"][e]).then_inc(late_in, 16)
                    pool.dma_start(w_down[:, e, :, :], io[f"m{layer}_down"][e]).then_inc(late_in, 16)
            for out in yb_out:
                pool.wait_ge(out, 8 * BLOCKS)
            for n in range(ALL_TILES):
                if n >= 2:
                    pool.wait_ge(out_ready, n + 1)
                for k in range(TOPK):
                    pool.indirect_dma_start(y_in[:, n % 2, k, :], None, routed_results,
                                            bass.IndirectOffsetOnAxis(ap=pos_slot(pos, k, n), axis=0)).then_inc(gathered[n % 2], 16)

        @block.scalar
        def _(act):
            consts = [(ident[:, :], io["ident"]), (misc[:, :], io["moe_misc"]), (w_gate[:, :, :], io[f"m{layer}_gate"])]
            if not gated:
                consts += [(gbias[:, :], io["m1_gbias"]), (b_row[:, :], io["m1_bias"])]
            for dst, src in consts:
                act.dma_start(dst, src).then_inc(consts_in, 16)
            for e in range(LATE):
                act.dma_start(w_up[:, e, :, :], io[f"m{layer}_up"][e]).then_inc(w_in, 16)
                act.dma_start(w_down[:, e, :, :], io[f"m{layer}_down"][e]).then_inc(w_in, 16)
            act.wait_ge(var_ready, 1)
            act.activation(root[:, :], mv[:, :, 1], ACT.Sqrt, bias=epst[:, 0:1]).then_inc(root_ready, 1)
            if not gated:
                act.wait_ge(b_ready, 1)
                act.wait_ge(ready, 2)
                for k in range(3):
                    for e in range(n_exp):
                        act.dma_start(b_table[k:k + 1, e, :], b_parts[e:e + 1, k, :]).then_inc(b_in, 16)
            for t in range(ALL_TILES // 2):
                act.wait_ge(gT_psum, t + 1)
                if t >= 2:
                    act.wait_ge(logit_psum, 2 * (t - 1))
                act.activation(gT[:, t % 2, :, :], bU[t % 2][0][:, :].rearrange("p (c n) -> p c n", c=2 * DC), ACT.Identity).then_inc(gT_ready, 1)
            act.wait_ge(exp_in, 1)
            act.activation(prob[:, :, :], logit[:, :, :], ACT.Exp if gated else ACT.Sigmoid).then_inc(exp_ready, 1)

            def turned(t):
                j, n = t.j, t.n
                act.wait_ge(xT_psum, j + 1)
                act.activation(xT[:, n % 2, :, :], bX[:, 0:DC * P].rearrange("p (c n) -> p c n", c=DC), ACT.Identity).then_inc(xT_ready, 1)

            def nonlinear(t):
                j, n = t.j, t.n
                act.wait_ge(u_psum, j + 1)
                if n >= 2:
                    act.wait_ge(h_ready if gated else hT_psum, j - 1)
                if gated:
                    act.activation(act_out[:, n % 2, :], bU[n % 2][0][:, :], ACT.Silu).then_inc(a_ready, 1)
                else:
                    for k in range(2):
                        i = act.activation(act_out[:, n % 2, k * 512:(k + 1) * 512], bU[n % 2][k][:, :], ACT.Gelu)
                    i.then_inc(a_ready, 1)

            def turned_hidden(t):
                j, n = t.j, t.n
                act.wait_ge(hT_psum, j + 1)
                if n >= 2:
                    act.wait_ge(y_psum, j - 1)
                act.activation(hT[:, n % 2, 0:4, :], bH0[:, :].rearrange("p (c n) -> p c n", c=4), ACT.Identity).then_inc(hT_ready, 1)

            turned(at(0))

            def act_block(t):
                j, n = t.j, t.n
                nonlinear(t)
                if n + 1 < BLOCKS:
                    turned(t.after())
                turned_hidden(t)
            for_blocks(act, BLOCKS, act_block)
            for q in range(2):
                act.sem_inc(stored[q], 16)
            with act.Fori(0, ALL_TILES // 2) as i:
                for q in range(2):
                    n = 2 * i + q
                    act.wait_ge(out_ready, n + 3)
                    act.dma_start(x_out.rearrange("b (t p) d -> p (b t) d", p=P)[:, bass.ds(n, 1), :].rearrange("p a d -> p (a d)"), part[:, q, :]).then_inc(stored[q], 16)
            for q in range(2):
                act.wait_ge(stored[q], 8 * ALL_TILES + 16)

        @block.vector
        def _(dve):
            s = Steps(dve, dve_step)
            one = lambda i: (s.do(i), s.done())
            one(dve.memset(epst[:, :], EPS))
            one(dve.memset(one8[:, :], 1.0))
            for q in range(4):
                dve.wait_ge(x_loaded[q], 16)
                for n in range(q * 8, q * 8 + 8):
                    s.do(dve.bn_stats(stats[:, n, :], xn_all[:, n, :]))
            s.done()
            for n in range(ALL_TILES):
                s.do(dve.bn_aggr(mv[:, n, :], stats[:, n, :]))
            s.done()
            dve.sem_inc(var_ready, 1)
            dve.wait_ge(root_ready, 1)
            one(dve.reciprocal(rstd[:, :], root[:, :]))
            for n in range(ALL_TILES):
                dve.tensor_scalar(xn_all[:, n, :], xn_all[:, n, :], mv[:, n, 0:1], rstd[:, n:n + 1],
                                  ALU.subtract, ALU.mult).then_inc(xn_ready, 1)
            dve.wait_ge(consts_in, 16 * N_CONST)
            one(dve.tensor_copy(before[:, :], misc[:, 0:P]))
            if not gated:
                for k in range(3):
                    one(dve.tensor_copy(b_parts[:, k, :], b_row[:, :]))
                    if k < 2:
                        one(dve.tensor_tensor(b_row[:, :], b_row[:, :], b_parts[:, k, :], ALU.subtract))
                dve.sem_inc(b_ready, 1)
            for n in range(ALL_TILES):
                dve.wait_ge(logit_psum, n + 1)
                lb = (bH0, bH1)[n % 2]
                if gated:
                    i = dve.tensor_copy(logit[:, n, :], lb[:, 0:EXPERTS])
                else:
                    i = dve.tensor_tensor(logit[:, n, :], lb[:, 0:EXPERTS], gbias[:, :], ALU.add)
                i.then_inc(logit_read, 1)
            dve.wait_ge(logit_read, ALL_TILES)
            wide = lambda a: a.rearrange("p (t a) -> p t a", a=1).to_broadcast(te)
            if gated:
                one(dve.tensor_reduce(small[:, :], logit[:, :, :], AX.X, ALU.max))
                one(dve.tensor_tensor(logit[:, :, :], logit[:, :, :], wide(small[:, :]), ALU.subtract))
            dve.sem_inc(exp_in, 1)
            dve.wait_ge(exp_ready, 1)
            if gated:
                one(dve.tensor_reduce(small[:, :], prob[:, :, :], AX.X, ALU.add))
                one(dve.reciprocal(small[:, :], small[:, :]))
                one(dve.tensor_tensor(prob[:, :, :], prob[:, :, :], wide(small[:, :]), ALU.mult))
            for n in range(ALL_TILES):
                s.do(dve.max(top[:, n, :], prob[:, n, :]))
            s.done()
            for n in range(ALL_TILES):
                s.do(dve.max_index(topi[:, n, :], top[:, n, :], prob[:, n, :]))
            s.done()
            one(dve.tensor_copy(topf[:, :, :], topi[:, :, :]))
            iota8 = misc[:, None, P:P + EXPERTS].to_broadcast(te)
            for k in range(TOPK):
                s.do(dve.tensor_tensor(hot[:, k, :, :], iota8, topf[:, :, k:k + 1].to_broadcast(te), ALU.is_equal))
            s.done()
            one(dve.tensor_tensor(both[:, :, :], hot[:, 0, :, :], hot[:, 1, :, :], ALU.add))
            one(dve.tensor_copy(both16[:, :, :], both[:, :, :]))
            dve.sem_inc(both_ready, 1)
            for k in range(TOPK):
                s.do(dve.tensor_copy(weight[:, k, :], top[:, :, k]))
            s.done()
            if not gated:
                one(dve.tensor_tensor(small[:, :], weight[:, 0, :], weight[:, 1, :], ALU.add))
                one(dve.tensor_scalar(small[:, :], small[:, :], 1e-6, None, ALU.add))
                one(dve.reciprocal(small[:, :], small[:, :]))
                for k in range(TOPK):
                    s.do(dve.tensor_tensor(weight[:, k, :], weight[:, k, :], small[:, :], ALU.mult))
                s.done()
            dve.wait_ge(rank_psum, 1)
            te_of = lambda bank: bank[:, 0:ALL_TILES * EXPERTS].rearrange("p (t e) -> p t e", e=EXPERTS)
            for e in range(EXPERTS):
                s.do(dve.tensor_tensor_scan(upto[:, :, e], one8[:, :], te_of(bU1)[:, :, e], 0.0, ALU.mult, ALU.add))
            s.done()
            one(dve.tensor_tensor(place[:, :, :], upto[:, :, :], te_of(bU1), ALU.subtract))
            one(dve.tensor_tensor(place[:, :, :], place[:, :, :], te_of(bU0), ALU.add))
            et = [P, EXPERTS, ALL_TILES]
            total = upto[:, ALL_TILES - 1, :].rearrange("p (e a) -> p e a", a=1).to_broadcast(et)
            mult128 = misc[:, None, P + EXPERTS:P + EXPERTS + ALL_TILES].to_broadcast(et)
            one(dve.tensor_tensor(over[:, :, :], total, mult128, ALU.is_gt))
            one(dve.tensor_reduce(nblk[:, :], over[:, :, :], AX.X, ALU.add))
            one(dve.tensor_tensor_scan(blk_end[:, :], one8[:, 0:EXPERTS], nblk[:, :], 0.0, ALU.mult, ALU.add))
            one(dve.tensor_tensor(blk_start[:, :], blk_end[:, :], nblk[:, :], ALU.subtract))
            one(dve.tensor_scalar(blk_start[:, :], blk_start[:, :], float(P), None, ALU.mult))
            one(dve.tensor_tensor(place[:, :, :], place[:, :, :], blk_start[:, None, :].to_broadcast(te), ALU.add))
            for k in range(TOPK):
                one(dve.tensor_tensor(picked[:, :, :], place[:, :, :], hot[:, k, :, :], ALU.mult))
                one(dve.tensor_reduce(posf[:, k, :], picked[:, :, :], AX.X, ALU.add))
            one(dve.tensor_copy(pos[:, :, :], posf[:, :, :]))
            be = [P, ROUTED, EXPERTS]
            iota_b = misc[:, P + EXPERTS + ALL_TILES:].rearrange("p (j a) -> p j a", a=1).to_broadcast(be)
            one(dve.tensor_tensor(passed[:, :, :], blk_end[:, None, :].to_broadcast(be), iota_b, ALU.is_le))
            if SH:
                one(dve.memset(ownerf[:, 0:SH], 0.0))
            one(dve.tensor_reduce(ownerf[:, SH:BLOCKS], passed[:, :, :], AX.X, ALU.add))
            one(dve.tensor_scalar(ownerf[:, SH:BLOCKS], ownerf[:, SH:BLOCKS], float(EXPERTS - 1), float(shared), ALU.min, ALU.add))
            one(dve.tensor_copy(owner[:, :], ownerf[:, :]))
            dve.sem_inc(routed, 2)

            def gate_hidden(t):
                j, n = t.j, t.n
                dve.wait_ge(a_ready, j + 1)
                if n >= 2:
                    dve.wait_ge(hT_psum, j - 1)
                dve.tensor_tensor(h[:, n % 2, :], act_out[:, n % 2, :], bU[n % 2][1][:, :], ALU.mult).then_inc(h_ready, 1)

            def turned_hidden(t):
                j, n = t.j, t.n
                dve.wait_ge(hT_psum, j + 1)
                if n >= 2:
                    dve.wait_ge(y_psum, j - 1)
                dve.tensor_copy(hT[:, n % 2, 4:8, :], bH1[:, :].rearrange("p (c n) -> p c n", c=4)).then_inc(hT_ready2, 1)

            def result(t):
                j, n = t.j, t.n
                dve.wait_ge(y_psum, j + 1)
                if n >= 2:
                    dve.wait_ge(yb_out[t.side], 16 * t.pair)
                dve.tensor_copy(yb[:, n % 2, :], bY[:, 0:D]).then_inc(yb_ready, 1)

            def dve_block(t):
                j, n = t.j, t.n
                if gated:
                    gate_hidden(t)
                if n:
                    result(t.before())
                if not gated:
                    turned_hidden(t)
            for_blocks(dve, BLOCKS, dve_block)
            result(at(BLOCKS - 1))

            once = s.n
            dve.sem_inc(out_ready, 2)
            with dve.Fori(0, ALL_TILES // 2) as i:
                per = 2 * (TOPK - 1 + shared)
                s.base, s.n = once + i * per, 0
                for q in range(2):
                    n = 2 * i + q
                    dve.wait_ge(gathered[q], 16 * TOPK * (i + 1))
                    dve.wait_ge(res_in[q], 16 * (1 + shared) * (i + 1))
                    dve.wait_ge(stored[q], 16 * (i + 1))
                    acc = x_res[:, q, :]
                    if shared:
                        one(dve.scalar_tensor_tensor(out=acc, in0=y_in[:, q, TOPK, :], scalar=0.1, in1=acc, op0=ALU.mult, op1=ALU.add))
                    w = lambda k: weight[:, k, bass.ds(n, 1)]
                    one(dve.scalar_tensor_tensor(out=acc, in0=y_in[:, q, 0, :], scalar=w(0), in1=acc, op0=ALU.mult, op1=ALU.add))
                    dve.scalar_tensor_tensor(out=part[:, q, :], in0=y_in[:, q, 1, :], scalar=w(1), in1=acc, op0=ALU.mult, op1=ALU.add).then_inc(out_ready, 1)

        @block.tensor
        def _(pe):
            pe.wait_ge(consts_in, 16 * N_CONST)
            for t in range(ALL_TILES // 2 + 1):
                if t < ALL_TILES // 2:
                    pe.wait_ge(xn_ready, 2 * t + 2)
                    if t >= 2:
                        pe.wait_ge(gT_ready, t - 1)
                    for q in range(2):
                        for c in range(DC):
                            col = (q * DC + c) * P
                            i = pe.transpose(bU[t % 2][0][:, col:col + P], xn_all[:, 2 * t + q, c * P:(c + 1) * P], ident[:, :])
                    i.then_inc(gT_psum, 1)
                if t:
                    pe.wait_ge(gT_ready, t)
                    for q in range(2):
                        n = 2 * (t - 1) + q
                        if n >= 2:
                            pe.wait_ge(logit_read, n - 1)
                        for c in range(DC):
                            i = pe.matmul((bH0, bH1)[n % 2][:, 0:EXPERTS], gT[:, (t - 1) % 2, q * DC + c, :], w_gate[:, c, :], start=(c == 0), stop=(c == DC - 1))
                        i.then_inc(logit_psum, 1)
            pe.wait_ge(both_ready, 1)
            pe.wait_ge(ready, 2)
            flat = both16[:, :, :].rearrange("p t e -> p (t e)")
            pe.matmul(bU0[:, 0:ALL_TILES * EXPERTS], before[:, :], flat, start=True, stop=True)
            pe.matmul(bU1[:, 0:ALL_TILES * EXPERTS], ones[:, :], flat, start=True, stop=True).then_inc(rank_psum, 1)
            pe.wait_ge(w_in, 16 * 2 * LATE)
            pe.wait_ge(routed, 2)
            if not gated:
                pe.wait_ge(b_in, 16 * 3 * n_exp)

            def turn(t):
                j, n = t.j, t.n
                pe.wait_ge(xb_in[t.side], 16 * (t.pair + 1))
                if n:
                    pe.wait_ge(xT_ready, j)
                for c in range(DC):
                    i = pe.transpose(bX[:, c * P:(c + 1) * P], xb[:, n % 2, c * P:(c + 1) * P], ident[:, :])
                i.then_inc(xT_psum, 1)

            def up(t):
                j, n = t.j, t.n
                e = pe.value_load(owner[0:1, bass.ds(j, 1)], min_val=0, max_val=n_exp - 1)
                pe.wait_ge(xT_ready, j + 1)
                if n >= 2:
                    pe.wait_ge(h_ready if gated else a_ready, j - 1)
                for k in range(2):
                    for c in range(DC):
                        i = pe.matmul(bU[n % 2][k][:, :], xT[:, n % 2, c, :],
                                      w_up[:, bass.ds(e, 1), c, k * 512:(k + 1) * 512].rearrange("p a n -> p (a n)"), start=(c == 0), stop=(gated and c == DC - 1))
                    if not gated:
                        i = pe.matmul(bU[n % 2][k][:, :], ones[:, :], b_table[:, bass.ds(e, 1), k * 512:(k + 1) * 512].rearrange("p a n -> p (a n)"), start=False, stop=True)
                i.then_inc(u_psum, 1)

            def turn_hidden(t):
                j, n = t.j, t.n
                pe.wait_ge(h_ready if gated else a_ready, j + 1)
                if n:
                    pe.wait_ge(hT_ready, j)
                    if not gated:
                        pe.wait_ge(hT_ready2, j)
                for c in range(hc):
                    i = pe.transpose((bH0, bH1)[c // 4][:, (c % 4) * P:(c % 4 + 1) * P], h[:, n % 2, c * P:(c + 1) * P], ident[:, :])
                i.then_inc(hT_psum, 1)

            def down(t):
                j, n = t.j, t.n
                e = pe.value_load(owner[0:1, bass.ds(j, 1)], min_val=0, max_val=n_exp - 1)
                pe.wait_ge(hT_ready, j + 1)
                if not gated:
                    pe.wait_ge(hT_ready2, j + 1)
                if n:
                    pe.wait_ge(yb_ready, j)
                for c in range(hc):
                    i = pe.matmul(bY[:, 0:D], hT[:, n % 2, c, :], w_down[:, bass.ds(e, 1), c, :].rearrange("p a n -> p (a n)"), start=(c == 0), stop=(gated and c == hc - 1))
                if not gated:
                    i = pe.matmul(bY[:, 0:D], ones[:, :], b_table[:, bass.ds(e, 1), UP:].rearrange("p a n -> p (a n)"), start=False, stop=True)
                i.then_inc(y_psum, 1)

            def pe_block(t):
                j, n = t.j, t.n
                up(t)
                if n + 1 < BLOCKS:
                    turn(t.after())
                if n:
                    down(t.before())
                turn_hidden(t)

            turn(at(0))
            if LATE < n_exp:
                for_blocks(pe, SH, pe_block, last=False)
                pe.wait_ge(late_in, 16 * 2 * (n_exp - LATE))
                for_blocks(pe, BLOCKS, pe_block, first=SH)
            else:
                for_blocks(pe, BLOCKS, pe_block)
            down(at(BLOCKS - 1))


def pos_slot(pos, k, n):
    return pos[:, k, n:n + 1]


class Turn:

    def __init__(self, pair, side, n):
        self.pair, self.side, self.n = pair, side, n
        self.j = 2 * pair + side

    def before(self):
        return Turn(self.pair - 1 if self.side == 0 else self.pair, 1 - self.side, self.n - 1)

    def after(self):
        return Turn(self.pair + 1 if self.side == 1 else self.pair, 1 - self.side, self.n + 1)


def at(j):
    return Turn(j // 2, j % 2, j)


def for_blocks(engine, blocks, step, first=0, last=True):
    lo = first
    if first == 0:
        step(at(0))
        step(at(1))
        lo = 2
    hi = blocks - 2 if last else blocks
    with engine.Fori(lo // 2, hi // 2) as pair:
        for side in range(2):
            step(Turn(pair, side, 2 + side))
    if last:
        step(at(hi))
        step(at(hi + 1))


HEADS, DH = 16, 16
GH = 4
GROUPS = HEADS // GH
TERMS = 6
KEY_ROWS = TERMS * DH
Q_PART = (0, 0, 0, 1, 1, 2)
K_PART = (0, 1, 2, 0, 1, 0)


def causal_attention(nc, io, x_in, x_out):
    with ExitStack() as stack:
        m = Memory(nc, stack, "ca")
        sb, sem = m.sb, m.sem
        x = sb("x", [P, ALL_TILES, D])
        w_kqv = sb("w_kqv", [P, DC, 3 * D])
        w_o = sb("w_o", [P, DC, D])
        ident = sb("ident", [P, P])
        ident16 = sb("ident16", [P, P], BF16)
        mask = sb("mask", [P, P])
        mask16 = sb("mask16", [P, P], BF16)
        rope = sb("rope", [P, 2, TILES, DH // 2])
        stats = sb("stats", [P, ALL_TILES, 6])
        mv = sb("mv", [P, ALL_TILES, 2])
        root = sb("root", [P, ALL_TILES])
        rstd = sb("rstd", [P, ALL_TILES])
        epst = sb("epst", [P, 1])
        xn = sb("xn", [P, 2, D])
        xT = sb("xT", [P, 2, DC, P])
        turn_a = sb("turn_a", [P, 2 * D])
        turn_b = sb("turn_b", [P, 2 * D])
        kq = sb("kq", [P, TILES, 2, D])
        v_all = sb("v_all", [P, TILES, D])
        vg = sb("vg", [P, TILES, GH, 2 * DH])
        left = sb("left", [P, 2, TILES, 2, GH * DH])
        parts = sb("parts", [P, 3, TILES, 2, GH * DH], BF16)
        terms = sb("terms", [P, 2, TILES, GH, KEY_ROWS], BF16)
        kT = sb("kT", [P, GH, SEQ], BF16)
        qT = sb("qT", [P, GH, SEQ], BF16)
        top = sb("top", [P, GH, TILES])
        topl = sb("topl", [P, 2, TILES, GH])
        top3 = sb("top3", [P, TILES, GH, 32], BF16)
        probs = sb("probs", [P, 2, GH, SEQ])
        oT = sb("oT", [P, SEQ])
        rden = sb("rden", [P, TILES, GH])
        acts = sb("acts", [P, TILES, D])
        aT = sb("aT", [P, 2, DC, P])

        wide = [stack.enter_context(nc.psum_tensor(f"ca_wide{i}", [P, 1024], F32)) for i in range(3)]
        narrow = [stack.enter_context(nc.psum_tensor(f"ca_narrow{i}", [P, 512], F32)) for i in range(2)]
        S, O = wide[0:2], wide[2]

        consts_in = sem("consts_in")
        x_loaded = [sem(f"x_loaded{b}") for b in range(BATCH)]
        ready, dve_step, pool_step = sem("ready"), sem("dve_step"), sem("pool_step")
        var_ready, root_ready = sem("var_ready"), sem("root_ready")
        xn_ready, xT_psum, xT_ready = sem("xn_ready"), sem("xT_psum"), sem("xT_ready")
        p_psum, p_read, v_ready = sem("p_psum"), sem("p_read"), sem("v_ready")
        parts_ready, terms_ready = sem("parts_ready"), sem("terms_ready")
        tr_psum, tr_ready = sem("tr_psum"), sem("tr_ready")
        s1_psum, top_ready, top3_ready, topT_psum, topT_ready = sem("s1_psum"), sem("top_ready"), sem("top3_ready"), sem("topT_psum"), sem("topT_ready")
        s2_psum, exp_ready, cut_ready, pv_done = sem("s2_psum"), sem("exp_ready"), sem("cut_ready"), sem("pv_done")
        oT_ready, o_psum, acts_ready = sem("oT_ready"), sem("o_psum"), sem("acts_ready")
        aT_psum, aT_ready, y_psum, x_done, stored = sem("aT_psum"), sem("aT_ready"), sem("y_psum"), sem("x_done"), sem("stored")
        rden_ready = sem("rden_ready")
        waited = sem("waited")
        N_CONST = 5
        SCALE = DH ** -0.5

        block = stack.enter_context(nc.Block())

        @block.sync
        def _(sp):
            for b in range(BATCH):
                sp.dma_start(x[:, b * TILES:(b + 1) * TILES, :], x_in[b].rearrange("(t p) d -> p t d", p=P)).then_inc(x_loaded[b], 16)
            with sp.Fori(0, BATCH) as b:
                sp.wait_ge(x_done, (b + 1) * TILES)
                sp.dma_start(x_out[b].rearrange("(t p) d -> p t d", p=P), x[:, bass.ds(b * TILES, TILES), :]).then_inc(stored, 16)
            sp.wait_ge(stored, 16 * BATCH)

        @block.gpsimd
        def _(pool):
            pool.memset(vg[:, :, :, :], 0.0).then_inc(pool_step, 1)
            pool.wait_ge(pool_step, 1)
            pool.memset(vg[:, :, :, DH:DH + 1], 1.0).then_inc(pool_step, 1)
            pool.wait_ge(pool_step, 2)
            pool.memset(top3[:, :, :, :], 0.0).then_inc(ready, 1)
            with pool.Fori(0, BATCH) as b:
                with pool.Fori(0, GROUPS) as hg:
                    g = b * GROUPS + hg
                    pool.wait_ge(v_ready, (b + 1) * TILES)
                    pool.wait_ge(pv_done, g * TILES + 1)
                    pool.sem_inc(waited, 1)
                    pool.tensor_copy(vg[:, :, :, 0:DH], v_all[:, :, bass.ds(hg * GH * DH, GH * DH)].rearrange("p t (h d) -> p t h d", d=DH))
                    pool.wait_ge(parts_ready, g + 1)
                    pool.wait_ge(tr_psum, g * 2 * GH + 1)
                    pool.sem_inc(waited, 1)
                    for side, which in ((0, K_PART), (1, Q_PART)):
                        for r in range(TERMS):
                            i = pool.tensor_copy(terms[:, side, :, :, r * DH:(r + 1) * DH].rearrange("p t h d -> p (t h) d"),
                                                 parts[:, which[r], :, side, :].rearrange("p t (h d) -> p t h d", d=DH))
                    i.then_inc(terms_ready, 1)
                    for j in range(TILES):
                        for h in range(GH):
                            pool.wait_ge(exp_ready, (g * TILES + j) * GH + h + 1)
                            pool.sem_inc(waited, 1)
                            on = probs[:, j % 2, h, j * P:(j + 1) * P]
                            pool.affine_select(out=on, in_=on, compare_op=ALU.is_ge, fill=0.0, base=0,
                                               pattern=[[1, P]], channel_multiplier=-1).then_inc(cut_ready, 1)

        @block.scalar
        def _(act):
            for dst, src in ((w_kqv[:, :, :], io["ca_w"]), (w_o[:, :, :], io["ca_wo"]), (ident[:, :], io["ident"]),
                             (mask[:, :], io["ca_mask"]), (rope[:, :, :, :], io["ca_rope"])):
                act.dma_start(dst, src).then_inc(consts_in, 16)
            act.wait_ge(var_ready, 1)
            act.activation(root[:, :], mv[:, :, 1], ACT.Sqrt, bias=epst[:, 0:1]).then_inc(root_ready, 1)
            with act.Fori(0, BATCH) as b:
                n0 = b * TILES
                for t in range(TILES):
                    act.wait_ge(xT_psum, n0 + t + 1)
                    act.activation(xT[:, t % 2, :, :], narrow[t % 2][:, 0:D].rearrange("p (c n) -> p c n", c=DC), ACT.Identity).then_inc(xT_ready, 1)
                    if t == 0:
                        act.wait_ge(terms_ready, b * GROUPS + 1)
                    act.wait_ge(p_psum, n0 + t + 1)
                    act.activation(v_all[:, t, :], S[t % 2][:, 2 * D:3 * D], ACT.Identity).then_inc(v_ready, 1)
                with act.Fori(0, GROUPS) as hg:
                    g = b * GROUPS + hg
                    for k in range(2 * GH):
                        act.wait_ge(tr_psum, g * 2 * GH + k + 2)
                        dst = (kT, qT)[k // GH][0:KEY_ROWS, k % GH, :]
                        act.activation(dst, narrow[k % 2][0:KEY_ROWS, :].bitcast(BF16), ACT.Identity).then_inc(tr_ready, 1)
                    for j in range(TILES):
                        if j == 0:
                            act.wait_ge(pv_done, g * TILES + 1)
                        elif j >= 2:
                            act.wait_ge(pv_done, g * TILES + j)
                        for h in range(GH):
                            act.wait_ge(s2_psum, (g * TILES + j) * GH + h + 1)
                            act.activation(probs[:, j % 2, h, j * P:], S[h % 2][:, j * P:], ACT.Exp, scale=SCALE).then_inc(exp_ready, 1)
                    for c in range(2):
                        act.wait_ge(pv_done, g * TILES + TILES + 1)
                        act.activation(oT[:, c * 512:(c + 1) * 512], O[:, c * 512:(c + 1) * 512], ACT.Identity).then_inc(oT_ready, 1)
                for t in range(TILES):
                    act.wait_ge(aT_psum, n0 + t + 1)
                    act.activation(aT[:, t % 2, :, :], narrow[t % 2][:, 0:D].rearrange("p (c n) -> p c n", c=DC), ACT.Identity).then_inc(aT_ready, 1)

        @block.vector
        def _(dve):
            s = Steps(dve, dve_step)
            one = lambda i: (s.do(i), s.done())
            one(dve.memset(epst[:, :], EPS))
            one(dve.memset(kT[KEY_ROWS:KEY_ROWS + 3, :, :], 1.0))
            for b in range(BATCH):
                dve.wait_ge(x_loaded[b], 16)
                for n in range(b * TILES, (b + 1) * TILES):
                    s.do(dve.bn_stats(stats[:, n, :], x[:, n, :]))
            s.done()
            for n in range(ALL_TILES):
                s.do(dve.bn_aggr(mv[:, n, :], stats[:, n, :]))
            s.done()
            dve.sem_inc(var_ready, 1)
            dve.wait_ge(consts_in, 16 * N_CONST)
            s.do(dve.tensor_copy(ident16[:, :], ident[:, :]))
            one(dve.tensor_copy(mask16[:, :], mask[:, :]))
            dve.wait_ge(root_ready, 1)
            one(dve.reciprocal(rstd[:, :], root[:, :]))
            dve.sem_inc(ready, 1)
            dve.wait_ge(ready, 2)
            once = s.n

            def normalise(b, t):
                n = b * TILES + t
                if t >= 2:
                    dve.wait_ge(xT_psum, n - 1)
                dve.tensor_scalar(xn[:, t % 2, :], x[:, bass.ds(n, 1), :].rearrange("p a d -> p (a d)"),
                                  mv[:, bass.ds(n, 1), 0], rstd[:, bass.ds(n, 1)],
                                  ALU.subtract, ALU.mult).then_inc(xn_ready, 1)

            def turn_pairs(b, t):
                dve.wait_ge(p_psum, b * TILES + t + 1)
                src = S[t % 2][:, 0:2 * D]
                pairs = lambda a: a.rearrange("p (h f a) -> p h f a", f=DH // 2, a=2)
                full = [P, 2 * HEADS, DH // 2, 2]
                cos = rope[:, 0, t, :].rearrange("p (a f c) -> p a f c", a=1, c=1).to_broadcast(full)
                sin = rope[:, 1, t, None, :].to_broadcast(full[:3])
                s.do(dve.tensor_tensor(pairs(turn_a[:, :]), pairs(src), cos, ALU.mult))
                for a in range(2):
                    s.do(dve.tensor_tensor(pairs(turn_b[:, :])[:, :, :, a], pairs(src)[:, :, :, 1 - a], sin, ALU.mult))
                s.done()
                out = pairs(kq[:, t, :, :].rearrange("p s n -> p (s n)"))
                for a, op in ((0, ALU.subtract), (1, ALU.add)):
                    s.do(dve.tensor_tensor(out[:, :, :, a], pairs(turn_a[:, :])[:, :, :, a], pairs(turn_b[:, :])[:, :, :, a], op))
                s.done()
                dve.sem_inc(p_read, 1)

            dve.sem_inc(acts_ready, 1)
            STAGE1, GROUP_STEPS, STAGE3 = TILES * 5, 5 + 6, 0
            PER = STAGE1 + GROUPS * GROUP_STEPS + STAGE3
            with dve.Fori(0, BATCH) as b:
                s.base, s.n = once + b * PER, 0
                normalise(b, 0)
                normalise(b, 1)
                for t in range(TILES):
                    if t + 2 < TILES:
                        normalise(b, t + 2)
                    turn_pairs(b, t)
                assert s.n == STAGE1
                with dve.Fori(0, GROUPS) as hg:
                    g = b * GROUPS + hg
                    s.base, s.n = once + b * PER + STAGE1 + hg * GROUP_STEPS, 0
                    dve.wait_ge(terms_ready, g + 1)
                    src = kq[:, :, :, bass.ds(hg * GH * DH, GH * DH)]
                    one(dve.tensor_copy(parts[:, 0, :, :, :], src))
                    one(dve.tensor_tensor(left[:, 0, :, :, :], src, parts[:, 0, :, :, :], ALU.subtract))
                    one(dve.tensor_copy(parts[:, 1, :, :, :], left[:, 0, :, :, :]))
                    one(dve.tensor_tensor(left[:, 1, :, :, :], left[:, 0, :, :, :], parts[:, 1, :, :, :], ALU.subtract))
                    one(dve.tensor_copy(parts[:, 2, :, :, :], left[:, 1, :, :, :]))
                    dve.sem_inc(parts_ready, 1)
                    for h in range(GH):
                        for i in range(TILES):
                            n = h * TILES + i
                            dve.wait_ge(s1_psum, g * GH * TILES + n + 1)
                            dve.tensor_reduce(top[:, h, i:i + 1], S[n % 2][:, 0:(i + 1) * P], AX.X, ALU.max).then_inc(top_ready, 1)
                    dve.wait_ge(top_ready, (g + 1) * GH * TILES)
                    by_tile = top[:, :, :].rearrange("p h t -> p t h")
                    one(dve.tensor_scalar(topl[:, 0, :, :], by_tile, -1.0, None, ALU.mult))
                    for k in range(3):
                        one(dve.tensor_copy(top3[:, :, :, k], topl[:, k % 2, :, :]))
                        if k < 2:
                            one(dve.tensor_tensor(topl[:, (k + 1) % 2, :, :], topl[:, k % 2, :, :], top3[:, :, :, k], ALU.subtract))
                    dve.sem_inc(top3_ready, 1)
                    dve.wait_ge(topT_psum, g + 1)
                    for h in range(GH):
                        dve.tensor_copy(qT[KEY_ROWS:KEY_ROWS + 3, h, :], narrow[0][32 * h:32 * h + 3, :].bitcast(BF16)).then_inc(topT_ready, 1)
                    for c in range(2):
                        half = slice(c * TILES // 2, (c + 1) * TILES // 2)
                        dve.wait_ge(o_psum, g * 2 + c + 1)
                        o = narrow[c][:, :].rearrange("p (t h d) -> p t h d", h=GH, d=2 * DH)
                        rc = rden[:, half, :]
                        dve.reciprocal(rc, o[:, :, :, DH]).then_inc(rden_ready, 1)
                        dve.wait_ge(rden_ready, g * 2 + c + 1)
                        out = acts[:, half, bass.ds(hg * GH * DH, GH * DH)].rearrange("p t (h d) -> p t h d", d=DH)
                        dve.tensor_tensor(out, o[:, :, :, 0:DH], rc.rearrange("p t (h a) -> p t h a", a=1).to_broadcast([P, TILES // 2, GH, DH]),
                                          ALU.mult).then_inc(acts_ready, 1)
                    assert s.n == GROUP_STEPS
                for t in range(TILES):
                    n = b * TILES + t
                    dve.wait_ge(y_psum, n + 1)
                    xs = x[:, bass.ds(n, 1), :].rearrange("p a d -> p (a d)")
                    dve.tensor_tensor(xs, xs, S[t % 2][:, 0:D], ALU.add).then_inc(x_done, 1)

        @block.tensor
        def _(pe):
            pe.wait_ge(ready, 2)
            pe.wait_ge(consts_in, 16 * N_CONST)
            pe.sem_inc(pv_done, 1)
            pe.sem_inc(tr_psum, 1)
            pe.sem_inc(terms_ready, 1)

            def turn_rows(b, t):
                n = b * TILES + t
                pe.wait_ge(xn_ready, n + 1)
                if t >= 2:
                    pe.wait_ge(xT_ready, n - 1)
                for c in range(DC):
                    i = pe.transpose(narrow[t % 2][:, c * P:(c + 1) * P], xn[:, t % 2, c * P:(c + 1) * P], ident[:, :])
                i.then_inc(xT_psum, 1)

            def project(b, t):
                n = b * TILES + t
                pe.wait_ge(xT_ready, n + 1)
                if t >= 2:
                    pe.wait_ge(p_read, n - 1)
                    pe.wait_ge(v_ready, n - 1)
                for lo, hi in ((0, 2 * D), (2 * D, 3 * D)):
                    for c in range(DC):
                        i = pe.matmul(S[t % 2][:, lo:hi], xT[:, t % 2, c, :], w_kqv[:, c, lo:hi], start=(c == 0), stop=(c == DC - 1))
                i.then_inc(p_psum, 1)

            def score(out, lhs, rhs, rows, lo, hi, diagonal):
                for c in range(2):
                    a, e = max(lo, c * 512), min(hi, (c + 1) * 512)
                    if a < e:
                        masked = diagonal is not None and a <= diagonal < e
                        i = pe.matmul(out[:, a:e], lhs, rhs[0:rows, a:e], start=True, stop=not masked)
                        if masked:
                            i = pe.matmul(out[:, diagonal:diagonal + P], ident16[:, :], mask16[:, :], start=False, stop=True)
                return i

            with pe.Fori(0, BATCH) as b:
                turn_rows(b, 0)
                for t in range(TILES):
                    if t + 1 < TILES:
                        turn_rows(b, t + 1)
                    project(b, t)
                pe.wait_ge(p_read, (b + 1) * TILES)
                pe.wait_ge(v_ready, (b + 1) * TILES)
                pe.sem_inc(waited, 1)
                with pe.Fori(0, GROUPS) as hg:
                    g = b * GROUPS + hg
                    pe.wait_ge(terms_ready, g + 2)
                    pe.wait_ge(acts_ready, 2 * g + 1)
                    for k in range(2 * GH):
                        if k >= 2:
                            pe.wait_ge(tr_ready, g * 2 * GH + k - 1)
                        for t in range(TILES):
                            i = pe.transpose(narrow[k % 2][0:KEY_ROWS, :].bitcast(BF16)[:, t * P:(t + 1) * P], terms[:, k // GH, t, k % GH, :], ident16[:, :])
                        i.then_inc(tr_psum, 1)
                    for h in range(GH):
                        pe.wait_ge(tr_ready, g * 2 * GH + GH + h + 1)
                        for i in range(TILES):
                            n = h * TILES + i
                            if n >= 2:
                                pe.wait_ge(top_ready, g * GH * TILES + n - 1)
                            score(S[n % 2], qT[0:KEY_ROWS, h, i * P:(i + 1) * P], kT[:, h, :], KEY_ROWS, 0, (i + 1) * P, i * P).then_inc(s1_psum, 1)
                    pe.wait_ge(top3_ready, g + 1)
                    for t in range(TILES):
                        i = pe.transpose(narrow[0][:, :].bitcast(BF16)[:, t * P:(t + 1) * P], top3[:, t, :, :].rearrange("p h k -> p (h k)"), ident16[:, :])
                    i.then_inc(topT_psum, 1)

                    def weigh(j):
                        pe.wait_ge(cut_ready, (g * TILES + j + 1) * GH)
                        for c in range(2):
                            lo, hi = max(j * P, c * 512), (c + 1) * 512
                            if lo < hi:
                                for h in range(GH):
                                    i = pe.matmul(O[32 * h:32 * h + 32, lo:hi], vg[:, j, h, :], probs[:, j % 2, h, lo:hi],
                                                  start=(j == 0), stop=(hi == (j + 1) * P), tile_position=(0, 32 * h))
                        i.then_inc(pv_done, 1)

                    for j in range(TILES):
                        for h in range(GH):
                            n = j * GH + h
                            if j == 0:
                                pe.wait_ge(topT_ready, g * GH + h + 1)
                            if n >= 2:
                                pe.wait_ge(exp_ready, g * GH * TILES + n - 1)
                            score(S[n % 2], kT[0:KEY_ROWS + 3, h, j * P:(j + 1) * P], qT[:, h, :], KEY_ROWS + 3, j * P, SEQ, None).then_inc(s2_psum, 1)
                        if j:
                            weigh(j - 1)
                    weigh(TILES - 1)
                    for c in range(2):
                        pe.wait_ge(oT_ready, g * 2 + c + 1)
                        for t in range(4):
                            i = pe.transpose(narrow[c][:, t * P:(t + 1) * P], oT[:, (4 * c + t) * P:(4 * c + t + 1) * P], ident[:, :])
                        i.then_inc(o_psum, 1)
                pe.wait_ge(acts_ready, 2 * GROUPS * (b + 1) + 1)
                for t in range(TILES + 1):
                    n = b * TILES + t
                    if t < TILES:
                        if t >= 2:
                            pe.wait_ge(aT_ready, n - 1)
                        for c in range(DC):
                            i = pe.transpose(narrow[t % 2][:, c * P:(c + 1) * P], acts[:, t, c * P:(c + 1) * P], ident[:, :])
                        i.then_inc(aT_psum, 1)
                    if t:
                        pe.wait_ge(aT_ready, n)
                        if t >= 3:
                            pe.wait_ge(x_done, n - 2)
                        for c in range(DC):
                            i = pe.matmul(S[(t - 1) % 2][:, 0:D], aT[:, (t - 1) % 2, c, :], w_o[:, c, :], start=(c == 0), stop=(c == DC - 1))
                        i.then_inc(y_psum, 1)
                pe.wait_ge(x_done, (b + 1) * TILES)
                pe.sem_inc(waited, 1)


def chunks(a):
    return a.reshape(-1, P, a.shape[-1]).transpose(1, 0, 2)


def on_three(row):
    out = np.zeros((P, row.size), np.float32)
    for p in (0, 32, 64):
        out[p] = row.reshape(-1)
    return out


def rope_tables():
    half = 32
    pos = np.arange(SEQ, dtype=np.float32)
    freq = np.float32(10000.0) ** (-np.arange(half, dtype=np.float32) / np.float32(half))
    angle = pos[:, None] * freq[None, :]
    sin, cos = np.sin(angle), np.cos(angle)
    ga = np.stack([np.concatenate([cos, cos], 1), np.concatenate([-sin, sin], 1)])
    ga = ga.reshape(2, TILES, P, 2 * half).transpose(2, 0, 1, 3)
    d = 16
    freq = np.float32(1.0) / np.float32(10000.0) ** (np.arange(0, d, 2, dtype=np.float32) / np.float32(d))
    angle = pos[:, None] * freq[None, :]
    ca = np.stack([np.cos(angle), np.sin(angle)])
    ca = ca.reshape(2, TILES, P, d // 2).transpose(2, 0, 1, 3)
    return ga.astype(np.float32), ca.astype(np.float32)


def lay(i):
    ga_rope, ca_rope = rope_tables()
    order = [1, 0, 2, 3]
    heads = np.stack([i["L0_attn_gamma"][order], i["L0_attn_beta"][order]])
    tok = np.arange(P)
    dist = np.minimum(np.abs(tok[:, None] - tok[None, :]), 32)
    same = tok[:, None] // 64 == tok[None, :] // 64
    out = {
        "ident": np.eye(P, dtype=np.float32),
        "ga_w": chunks(np.concatenate([i["L0_attn_Wv"], i["L0_attn_Wg"], i["L0_attn_Wqk"]], 0).T),
        "ga_wo": chunks(i["L0_attn_Wo"].T),
        "ga_rope": ga_rope,
        "ga_heads": np.broadcast_to(heads, (P, 2, 4, 64)),
        "ga_bias": np.where(same, i["L0_attn_pos_emb"][dist], np.float32(-1e30)),
        "ga_ln1": np.stack([i["L0_attn_ln1_w"].reshape(2, P).T, i["L0_attn_ln1_b"].reshape(2, P).T], 1),
        "ga_ln2": np.broadcast_to(np.stack([i["L0_attn_ln2_w"], i["L0_attn_ln2_b"]]), (P, 2, 256)),
        "ga_brow": on_three(np.concatenate([i["L0_attn_bv"], i["L0_attn_bg"], i["L0_attn_bqk"], i["L0_attn_bo"]])),
    }
    out.update(lay_rest(i, ca_rope))
    return {k: np.ascontiguousarray(v) for k, v in out.items()}


def lay_rest(i, ca_rope):
    tok = np.arange(P)
    misc = np.concatenate([tok[:, None] < tok[None, :]] + [np.broadcast_to(r, (P, r.size)) for r in
                          (np.arange(EXPERTS), P * np.arange(ALL_TILES), np.arange(ROUTED))], 1).astype(np.float32)
    up0 = np.concatenate([i["L0_ffn_w1"], i["L0_ffn_w3"]], 2)
    up1 = np.concatenate([i["L1_ffn_sWu"][None], i["L1_ffn_Wu"]], 0).transpose(0, 2, 1)
    down1 = np.concatenate([i["L1_ffn_sWd"][None], i["L1_ffn_Wd"]], 0).transpose(0, 2, 1)
    each = lambda w: np.stack([chunks(e) for e in w])
    kqv = i["L1_attn_W_KQV"].T
    return {
        "ca_w": chunks(kqv), "ca_wo": chunks(i["L1_attn_W_O"].T), "ca_rope": ca_rope,
        "ca_mask": np.where(tok[None, :] > tok[:, None], np.float32(-1e30), np.float32(0)),
        "moe_misc": misc,
        "m0_gate": chunks(i["L0_ffn_gate_w"].T), "m0_up": each(up0), "m0_down": each(i["L0_ffn_w2"]),
        "m1_gate": chunks(i["L1_ffn_gate_w"].T), "m1_up": each(up1), "m1_down": each(down1),
        "m1_gbias": np.broadcast_to(i["L1_ffn_gate_bias"], (P, EXPERTS)),
        "m1_bias": np.concatenate([np.concatenate([i["L1_ffn_sbu"][None], i["L1_ffn_bu"]], 0),
                                   np.concatenate([i["L1_ffn_sbd"][None], i["L1_ffn_bd"]], 0)], 1),
    }


def program(nc, io, out):
    at_most = (ROUTED + ALL_TILES) * P
    rows = nc.dram_tensor("expert_rows", [at_most, D], F32).ap()
    results = nc.dram_tensor("expert_results", [at_most, D], F32).ap()
    between = [nc.dram_tensor(f"x_{k}", [BATCH, SEQ, D], F32).ap() for k in range(3)]
    gated_attention(nc, io, io["x"], between[0])
    experts(nc, io, between[0], between[1], rows, results, 0)
    causal_attention(nc, io, between[1], between[2])
    experts(nc, io, between[2], out, rows, results, 1)


def kernel(**inputs):
    import concourse.bacc as bacc
    from concourse.bass_utils import run_bass_kernel_spmd

    nc = bacc.Bacc("TRN2", target_bir_lowering=False, num_devices=1)
    arrays = lay({k: np.asarray(v) for k, v in inputs.items()})
    arrays["x"] = np.ascontiguousarray(inputs["L0_attn_x"])
    io = {k: nc.dram_tensor(f"in_{k}", a.shape, mybir.dt.from_np(a.dtype), kind="ExternalInput").ap() for k, a in arrays.items()}
    out = nc.dram_tensor("out", [BATCH, SEQ, D], F32, kind="ExternalOutput").ap()
    program(nc, io, out)
    r = run_bass_kernel_spmd(nc, [{f"in_{k}": a for k, a in arrays.items()}], core_ids=[0])
    return r.results[0]["out"]
```

```python
from contextlib import ExitStack

import concourse.bass as bass
import numpy as np
from concourse import mybir

F32 = mybir.dt.float32
BF16 = mybir.dt.bfloat16
U32 = mybir.dt.uint32
I32 = mybir.dt.int32
ALU = mybir.AluOpType
ACT = mybir.ActivationFunctionType
AX = mybir.AxisListType

P = 128
BATCH, SEQ, D = 4, 1024, 256
TILES = SEQ // P
ALL_TILES = BATCH * TILES
DC = D // P
EPS = 1e-5


class Steps:

    def __init__(self, engine, semaphore, base=0):
        self.engine, self.semaphore, self.base, self.n = engine, semaphore, base, 0

    def do(self, instruction):
        self.n += 1
        return instruction.then_inc(self.semaphore, 1)

    def done(self):
        self.engine.wait_ge(self.semaphore, self.base + self.n)


class Memory:

    def __init__(self, nc, stack, tag):
        self.nc, self.stack, self.tag, self.sems = nc, stack, tag, []
        stack.callback(self.clear)

    def clear(self):
        self.nc.clear_and_free_semaphores(self.sems)
        self.nc.all_engine_barrier()

    def sb(self, name, shape, dtype=F32):
        return self.stack.enter_context(self.nc.sbuf_tensor(f"{self.tag}_{name}", shape, dtype))

    def banks(self, n):
        return [self.stack.enter_context(self.nc.psum_tensor(f"{self.tag}_bank{i}", [P, 512], F32)) for i in range(n)]

    def sem(self, name):
        self.sems.append(self.nc.alloc_semaphore(f"{self.tag}_{name}"))
        return self.sems[-1]


def split_bias(steps, rows, left, table):
    v = steps.engine
    for k, p in enumerate((0, 32, 64)):
        row, rest, part = rows[p:p + 1, :], left[p:p + 1, :], table[p:p + 1, :]
        for _ in range(k):
            steps.do(v.tensor_copy(part, row)); steps.done()
            steps.do(v.tensor_tensor(rest, row, part, ALU.subtract)); steps.done()
            steps.do(v.tensor_copy(row, rest)); steps.done()
        steps.do(v.tensor_copy(part, row)); steps.done()


QK, HID, GROUP = 64, 512, 64
HC = HID // P
NVG = 2 * HID + QK


def gated_attention(nc, io, x_in, x_out):
    with ExitStack() as stack:
        m = Memory(nc, stack, "ga")
        sb, sem = m.sb, m.sem
        x = sb("x", [P, ALL_TILES, D])
        w_vgk = sb("w_vgk", [P, DC, NVG])
        w_o = sb("w_o", [P, HC, D])
        ident = sb("ident", [P, P])
        rope = sb("rope", [P, 2, TILES, QK])
        heads_wb = sb("heads_wb", [P, 2, 4, QK])
        group_bias = sb("group_bias", [P, P])
        ln1 = sb("ln1", [P, 2, DC])
        ln2 = sb("ln2", [P, 2, D])
        brow = sb("brow", [P, NVG + D])
        bleft = sb("bleft", [P, NVG + D])
        bparts = sb("bparts", [P, NVG + D], BF16)
        ones = sb("ones", [P, P], BF16)
        stats = sb("stats", [P, ALL_TILES, 6])
        mv = sb("mv", [P, ALL_TILES, 2])
        root = sb("root", [P, ALL_TILES])
        r1 = sb("r1", [P, ALL_TILES])
        var2 = sb("var2", [P, ALL_TILES])
        rstd = sb("rstd", [P, ALL_TILES])
        xn = sb("xn", [P, 2, D])
        xT = sb("xT", [P, 2, DC, P])
        v = sb("v", [P, TILES, HID])
        gate = sb("gate", [P, TILES, HID])
        qk = sb("qk", [P, 2, QK])
        hm = sb("hm", [P, 4, QK])
        hb = sb("hb", [P, 4, QK])
        hc = sb("hc", [P, 4, QK])
        hs = sb("hs", [P, 4, QK])
        heads = sb("heads", [P, 2, 5, QK])
        headsT = sb("headsT", [P, TILES, 2, P])
        z = sb("z", [P, P])
        attnT = sb("attnT", [P, TILES, P])
        kv = sb("kv", [P, HID])
        go = sb("go", [P, 2, HID])
        goT = sb("goT", [P, 2, HC, P])
        y = sb("y", [P, TILES, D])
        ystats = sb("ystats", [P, TILES, 6])
        ymv = sb("ymv", [P, TILES, 2])
        yroot = sb("yroot", [P, TILES])
        yrstd = sb("yrstd", [P, TILES])
        epst = sb("epst", [P, 1])

        bT, bR, bV, bG, bQ, bS, bKV, bY = m.banks(8)
        bO = [bV, bG]
        bGT = [bQ, bS]

        consts_in = sem("consts_in")
        x_loaded = sem("x_loaded")
        dve_step = sem("dve_step")
        ready = sem("ready")
        var_ready, root_ready = sem("var_ready"), sem("root_ready")
        xn_ready, xT_psum, xT_ready = sem("xn_ready"), sem("xT_psum"), sem("xT_ready")
        v_psum, g_psum, q_psum = sem("v_psum"), sem("g_psum"), sem("q_psum")
        v_ready, g_ready, q_ready = sem("v_ready"), sem("g_ready"), sem("q_ready")
        heads_ready, headsT_psum, headsT_ready = sem("heads_ready"), sem("headsT_psum"), sem("headsT_ready")
        s_psum, attn_ready = sem("s_psum"), sem("attn_ready")
        kv_psum, kv_ready = sem("kv_psum"), sem("kv_ready")
        o_psum, go_ready, goT_psum, goT_ready = sem("o_psum"), sem("go_ready"), sem("goT_psum"), sem("goT_ready")
        y_psum, y_ready = sem("y_psum"), sem("y_ready")
        yvar_ready, yroot_ready = sem("yvar_ready"), sem("yroot_ready")
        x_done, stored = sem("x_done"), sem("stored")
        waited = sem("waited")
        N_CONST = 9

        block = stack.enter_context(nc.Block())

        @block.sync
        def _(sp):
            for b in range(BATCH):
                sp.dma_start(x[:, b * TILES:(b + 1) * TILES, :], x_in[b].rearrange("(t p) d -> p t d", p=P)).then_inc(x_loaded, 16)
            with sp.Fori(0, BATCH) as b:
                sp.wait_ge(x_done, b + 1)
                sp.dma_start(x_out[b].rearrange("(t p) d -> p t d", p=P), x[:, bass.ds(b * TILES, TILES), :]).then_inc(stored, 16)
            sp.wait_ge(stored, 16 * BATCH)

        @block.gpsimd
        def _(pool):
            pool.memset(ones[:, :], 1.0).then_inc(ready, 1)
            pool.memset(bparts[:, :], 0.0).then_inc(ready, 1)
            pool.memset(kv[:, :], 0.0).then_inc(ready, 1)
            pool.memset(heads[:, :, :, :], 0.0).then_inc(ready, 1)

        @block.scalar
        def _(act):
            for dst, src in ((w_vgk[:, :, :], io["ga_w"]), (w_o[:, :, :], io["ga_wo"]), (ident[:, :], io["ident"]),
                             (rope[:, :, :, :], io["ga_rope"]), (heads_wb[:, :, :, :], io["ga_heads"]),
                             (group_bias[:, :], io["ga_bias"]), (ln1[:, :, :], io["ga_ln1"]), (ln2[:, :, :], io["ga_ln2"]),
                             (brow[:, :], io["ga_brow"])):
                act.dma_start(dst, src).then_inc(consts_in, 16)
            for k, s in enumerate((mv[:, :, 1], var2[:, :])):
                act.wait_ge(var_ready, k + 1)
                act.activation(root[:, :], s, ACT.Sqrt, bias=epst[:, 0:1]).then_inc(root_ready, 1)
            with act.Fori(0, BATCH) as b:
                n0 = b * TILES
                for t in range(TILES):
                    act.wait_ge(xT_psum, n0 + t + 1)
                    for c in range(DC):
                        i = act.activation(xT[:, t % 2, c, :], bT[:, c * P:(c + 1) * P], ACT.Identity,
                                           bias=ln1[:, 1, c:c + 1], scale=ln1[:, 0, c:c + 1])
                    i.then_inc(xT_ready, 1)
                    act.wait_ge(q_psum, n0 + t + 1)
                    act.activation(qk[:, t % 2, :], bQ[:, 0:QK], ACT.Silu).then_inc(q_ready, 1)
                    if t == 0:
                        act.wait_ge(o_psum, n0 + 1)
                    act.wait_ge(v_psum, n0 + t + 1)
                    act.activation(v[:, t, :], bV[:, :], ACT.Silu).then_inc(v_ready, 1)
                    act.wait_ge(g_psum, n0 + t + 1)
                    act.activation(gate[:, t, :], bG[:, :], ACT.Silu).then_inc(g_ready, 1)
                    act.wait_ge(headsT_psum, n0 + t + 1)
                    act.activation(headsT[:, t, :, :], bR[:, 0:2 * P].rearrange("p (c n) -> p c n", c=2), ACT.Identity).then_inc(headsT_ready, 1)
                act.wait_ge(kv_psum, b + 1)
                act.activation(kv[0:QK, :], bKV[0:QK, :], ACT.Identity, scale=1.0 / SEQ).then_inc(kv_ready, 1)
                for t in range(TILES):
                    act.wait_ge(goT_psum, n0 + t + 1)
                    act.activation(goT[:, t % 2, :, :], bGT[t % 2][:, :].rearrange("p (c n) -> p c n", c=HC), ACT.Identity).then_inc(goT_ready, 1)
                    act.wait_ge(y_psum, n0 + t + 1)
                    act.activation(y[:, t, :], bY[:, 0:D], ACT.Identity).then_inc(y_ready, 1)
                act.wait_ge(yvar_ready, b + 1)
                act.activation(yroot[:, :], ymv[:, :, 1], ACT.Sqrt, bias=epst[:, 0:1]).then_inc(yroot_ready, 1)

        @block.vector
        def _(dve):
            s = Steps(dve, dve_step)
            dve.wait_ge(ready, 4)
            dve.wait_ge(consts_in, 16 * N_CONST)
            s.do(dve.memset(epst[:, :], EPS))
            split_bias(s, brow, bleft, bparts)
            s.done()
            dve.sem_inc(ready, 1)
            dve.wait_ge(x_loaded, 16 * BATCH)
            for n in range(ALL_TILES):
                s.do(dve.bn_stats(stats[:, n, :], x[:, n, :]))
            s.done()
            for n in range(ALL_TILES):
                s.do(dve.bn_aggr(mv[:, n, :], stats[:, n, :]))
            s.done()
            dve.sem_inc(var_ready, 1)
            dve.wait_ge(root_ready, 1)
            s.do(dve.reciprocal(r1[:, :], root[:, :])); s.done()
            s.do(dve.tensor_tensor(var2[:, :], r1[:, :], r1[:, :], ALU.mult)); s.done()
            s.do(dve.tensor_tensor(var2[:, :], var2[:, :], mv[:, :, 1], ALU.mult)); s.done()
            dve.sem_inc(var_ready, 1)
            dve.wait_ge(root_ready, 2)
            s.do(dve.reciprocal(rstd[:, :], root[:, :])); s.done()
            s.do(dve.tensor_tensor(rstd[:, :], rstd[:, :], r1[:, :], ALU.mult)); s.done()
            once = s.n

            def normalise(b, t):
                n = b * TILES + t
                if t >= 2:
                    dve.wait_ge(xT_psum, n - 1)
                dve.tensor_scalar(xn[:, t % 2, :], x[:, bass.ds(n, 1), :].rearrange("p a d -> p (a d)"),
                                  mv[:, bass.ds(n, 1), 0], rstd[:, bass.ds(n, 1)],
                                  ALU.subtract, ALU.mult).then_inc(xn_ready, 1)

            def make_heads(b, t):
                n = b * TILES + t
                dve.wait_ge(q_ready, n + 1)
                if t >= 2:
                    dve.wait_ge(headsT_psum, n - 1)
                    if t >= 3:
                        dve.wait_ge(s_psum, n - 2)
                q4 = qk[:, t % 2, None, :].to_broadcast([P, 4, QK])
                s.do(dve.tensor_tensor(hm[:, :, :], q4, heads_wb[:, 0, :, :], ALU.mult)); s.done()
                s.do(dve.tensor_tensor(hb[:, :, :], hm[:, :, :], heads_wb[:, 1, :, :], ALU.add)); s.done()
                cos = rope[:, 0, t, None, :].to_broadcast([P, 4, QK])
                s.do(dve.tensor_tensor(hc[:, :, :], hb[:, :, :], cos, ALU.mult))
                for a, c in ((0, 1), (1, 0)):
                    half = QK // 2
                    sin = rope[:, 1, t, None, a * half:(a + 1) * half].to_broadcast([P, 4, half])
                    s.do(dve.tensor_tensor(hs[:, :, a * half:(a + 1) * half], hb[:, :, c * half:(c + 1) * half], sin, ALU.mult))
                s.done()
                dve.tensor_tensor(heads[:, t % 2, 0:2, :], hc[:, 0:2, :], hs[:, 0:2, :], ALU.add)
                s.do(dve.tensor_tensor(heads[:, t % 2, 3:5, :], hc[:, 2:4, :], hs[:, 2:4, :], ALU.add)); s.done()
                dve.sem_inc(heads_ready, 1)

            def attention(b, t):
                dve.wait_ge(s_psum, b * TILES + t + 1)
                s.do(dve.scalar_tensor_tensor(out=z[:, :], in0=bS[:, 0:P], scalar=1.0 / GROUP, in1=group_bias[:, :],
                                              op0=ALU.mult, op1=ALU.add)); s.done()
                s.do(dve.scalar_tensor_tensor(out=attnT[:, t, :], in0=z[:, :], scalar=0.0, in1=z[:, :],
                                              op0=ALU.max, op1=ALU.mult)); s.done()
                dve.sem_inc(attn_ready, 1)

            def gated(b, t):
                n = b * TILES + t
                dve.wait_ge(o_psum, n + 2)
                if t >= 2:
                    dve.wait_ge(goT_psum, n - 1)
                dve.wait_ge(g_ready, n + 1)
                dve.tensor_tensor(go[:, t % 2, :], bO[t % 2][:, :], gate[:, t, :], ALU.mult).then_inc(go_ready, 1)

            def row_stats(b, t):
                dve.wait_ge(y_ready, b * TILES + t + 1)
                s.do(dve.bn_stats(ystats[:, t, :], y[:, t, :]))

            with dve.Fori(0, BATCH) as b:
                PER = TILES * (6 + 2 + 1 + 1 + 1) + 4
                s.base, s.n = once + b * PER, 0
                normalise(b, 0)
                normalise(b, 1)
                for t in range(TILES):
                    make_heads(b, t)
                    if t + 2 < TILES:
                        normalise(b, t + 2)
                    if t:
                        attention(b, t - 1)
                attention(b, TILES - 1)
                for t in range(TILES):
                    gated(b, t)
                    if t:
                        row_stats(b, t - 1)
                row_stats(b, TILES - 1)
                s.done()
                dve.sem_inc(waited, 1)
                for t in range(TILES):
                    s.do(dve.bn_aggr(ymv[:, t, :], ystats[:, t, :]))
                s.done()
                dve.sem_inc(yvar_ready, 1)
                dve.wait_ge(yroot_ready, b + 1)
                s.do(dve.reciprocal(yrstd[:, :], yroot[:, :])); s.done()
                for t in range(TILES):
                    s.do(dve.tensor_scalar(y[:, t, :], y[:, t, :], ymv[:, t, 0:1], yrstd[:, t:t + 1], ALU.subtract, ALU.mult))
                s.done()
                wide = [P, TILES, D]
                s.do(dve.tensor_tensor(y[:, :, :], y[:, :, :], ln2[:, 0, None, :].to_broadcast(wide), ALU.mult)); s.done()
                s.do(dve.tensor_tensor(y[:, :, :], y[:, :, :], ln2[:, 1, None, :].to_broadcast(wide), ALU.add)); s.done()
                xs = x[:, bass.ds(b * TILES, TILES), :]
                s.do(dve.tensor_tensor(xs, xs, y[:, :, :], ALU.add)); s.done()
                dve.sem_inc(x_done, 1)
                assert s.n == PER

        @block.tensor
        def _(pe):
            pe.wait_ge(ready, 5)
            pe.sem_inc(o_psum, 1)

            def turn_rows(b, t):
                n = b * TILES + t
                pe.wait_ge(xn_ready, n + 1)
                if t:
                    pe.wait_ge(xT_ready, n)
                for c in range(DC):
                    i = pe.transpose(bT[:, c * P:(c + 1) * P], xn[:, t % 2, c * P:(c + 1) * P], ident[:, :])
                i.then_inc(xT_psum, 1)

            def project(b, t):
                n = b * TILES + t
                pe.wait_ge(xT_ready, n + 1)
                if t:
                    pe.wait_ge(g_ready, n)
                for bank, at, width, signal in ((bQ, 2 * HID, QK, q_psum), (bV, 0, HID, v_psum), (bG, HID, HID, g_psum)):
                    for c in range(DC):
                        pe.matmul(bank[:, 0:width], xT[:, t % 2, c, :], w_vgk[:, c, at:at + width], start=(c == 0), stop=False)
                    pe.matmul(bank[:, 0:width], ones[:, :], bparts[:, at:at + width], start=False, stop=True).then_inc(signal, 1)

            def turn_heads(b, t):
                n = b * TILES + t
                pe.wait_ge(heads_ready, n + 1)
                if t:
                    pe.wait_ge(headsT_ready, n)
                for c in range(2):
                    i = pe.transpose(bR[:, c * P:(c + 1) * P], heads[:, t % 2, 2 * c:2 * c + 2, :].rearrange("p a d -> p (a d)"), ident[:, :])
                i.then_inc(headsT_psum, 1)

            def scores(b, t):
                n = b * TILES + t
                pe.wait_ge(v_ready, n + 1)
                i = pe.matmul(bKV[0:QK, :], heads[:, t % 2, 4, :], v[:, t, :], start=(t == 0), stop=(t == TILES - 1))
                if t == TILES - 1:
                    i.then_inc(kv_psum, 1)
                pe.wait_ge(headsT_ready, n + 1)
                if t:
                    pe.wait_ge(attn_ready, n)
                pe.matmul(bS[:, 0:P], headsT[:, t, 1, :], headsT[:, t, 0, :], start=True, stop=True).then_inc(s_psum, 1)

            def outputs(b, t):
                n = b * TILES + t
                if t == 0:
                    pe.wait_ge(kv_ready, b + 1)
                    pe.wait_ge(g_ready, (b + 1) * TILES)
                    pe.wait_ge(attn_ready, (b + 1) * TILES)
                if t >= 2:
                    pe.wait_ge(go_ready, n - 1)
                pe.matmul(bO[t % 2][:, :], attnT[:, t, :], v[:, t, :], start=True, stop=False)
                pe.matmul(bO[t % 2][:, :], headsT[:, t, 0, :], kv[:, :], start=False, stop=True).then_inc(o_psum, 1)

            def turn_gated(b, t):
                n = b * TILES + t
                pe.wait_ge(go_ready, n + 1)
                if t >= 2:
                    pe.wait_ge(goT_ready, n - 1)
                for c in range(HC):
                    i = pe.transpose(bGT[t % 2][:, c * P:(c + 1) * P], go[:, t % 2, c * P:(c + 1) * P], ident[:, :])
                i.then_inc(goT_psum, 1)

            def project_out(b, t):
                n = b * TILES + t
                pe.wait_ge(goT_ready, n + 1)
                if t:
                    pe.wait_ge(y_ready, n)
                for c in range(HC):
                    pe.matmul(bY[:, 0:D], goT[:, t % 2, c, :], w_o[:, c, :], start=(c == 0), stop=False)
                pe.matmul(bY[:, 0:D], ones[:, :], bparts[:, NVG:NVG + D], start=False, stop=True).then_inc(y_psum, 1)

            with pe.Fori(0, BATCH) as b:
                turn_rows(b, 0)
                for t in range(TILES):
                    project(b, t)
                    if t + 1 < TILES:
                        turn_rows(b, t + 1)
                    if t:
                        scores(b, t - 1)
                    turn_heads(b, t)
                scores(b, TILES - 1)
                for t in range(TILES + 2):
                    if t < TILES:
                        outputs(b, t)
                    if 1 <= t <= TILES:
                        turn_gated(b, t - 1)
                    if t >= 2:
                        project_out(b, t - 2)


EXPERTS, TOPK, UP = 8, 2, 1024
ASSIGNED = TOPK * BATCH * SEQ
ROUTED = (ASSIGNED + EXPERTS * (P - 1)) // P
ROUTED += ROUTED % 2


def experts(nc, io, x_in, x_out, rows, results, layer):
    gated = layer == 0
    shared = 0 if gated else 1
    n_exp = EXPERTS + shared
    hidden = UP // 2 if gated else UP
    hc = hidden // P
    SH = shared * ALL_TILES
    BLOCKS = SH + ROUTED
    with ExitStack() as stack:
        m = Memory(nc, stack, f"moe{layer}")
        sb, sem = m.sb, m.sem
        w_up = sb("w_up", [P, n_exp, DC, UP])
        w_down = sb("w_down", [P, n_exp, hc, D])
        if gated:
            xn_all = sb("xn_all", [P, ALL_TILES, D])
            LATE = n_exp
        else:
            LATE = n_exp - ALL_TILES * D // (DC * UP)
            xn_all = w_up[:, LATE:n_exp, :, :].rearrange("p e c n -> p (e c n)").rearrange("p (t d) -> p t d", d=D)
        spare = None if gated else w_down[:, LATE:n_exp, :, :].rearrange("p e c n -> p (e c n)")
        used = [0]

        def early(name, shape, dtype=F32):
            if gated:
                return sb(name, shape, dtype)
            n = int(np.prod(shape[1:])) * (2 if dtype == BF16 else 4) // 4
            view = spare[0:shape[0], used[0]:used[0] + n]
            used[0] += n
            if dtype != F32:
                view = view.bitcast(dtype)
            if len(shape) == 3:
                view = view.rearrange("p (a b) -> p a b", b=shape[2])
            if len(shape) == 4:
                view = view.rearrange("p (a b c) -> p a b c", b=shape[2], c=shape[3])
            return view

        ident = sb("ident", [P, P])
        misc = early("misc", [P, P + EXPERTS + ALL_TILES + ROUTED])
        w_gate = early("w_gate", [P, DC, EXPERTS])
        gbias = early("gbias", [P, EXPERTS])
        before = early("before", [P, P], BF16)
        ones = sb("ones", [P, P], BF16)
        zero = sb("zero", [P, 4 * D])
        if not gated:
            b_row = early("b_row", [n_exp, UP + D])
            b_parts = early("b_parts", [n_exp, 3, UP + D], BF16)
            b_table = sb("b_table", [P, n_exp, UP + D], BF16)
        stats = early("stats", [P, ALL_TILES, 6])
        mv = early("mv", [P, ALL_TILES, 2])
        root = early("root", [P, ALL_TILES])
        rstd = early("rstd", [P, ALL_TILES])
        epst = sb("epst", [P, 1])
        te = [P, ALL_TILES, EXPERTS]
        logit = early("logit", te)
        prob = early("prob", te)
        top = early("top", te)
        topi = early("topi", te, U32)
        topf = early("topf", te)
        small = early("small", [P, ALL_TILES])
        hot = early("hot", [P, TOPK, ALL_TILES, EXPERTS])
        both = early("both", te)
        both16 = early("both16", te, BF16)
        upto = early("upto", te)
        place = early("place", te)
        picked = early("picked", te)
        over = early("over", [P, EXPERTS, ALL_TILES])
        nblk = early("nblk", [P, EXPERTS])
        blk_end = sb("blk_end", [P, EXPERTS])
        blk_start = early("blk_start", [P, EXPERTS])
        one8 = early("one8", [P, ALL_TILES])
        posf = early("posf", [P, TOPK, ALL_TILES])
        pos = sb("pos", [P, TOPK, ALL_TILES], U32)
        weight = sb("weight", [P, TOPK, ALL_TILES])
        passed = early("passed", [P, ROUTED, EXPERTS])
        ownerf = early("ownerf", [P, BLOCKS])
        owner = sb("owner", [P, BLOCKS], I32)
        xb = sb("xb", [P, 2, D])
        xT = sb("xT", [P, 2, DC, P])
        act_out = sb("act_out", [P, 2, hidden])
        h = sb("h", [P, 2, hidden]) if gated else act_out
        hT = sb("hT", [P, 2, hc, P])
        gT = hT[:, :, 0:2 * DC, :]
        yb = sb("yb", [P, 2, D])
        rest = sb("sums", [P, 2, 4, D]) if gated else act_out.rearrange("p s (k d) -> p s k d", d=D)
        y_in, x_res, part = rest[:, :, 0:TOPK + shared, :], rest[:, :, 3, :], yb

        bX, bU0, bU1, bU2, bU3, bH0, bH1, bY = m.banks(8)
        bU = [(bU0, bU1), (bU2, bU3)]

        consts_in, w_in, x_loaded = sem("consts_in"), sem("w_in"), [sem(f"x_loaded{q}") for q in range(4)]
        late_in = sem("late_in")
        ready, dve_step = sem("ready"), sem("dve_step")
        var_ready, root_ready, xn_ready = sem("var_ready"), sem("root_ready"), sem("xn_ready")
        gT_psum, gT_ready, logit_psum, logit_read = sem("gT_psum"), sem("gT_ready"), sem("logit_psum"), sem("logit_read")
        exp_in, exp_ready = sem("exp_in"), sem("exp_ready")
        both_ready, rank_psum, routed = sem("both_ready"), sem("rank_psum"), sem("routed")
        cleared, sent, copied = sem("cleared"), sem("sent"), sem("copied")
        b_ready, b_in = sem("b_ready"), sem("b_in")
        xb_in, xT_psum, xT_ready = [sem("xb_in0"), sem("xb_in1")], sem("xT_psum"), sem("xT_ready")
        u_psum, a_ready, h_ready = sem("u_psum"), sem("a_ready"), sem("h_ready")
        hT_psum, hT_ready, y_psum, yb_ready, yb_out = sem("hT_psum"), sem("hT_ready"), sem("y_psum"), sem("yb_ready"), [sem("yb_out0"), sem("yb_out1")]
        hT_ready2 = sem("hT_ready2")
        out_ready = sem("out_ready")
        gathered, res_in, stored = [[sem(f"{x}{q}") for q in range(2)] for x in ("gathered", "res_in", "stored")]
        sh_in = sem("sh_in")
        N_CONST = 3 + (2 if not gated else 0)
        HALF_TILES = ALL_TILES // 2

        SHARED_ROWS = ROUTED * P
        routed_rows, routed_results = rows[0:SHARED_ROWS, :], results[0:SHARED_ROWS, :]
        x_tiles = x_in.rearrange("b (t p) d -> p (b t) d", p=P)
        block = stack.enter_context(nc.Block())

        @block.sync
        def _(sp):
            for q in range(4):
                n = ALL_TILES // 4
                sp.dma_start(xn_all[:, q * n:(q + 1) * n, :], x_tiles[:, q * n:(q + 1) * n, :]).then_inc(x_loaded[q], 16)
            if not gated:
                sp.wait_ge(xn_ready, ALL_TILES)
                sp.dma_start(rows[SHARED_ROWS:SHARED_ROWS + SH * P, :].rearrange("(t p) d -> p t d", p=P), xn_all[:, :, :]).then_inc(copied, 16)
                sp.wait_ge(copied, 16)

            def load_block(t, origin):
                if t.n >= 2:
                    sp.wait_ge(xT_psum, t.j - 1)
                sp.dma_start(xb[:, t.side, :], rows[bass.ds(t.j * P + origin, P), :]).then_inc(xb_in[t.side], 16)

            def store_block(t, origin):
                sp.wait_ge(yb_ready, t.j + 1)
                sp.dma_start(results[bass.ds(t.j * P + origin, P), :], yb[:, t.side, :]).then_inc(yb_out[t.side], 16)

            def pass_blocks(first, end, origin):
                for side in range(2):
                    load_block(Turn(first // 2, side, first + side), origin)
                if first:
                    for side in range(2):
                        store_block(at(first - 2 + side), SHARED_ROWS)
                with sp.Fori(first // 2 + 1, end // 2) as pair:
                    for side in range(2):
                        load_block(Turn(pair, side, 2 + side), origin)
                        store_block(Turn(pair - 1, side, 2 + side), origin)

            if SH:
                pass_blocks(0, SH, SHARED_ROWS)
            sp.wait_ge(sent, 16 * TOPK * ALL_TILES)
            pass_blocks(SH, BLOCKS, -SH * P)
            for side in range(2):
                store_block(at(BLOCKS - 2 + side), -SH * P)
            for out in yb_out:
                sp.wait_ge(out, 8 * BLOCKS)
            with sp.Fori(0, ALL_TILES // 2) as i:
                for q in range(2):
                    n = 2 * i + q
                    sp.wait_ge(out_ready, n + 1)
                    sp.dma_start(x_res[:, q, :], x_tiles[:, bass.ds(n, 1), :].rearrange("p a d -> p (a d)")).then_inc(res_in[q], 16)
                    if shared:
                        sp.dma_start(y_in[:, q, TOPK, :], results[bass.ds(n * P + SHARED_ROWS, P), :]).then_inc(res_in[q], 16)

        @block.gpsimd
        def _(pool):
            if gated:
                pool.memset(zero[:, :], 0.0).then_inc(ready, 1)
            pool.memset(ones[:, :], 1.0).then_inc(ready, 1)
            if not gated:
                pool.memset(b_table[:, :, :], 0.0).then_inc(ready, 1)
            if gated:
                pool.wait_ge(ready, 1)
                per = P * 4
                for k in range(rows.shape[0] // per):
                    pool.dma_start(rows[k * per:(k + 1) * per, :].rearrange("(p r) d -> p (r d)", p=P), zero[:, :]).then_inc(cleared, 16)
                pool.wait_ge(cleared, 16 * (rows.shape[0] // per))
            pool.wait_ge(routed, 1)
            pool.wait_ge(xn_ready, ALL_TILES)
            for n in range(ALL_TILES):
                for k in range(TOPK):
                    pool.indirect_dma_start(routed_rows, bass.IndirectOffsetOnAxis(ap=pos_slot(pos, k, n), axis=0),
                                            xn_all[:, n, :], None).then_inc(sent, 16)
            if LATE < n_exp:
                pool.wait_ge(sent, 16 * TOPK * ALL_TILES)
                pool.wait_ge(copied, 16)
                pool.wait_ge(gT_psum, ALL_TILES // 2)
                pool.wait_ge(b_in, 16 * 3 * n_exp)
                for e in range(LATE, n_exp):
                    pool.dma_start(w_up[:, e, :, :], io[f"m{layer}_up"][e]).then_inc(late_in, 16)
                    pool.dma_start(w_down[:, e, :, :], io[f"m{layer}_down"][e]).then_inc(late_in, 16)
            for out in yb_out:
                pool.wait_ge(out, 8 * BLOCKS)
            for n in range(ALL_TILES):
                if n >= 2:
                    pool.wait_ge(out_ready, n + 1)
                for k in range(TOPK):
                    pool.indirect_dma_start(y_in[:, n % 2, k, :], None, routed_results,
                                            bass.IndirectOffsetOnAxis(ap=pos_slot(pos, k, n), axis=0)).then_inc(gathered[n % 2], 16)

        @block.scalar
        def _(act):
            consts = [(ident[:, :], io["ident"]), (misc[:, :], io["moe_misc"]), (w_gate[:, :, :], io[f"m{layer}_gate"])]
            if not gated:
                consts += [(gbias[:, :], io["m1_gbias"]), (b_row[:, :], io["m1_bias"])]
            for dst, src in consts:
                act.dma_start(dst, src).then_inc(consts_in, 16)
            for e in range(LATE):
                act.dma_start(w_up[:, e, :, :], io[f"m{layer}_up"][e]).then_inc(w_in, 16)
                act.dma_start(w_down[:, e, :, :], io[f"m{layer}_down"][e]).then_inc(w_in, 16)
            act.wait_ge(var_ready, 1)
            act.activation(root[:, :], mv[:, :, 1], ACT.Sqrt, bias=epst[:, 0:1]).then_inc(root_ready, 1)
            if not gated:
                act.wait_ge(b_ready, 1)
                act.wait_ge(ready, 2)
                for k in range(3):
                    for e in range(n_exp):
                        act.dma_start(b_table[k:k + 1, e, :], b_parts[e:e + 1, k, :]).then_inc(b_in, 16)
            for t in range(ALL_TILES // 2):
                act.wait_ge(gT_psum, t + 1)
                if t >= 2:
                    act.wait_ge(logit_psum, 2 * (t - 1))
                act.activation(gT[:, t % 2, :, :], bU[t % 2][0][:, :].rearrange("p (c n) -> p c n", c=2 * DC), ACT.Identity).then_inc(gT_ready, 1)
            act.wait_ge(exp_in, 1)
            act.activation(prob[:, :, :], logit[:, :, :], ACT.Exp if gated else ACT.Sigmoid).then_inc(exp_ready, 1)

            def turned(t):
                j, n = t.j, t.n
                act.wait_ge(xT_psum, j + 1)
                act.activation(xT[:, n % 2, :, :], bX[:, 0:DC * P].rearrange("p (c n) -> p c n", c=DC), ACT.Identity).then_inc(xT_ready, 1)

            def nonlinear(t):
                j, n = t.j, t.n
                act.wait_ge(u_psum, j + 1)
                if n >= 2:
                    act.wait_ge(h_ready if gated else hT_psum, j - 1)
                if gated:
                    act.activation(act_out[:, n % 2, :], bU[n % 2][0][:, :], ACT.Silu).then_inc(a_ready, 1)
                else:
                    for k in range(2):
                        i = act.activation(act_out[:, n % 2, k * 512:(k + 1) * 512], bU[n % 2][k][:, :], ACT.Gelu)
                    i.then_inc(a_ready, 1)

            def turned_hidden(t):
                j, n = t.j, t.n
                act.wait_ge(hT_psum, j + 1)
                if n >= 2:
                    act.wait_ge(y_psum, j - 1)
                act.activation(hT[:, n % 2, 0:4, :], bH0[:, :].rearrange("p (c n) -> p c n", c=4), ACT.Identity).then_inc(hT_ready, 1)

            turned(at(0))

            def act_block(t):
                j, n = t.j, t.n
                nonlinear(t)
                if n + 1 < BLOCKS:
                    turned(t.after())
                turned_hidden(t)
            for_blocks(act, BLOCKS, act_block)
            for q in range(2):
                act.sem_inc(stored[q], 16)
            with act.Fori(0, ALL_TILES // 2) as i:
                for q in range(2):
                    n = 2 * i + q
                    act.wait_ge(out_ready, n + 3)
                    act.dma_start(x_out.rearrange("b (t p) d -> p (b t) d", p=P)[:, bass.ds(n, 1), :].rearrange("p a d -> p (a d)"), part[:, q, :]).then_inc(stored[q], 16)
            for q in range(2):
                act.wait_ge(stored[q], 8 * ALL_TILES + 16)

        @block.vector
        def _(dve):
            s = Steps(dve, dve_step)
            one = lambda i: (s.do(i), s.done())
            one(dve.memset(epst[:, :], EPS))
            one(dve.memset(one8[:, :], 1.0))
            for q in range(4):
                dve.wait_ge(x_loaded[q], 16)
                for n in range(q * 8, q * 8 + 8):
                    s.do(dve.bn_stats(stats[:, n, :], xn_all[:, n, :]))
            s.done()
            for n in range(ALL_TILES):
                s.do(dve.bn_aggr(mv[:, n, :], stats[:, n, :]))
            s.done()
            dve.sem_inc(var_ready, 1)
            dve.wait_ge(root_ready, 1)
            one(dve.reciprocal(rstd[:, :], root[:, :]))
            for n in range(ALL_TILES):
                dve.tensor_scalar(xn_all[:, n, :], xn_all[:, n, :], mv[:, n, 0:1], rstd[:, n:n + 1],
                                  ALU.subtract, ALU.mult).then_inc(xn_ready, 1)
            dve.wait_ge(consts_in, 16 * N_CONST)
            one(dve.tensor_copy(before[:, :], misc[:, 0:P]))
            if not gated:
                for k in range(3):
                    one(dve.tensor_copy(b_parts[:, k, :], b_row[:, :]))
                    if k < 2:
                        one(dve.tensor_tensor(b_row[:, :], b_row[:, :], b_parts[:, k, :], ALU.subtract))
                dve.sem_inc(b_ready, 1)
            for n in range(ALL_TILES):
                dve.wait_ge(logit_psum, n + 1)
                lb = (bH0, bH1)[n % 2]
                if gated:
                    i = dve.tensor_copy(logit[:, n, :], lb[:, 0:EXPERTS])
                else:
                    i = dve.tensor_tensor(logit[:, n, :], lb[:, 0:EXPERTS], gbias[:, :], ALU.add)
                i.then_inc(logit_read, 1)
            dve.wait_ge(logit_read, ALL_TILES)
            wide = lambda a: a.rearrange("p (t a) -> p t a", a=1).to_broadcast(te)
            if gated:
                one(dve.tensor_reduce(small[:, :], logit[:, :, :], AX.X, ALU.max))
                one(dve.tensor_tensor(logit[:, :, :], logit[:, :, :], wide(small[:, :]), ALU.subtract))
            dve.sem_inc(exp_in, 1)
            dve.wait_ge(exp_ready, 1)
            if gated:
                one(dve.tensor_reduce(small[:, :], prob[:, :, :], AX.X, ALU.add))
                one(dve.reciprocal(small[:, :], small[:, :]))
                one(dve.tensor_tensor(prob[:, :, :], prob[:, :, :], wide(small[:, :]), ALU.mult))
            for n in range(ALL_TILES):
                s.do(dve.max(top[:, n, :], prob[:, n, :]))
            s.done()
            for n in range(ALL_TILES):
                s.do(dve.max_index(topi[:, n, :], top[:, n, :], prob[:, n, :]))
            s.done()
            one(dve.tensor_copy(topf[:, :, :], topi[:, :, :]))
            iota8 = misc[:, None, P:P + EXPERTS].to_broadcast(te)
            for k in range(TOPK):
                s.do(dve.tensor_tensor(hot[:, k, :, :], iota8, topf[:, :, k:k + 1].to_broadcast(te), ALU.is_equal))
            s.done()
            one(dve.tensor_tensor(both[:, :, :], hot[:, 0, :, :], hot[:, 1, :, :], ALU.add))
            one(dve.tensor_copy(both16[:, :, :], both[:, :, :]))
            dve.sem_inc(both_ready, 1)
            for k in range(TOPK):
                s.do(dve.tensor_copy(weight[:, k, :], top[:, :, k]))
            s.done()
            if not gated:
                one(dve.tensor_tensor(small[:, :], weight[:, 0, :], weight[:, 1, :], ALU.add))
                one(dve.tensor_scalar(small[:, :], small[:, :], 1e-6, None, ALU.add))
                one(dve.reciprocal(small[:, :], small[:, :]))
                for k in range(TOPK):
                    s.do(dve.tensor_tensor(weight[:, k, :], weight[:, k, :], small[:, :], ALU.mult))
                s.done()
            dve.wait_ge(rank_psum, 1)
            te_of = lambda bank: bank[:, 0:ALL_TILES * EXPERTS].rearrange("p (t e) -> p t e", e=EXPERTS)
            for e in range(EXPERTS):
                s.do(dve.tensor_tensor_scan(upto[:, :, e], one8[:, :], te_of(bU1)[:, :, e], 0.0, ALU.mult, ALU.add))
            s.done()
            one(dve.tensor_tensor(place[:, :, :], upto[:, :, :], te_of(bU1), ALU.subtract))
            one(dve.tensor_tensor(place[:, :, :], place[:, :, :], te_of(bU0), ALU.add))
            et = [P, EXPERTS, ALL_TILES]
            total = upto[:, ALL_TILES - 1, :].rearrange("p (e a) -> p e a", a=1).to_broadcast(et)
            mult128 = misc[:, None, P + EXPERTS:P + EXPERTS + ALL_TILES].to_broadcast(et)
            one(dve.tensor_tensor(over[:, :, :], total, mult128, ALU.is_gt))
            one(dve.tensor_reduce(nblk[:, :], over[:, :, :], AX.X, ALU.add))
            one(dve.tensor_tensor_scan(blk_end[:, :], one8[:, 0:EXPERTS], nblk[:, :], 0.0, ALU.mult, ALU.add))
            one(dve.tensor_tensor(blk_start[:, :], blk_end[:, :], nblk[:, :], ALU.subtract))
            one(dve.tensor_scalar(blk_start[:, :], blk_start[:, :], float(P), None, ALU.mult))
            one(dve.tensor_tensor(place[:, :, :], place[:, :, :], blk_start[:, None, :].to_broadcast(te), ALU.add))
            for k in range(TOPK):
                one(dve.tensor_tensor(picked[:, :, :], place[:, :, :], hot[:, k, :, :], ALU.mult))
                one(dve.tensor_reduce(posf[:, k, :], picked[:, :, :], AX.X, ALU.add))
            one(dve.tensor_copy(pos[:, :, :], posf[:, :, :]))
            be = [P, ROUTED, EXPERTS]
            iota_b = misc[:, P + EXPERTS + ALL_TILES:].rearrange("p (j a) -> p j a", a=1).to_broadcast(be)
            one(dve.tensor_tensor(passed[:, :, :], blk_end[:, None, :].to_broadcast(be), iota_b, ALU.is_le))
            if SH:
                one(dve.memset(ownerf[:, 0:SH], 0.0))
            one(dve.tensor_reduce(ownerf[:, SH:BLOCKS], passed[:, :, :], AX.X, ALU.add))
            one(dve.tensor_scalar(ownerf[:, SH:BLOCKS], ownerf[:, SH:BLOCKS], float(EXPERTS - 1), float(shared), ALU.min, ALU.add))
            one(dve.tensor_copy(owner[:, :], ownerf[:, :]))
            dve.sem_inc(routed, 2)

            def gate_hidden(t):
                j, n = t.j, t.n
                dve.wait_ge(a_ready, j + 1)
                if n >= 2:
                    dve.wait_ge(hT_psum, j - 1)
                dve.tensor_tensor(h[:, n % 2, :], act_out[:, n % 2, :], bU[n % 2][1][:, :], ALU.mult).then_inc(h_ready, 1)

            def turned_hidden(t):
                j, n = t.j, t.n
                dve.wait_ge(hT_psum, j + 1)
                if n >= 2:
                    dve.wait_ge(y_psum, j - 1)
                dve.tensor_copy(hT[:, n % 2, 4:8, :], bH1[:, :].rearrange("p (c n) -> p c n", c=4)).then_inc(hT_ready2, 1)

            def result(t):
                j, n = t.j, t.n
                dve.wait_ge(y_psum, j + 1)
                if n >= 2:
                    dve.wait_ge(yb_out[t.side], 16 * t.pair)
                dve.tensor_copy(yb[:, n % 2, :], bY[:, 0:D]).then_inc(yb_ready, 1)

            def dve_block(t):
                j, n = t.j, t.n
                if gated:
                    gate_hidden(t)
                if n:
                    result(t.before())
                if not gated:
                    turned_hidden(t)
            for_blocks(dve, BLOCKS, dve_block)
            result(at(BLOCKS - 1))

            once = s.n
            dve.sem_inc(out_ready, 2)
            with dve.Fori(0, ALL_TILES // 2) as i:
                per = 2 * (TOPK - 1 + shared)
                s.base, s.n = once + i * per, 0
                for q in range(2):
                    n = 2 * i + q
                    dve.wait_ge(gathered[q], 16 * TOPK * (i + 1))
                    dve.wait_ge(res_in[q], 16 * (1 + shared) * (i + 1))
                    dve.wait_ge(stored[q], 16 * (i + 1))
                    acc = x_res[:, q, :]
                    if shared:
                        one(dve.scalar_tensor_tensor(out=acc, in0=y_in[:, q, TOPK, :], scalar=0.1, in1=acc, op0=ALU.mult, op1=ALU.add))
                    w = lambda k: weight[:, k, bass.ds(n, 1)]
                    one(dve.scalar_tensor_tensor(out=acc, in0=y_in[:, q, 0, :], scalar=w(0), in1=acc, op0=ALU.mult, op1=ALU.add))
                    dve.scalar_tensor_tensor(out=part[:, q, :], in0=y_in[:, q, 1, :], scalar=w(1), in1=acc, op0=ALU.mult, op1=ALU.add).then_inc(out_ready, 1)

        @block.tensor
        def _(pe):
            pe.wait_ge(consts_in, 16 * N_CONST)
            for t in range(ALL_TILES // 2 + 1):
                if t < ALL_TILES // 2:
                    pe.wait_ge(xn_ready, 2 * t + 2)
                    if t >= 2:
                        pe.wait_ge(gT_ready, t - 1)
                    for q in range(2):
                        for c in range(DC):
                            col = (q * DC + c) * P
                            i = pe.transpose(bU[t % 2][0][:, col:col + P], xn_all[:, 2 * t + q, c * P:(c + 1) * P], ident[:, :])
                    i.then_inc(gT_psum, 1)
                if t:
                    pe.wait_ge(gT_ready, t)
                    for q in range(2):
                        n = 2 * (t - 1) + q
                        if n >= 2:
                            pe.wait_ge(logit_read, n - 1)
                        for c in range(DC):
                            i = pe.matmul((bH0, bH1)[n % 2][:, 0:EXPERTS], gT[:, (t - 1) % 2, q * DC + c, :], w_gate[:, c, :], start=(c == 0), stop=(c == DC - 1))
                        i.then_inc(logit_psum, 1)
            pe.wait_ge(both_ready, 1)
            pe.wait_ge(ready, 2)
            flat = both16[:, :, :].rearrange("p t e -> p (t e)")
            pe.matmul(bU0[:, 0:ALL_TILES * EXPERTS], before[:, :], flat, start=True, stop=True)
            pe.matmul(bU1[:, 0:ALL_TILES * EXPERTS], ones[:, :], flat, start=True, stop=True).then_inc(rank_psum, 1)
            pe.wait_ge(w_in, 16 * 2 * LATE)
            pe.wait_ge(routed, 2)
            if not gated:
                pe.wait_ge(b_in, 16 * 3 * n_exp)

            def turn(t):
                j, n = t.j, t.n
                pe.wait_ge(xb_in[t.side], 16 * (t.pair + 1))
                if n:
                    pe.wait_ge(xT_ready, j)
                for c in range(DC):
                    i = pe.transpose(bX[:, c * P:(c + 1) * P], xb[:, n % 2, c * P:(c + 1) * P], ident[:, :])
                i.then_inc(xT_psum, 1)

            def up(t):
                j, n = t.j, t.n
                e = pe.value_load(owner[0:1, bass.ds(j, 1)], min_val=0, max_val=n_exp - 1)
                pe.wait_ge(xT_ready, j + 1)
                if n >= 2:
                    pe.wait_ge(h_ready if gated else a_ready, j - 1)
                for k in range(2):
                    for c in range(DC):
                        i = pe.matmul(bU[n % 2][k][:, :], xT[:, n % 2, c, :],
                                      w_up[:, bass.ds(e, 1), c, k * 512:(k + 1) * 512].rearrange("p a n -> p (a n)"), start=(c == 0), stop=(gated and c == DC - 1))
                    if not gated:
                        i = pe.matmul(bU[n % 2][k][:, :], ones[:, :], b_table[:, bass.ds(e, 1), k * 512:(k + 1) * 512].rearrange("p a n -> p (a n)"), start=False, stop=True)
                i.then_inc(u_psum, 1)

            def turn_hidden(t):
                j, n = t.j, t.n
                pe.wait_ge(h_ready if gated else a_ready, j + 1)
                if n:
                    pe.wait_ge(hT_ready, j)
                    if not gated:
                        pe.wait_ge(hT_ready2, j)
                for c in range(hc):
                    i = pe.transpose((bH0, bH1)[c // 4][:, (c % 4) * P:(c % 4 + 1) * P], h[:, n % 2, c * P:(c + 1) * P], ident[:, :])
                i.then_inc(hT_psum, 1)

            def down(t):
                j, n = t.j, t.n
                e = pe.value_load(owner[0:1, bass.ds(j, 1)], min_val=0, max_val=n_exp - 1)
                pe.wait_ge(hT_ready, j + 1)
                if not gated:
                    pe.wait_ge(hT_ready2, j + 1)
                if n:
                    pe.wait_ge(yb_ready, j)
                for c in range(hc):
                    i = pe.matmul(bY[:, 0:D], hT[:, n % 2, c, :], w_down[:, bass.ds(e, 1), c, :].rearrange("p a n -> p (a n)"), start=(c == 0), stop=(gated and c == hc - 1))
                if not gated:
                    i = pe.matmul(bY[:, 0:D], ones[:, :], b_table[:, bass.ds(e, 1), UP:].rearrange("p a n -> p (a n)"), start=False, stop=True)
                i.then_inc(y_psum, 1)

            def pe_block(t):
                j, n = t.j, t.n
                up(t)
                if n + 1 < BLOCKS:
                    turn(t.after())
                if n:
                    down(t.before())
                turn_hidden(t)

            turn(at(0))
            if LATE < n_exp:
                for_blocks(pe, SH, pe_block, last=False)
                pe.wait_ge(late_in, 16 * 2 * (n_exp - LATE))
                for_blocks(pe, BLOCKS, pe_block, first=SH)
            else:
                for_blocks(pe, BLOCKS, pe_block)
            down(at(BLOCKS - 1))


def pos_slot(pos, k, n):
    return pos[:, k, n:n + 1]


class Turn:

    def __init__(self, pair, side, n):
        self.pair, self.side, self.n = pair, side, n
        self.j = 2 * pair + side

    def before(self):
        return Turn(self.pair - 1 if self.side == 0 else self.pair, 1 - self.side, self.n - 1)

    def after(self):
        return Turn(self.pair + 1 if self.side == 1 else self.pair, 1 - self.side, self.n + 1)


def at(j):
    return Turn(j // 2, j % 2, j)


def for_blocks(engine, blocks, step, first=0, last=True):
    lo = first
    if first == 0:
        step(at(0))
        step(at(1))
        lo = 2
    hi = blocks - 2 if last else blocks
    with engine.Fori(lo // 2, hi // 2) as pair:
        for side in range(2):
            step(Turn(pair, side, 2 + side))
    if last:
        step(at(hi))
        step(at(hi + 1))


HEADS, DH = 16, 16
GH = 4
GROUPS = HEADS // GH
TERMS = 6
KEY_ROWS = TERMS * DH
Q_PART = (0, 0, 0, 1, 1, 2)
K_PART = (0, 1, 2, 0, 1, 0)
POOL_STEPS = (TILES * 6 + GROUPS * 6,) * 2
DVE_STEPS = (GROUPS * 14, GROUPS * 14 + TILES)


UNITS = 3 * TILES // 2 * GH
HALF = 4


def query_units():
    return [(h, i, c * 512, min((i + 1) * P, (c + 1) * 512)) for h in range(GH) for i in range(TILES) for c in range(i // HALF + 1)]


def key_units(j):
    return [(h, max(j * P, c * 512), (c + 1) * 512) for h in range(GH) for c in range(j // HALF, 2)]


SLOTS = 8
QUERIES_AT = (0, 6, 8, 10, 12, 12, 0, 0)
WEIGH_AT = {2: (4, 7), 1: (6,)}
ROWS_AT = (3, 3, 0, 0)
SPLIT_AT = ((1, 2, 2, 3, 4),) * 2 + ((3, 3, 4, 4, 5), (1, 2, 2, 3, 4))


def key_slot(j, slot):
    n = len(key_units(j))
    return (slot * n // SLOTS,) if slot * n % SLOTS == 0 else ()


def query_slot(j, slot):
    before, n = sum(QUERIES_AT[:j]), QUERIES_AT[j]
    return range(before + n * slot // SLOTS, before + n * (slot + 1) // SLOTS)


def beside(extras, slot):
    n = len(extras)
    return extras[n * slot // SLOTS:n * (slot + 1) // SLOTS]


def units_before(j):
    return sum(len(key_units(k)) for k in range(j))


class Plan:

    def __init__(self, first, last, start=0, later=0):
        self.start, self.later, self.uses, self.extras = start, later, [], {}
        for hg in range(GROUPS):
            follows = not (last and hg == GROUPS - 1)
            steps = [[] for _ in range(TILES)]
            if follows:
                for h in range(GH):
                    steps[h] += [("terms", hg, h, side) for side in range(2)]
            if not (first and hg == 0):
                steps[1] += [("out", hg, c) for c in range(2)]
            if not last:
                tiles = (range(0, 3), range(3, 6), range(6, 8), ())[hg]
                for k, t in enumerate(tiles):
                    at_step = ROWS_AT[hg] + k
                    steps[at_step] += [("rows", t)]
                    steps[at_step + 1] = [("keys", t), ("values", t)] + steps[at_step + 1]
            if hg == 0 and not first:
                for t in range(TILES):
                    steps[2 + t // 2] += [("acts", t)]
                for t in range(TILES):
                    at_step = 3 + t // 2
                    steps[at_step].insert(t % 2, ("sum", t))
            self.extras[hg] = steps
            for step in steps:
                self.uses += step
            if follows:
                self.uses.append(("tops", hg))
        self.place = {key: k for k, key in enumerate(self.uses)}

    def spot(self, key):
        k = self.start + self.place[key]
        return k % 2, self.later + k // 2


class Opening(Plan):

    def __init__(self):
        self.start, self.later = 0, 0
        self.uses = [(kind, t) for t in range(TILES) for kind in ("rows", "keys", "values")]
        self.uses += [("terms", -1, h, side) for h in range(GH) for side in range(2)] + [("tops", -1)]
        self.place = {key: k for k, key in enumerate(self.uses)}


def causal_attention(nc, io, x_in, x_out):
    with ExitStack() as stack:
        m = Memory(nc, stack, "ca")
        sb, sem = m.sb, m.sem
        x = sb("x", [P, ALL_TILES, D])
        w_kqv = sb("w_kqv", [P, DC, 3 * D])
        w_o = sb("w_o", [P, DC, D])
        ident = sb("ident", [P, P])
        ident16 = sb("ident16", [P, P], BF16)
        mask = sb("mask", [P, P])
        mask16 = sb("mask16", [P, P], BF16)
        rope = sb("rope", [P, 2, TILES, DH // 2])
        stats = sb("stats", [P, ALL_TILES, 6])
        mv = sb("mv", [P, ALL_TILES, 2])
        root = sb("root", [P, ALL_TILES])
        rstd = sb("rstd", [P, ALL_TILES])
        epst = sb("epst", [P, 1])
        xn = sb("xn", [P, 2, D])
        xT = sb("xT", [P, 2, DC, P])
        raw = sb("raw", [P, 2, 2 * D])
        scratch = sb("scratch", [P, 4 * D])
        turn = scratch[:, :].rearrange("p (k d) -> p k d", k=4)
        left = scratch[:, :].rearrange("p (s t n) -> p s t n", t=TILES, s=2)
        kq = sb("kq", [P, 2, TILES, 2, D])
        v_all = sb("v_all", [P, 2, TILES, D])
        vg = sb("vg", [P, TILES, GH, 2 * DH])
        parts = sb("parts", [P, 3, 2, TILES, GH * DH], BF16)
        terms = sb("terms", [P, 2, TILES, GH, KEY_ROWS], BF16)
        kT = sb("kT", [P, 2, GH, SEQ], BF16)
        qT = sb("qT", [P, 2, GH, SEQ], BF16)
        top = sb("top", [P, 2, GH, TILES])
        topl = sb("topl", [P, 2, TILES, GH])
        top3 = sb("top3", [P, TILES, GH, 32], BF16)
        probs = sb("probs", [P, 2, GH, SEQ])
        oT = sb("oT", [P, SEQ])
        rden = sb("rden", [P, TILES, GH])
        acts = sb("acts", [P, TILES, D])
        aT = sb("aT", [P, 2, DC, P])

        O = stack.enter_context(nc.psum_tensor("ca_wide", [P, 1024], F32))
        banks = m.banks(6)
        key_banks, query_banks, narrow = banks[0:2], banks[2:4], banks[4:6]

        consts_in = sem("consts_in")
        x_loaded = [sem(f"x_loaded{b}") for b in range(BATCH)]
        ready, zeroed, dve_step, pool_step = sem("ready"), sem("zeroed"), sem("dve_step"), sem("pool_step")
        var_ready, root_ready, xn_ready = sem("var_ready"), sem("root_ready"), sem("xn_ready")
        full, read = [sem("full0"), sem("full1")], [sem("read0"), sem("read1")]
        roped, parts_ready, terms_ready, vg_ready = sem("roped"), sem("parts_ready"), sem("terms_ready"), sem("vg_ready")
        s1_psum, top_ready = sem("s1_psum"), sem("top_ready")
        s2_psum, exp_ready, cut_ready, pv_done = sem("s2_psum"), sem("exp_ready"), sem("cut_ready"), sem("pv_done")
        oT_ready, rden_ready = sem("oT_ready"), sem("rden_ready")
        x_done, stored, values_in = sem("x_done"), sem("stored"), sem("values_in")
        closing, closing_read, closing_turned, closing_aT, closing_y = [sem(f"closing{k}") for k in range(5)]
        waited = sem("waited")
        N_CONST = 5
        SCALE = DH ** -0.5

        opening = Opening()
        first_plan = Plan(True, False, len(opening.uses))
        middle = len(opening.uses) + len(first_plan.uses)
        MIDDLE_USES = len(Plan(False, False).uses)
        assert MIDDLE_USES % 2 == 0

        def last_plan_uses():
            n = middle + (BATCH - 2) * MIDDLE_USES + len(Plan(False, True).uses)
            return (n + 1) // 2, n // 2

        def wait(engine, semaphore, value):
            if isinstance(value, int):
                if value > 0:
                    engine.wait_ge(semaphore, value)
            else:
                engine.wait_ge(semaphore, value)
                if engine is nc.gpsimd:
                    engine.sem_inc(waited, 1)

        def turns(engine, turn_of, steps_of, steps=None):
            start = steps.n if steps else 0

            def based(b, base):
                if steps:
                    steps.base, steps.n = base, 0
                return b

            turn_of(based(0, start), 0, 1, first_plan)
            start += steps_of[0] if steps else 0
            assert not steps or steps.n == steps_of[0], (steps.n, steps_of)
            engine.sem_inc(waited, 1)
            with engine.Fori(1, BATCH - 1) as b:
                turn_of(based(b, start + (b - 1) * (steps_of[1] if steps else 0)), 2 - b, b - 1, Plan(False, False, middle, (b - 1) * (MIDDLE_USES // 2)))
                assert not steps or steps.n == steps_of[1], (steps.n, steps_of)
                engine.sem_inc(waited, 1)
            start += (BATCH - 2) * (steps_of[1] if steps else 0)
            turn_of(based(BATCH - 1, start), 1, 0, Plan(False, True, middle + (BATCH - 2) * MIDDLE_USES))

        def filled(engine, plan, key):
            bank, before = plan.spot(key)
            wait(engine, full[bank], before + 1)
            return narrow[bank], read[bank]

        block = stack.enter_context(nc.Block())

        @block.sync
        def _(sp):
            for b in range(BATCH):
                sp.dma_start(x[:, b * TILES:(b + 1) * TILES, :], x_in[b].rearrange("(t p) d -> p t d", p=P)).then_inc(x_loaded[b], 16)
            with sp.Fori(0, BATCH) as b:
                sp.wait_ge(x_done, (b + 1) * TILES)
                sp.dma_start(x_out[b].rearrange("(t p) d -> p t d", p=P), x[:, bass.ds(b * TILES, TILES), :]).then_inc(stored, 16)
            sp.wait_ge(stored, 16 * BATCH)

        @block.gpsimd
        def _(pool):
            s = Steps(pool, pool_step)

            def one(instruction):
                s.do(instruction)
                wait(pool, pool_step, s.base + s.n)

            one(pool.memset(vg[:, :, :, :], 0.0))
            one(pool.memset(vg[:, :, :, DH:DH + 1], 1.0))
            pool.memset(top3[:, :, :, :], 0.0).then_inc(zeroed, 1)
            pool.wait_ge(consts_in, 16 * N_CONST)

            def turn_pairs(b, t, where, plan):
                bank, before = plan.spot(("keys", t))
                wait(pool, read[bank], before + 1)
                half = 2 * HEADS
                pairs = raw[:, t % 2, :].rearrange("p (h f a) -> p h f a", f=DH // 2, a=2)
                even, odd = pairs[:, :, :, 0], pairs[:, :, :, 1]
                cos = rope[:, 0, t, None, :].to_broadcast([P, half, DH // 2])
                sin = rope[:, 1, t, None, :].to_broadcast([P, half, DH // 2])
                tmp = [turn[:, k, :].rearrange("p (h f) -> p h f", f=DH // 2) for k in range(4)]
                for k, (a, w) in enumerate(((even, cos), (odd, sin), (even, sin), (odd, cos))):
                    s.do(pool.tensor_tensor(tmp[k], a, w, ALU.mult))
                wait(pool, pool_step, s.base + s.n)
                out = kq[:, where, t, :, :].rearrange("p s (h a f) -> p (s h) a f", a=2, f=DH // 2) if isinstance(where, int) else \
                    kq[:, bass.ds(where, 1), t, :, :].rearrange("p w s (h a f) -> p (w s h) a f", a=2, f=DH // 2)
                s.do(pool.tensor_tensor(out[:, :, 0, :], tmp[0], tmp[1], ALU.subtract))
                one(pool.tensor_tensor(out[:, :, 1, :], tmp[2], tmp[3], ALU.add))
                pool.sem_inc(roped, 1)

            def split(hg, where, before, k):
                lo, hi = hg * GH * DH, (hg + 1) * GH * DH
                src = kq[:, where, :, :, lo:hi].rearrange("p t s n -> p s t n") if isinstance(where, int) else \
                    kq[:, bass.ds(where, 1), :, :, lo:hi].rearrange("p w t s n -> p s (w t) n")
                if k == 0:
                    wait(pool, terms_ready, before)
                rest = src if k < 2 else left[:, :, :, :]
                if k % 2 == 0:
                    one(pool.tensor_copy(parts[:, k // 2, :, :, :], rest))
                else:
                    one(pool.tensor_tensor(left[:, :, :, :], rest, parts[:, k // 2, :, :, :], ALU.subtract))
                if k == 4:
                    pool.sem_inc(parts_ready, 1)

            for t in range(TILES):
                turn_pairs(0, t, 0, opening)
            for hg in range(2):
                for k in range(5):
                    split(hg, 0, hg, k)

            def copy_values(b, hg, cur):
                wait(pool, pv_done, (b * GROUPS + hg) * TILES)
                if hg == 0:
                    wait(pool, values_in, b + 1)
                lo, hi = hg * GH * DH, (hg + 1) * GH * DH
                src = v_all[:, cur, :, lo:hi] if isinstance(cur, int) else v_all[:, bass.ds(cur, 1), :, lo:hi].rearrange("p w t n -> p (w t) n")
                one(pool.tensor_copy(vg[:, :, :, 0:DH], src.rearrange("p t (h d) -> p t h d", d=DH)))
                pool.sem_inc(vg_ready, 1)

            def pool_turn(b, cur, nxt, plan):
                last = isinstance(b, int) and b == BATCH - 1
                for hg in range(GROUPS):
                    g = b * GROUPS + hg
                    for j in range(TILES):
                        u = g * UNITS + units_before(j)
                        for k, (h, a, e) in enumerate(key_units(j)):
                            if a == j * P:
                                wait(pool, exp_ready, u + k + 1)
                                on = probs[:, j % 2, h, a:a + P]
                                pool.affine_select(out=on, in_=on, compare_op=ALU.is_ge, fill=0.0, base=0,
                                                   pattern=[[1, P]], channel_multiplier=-1).then_inc(cut_ready, 1)
                        if j == 0:
                            copy_values(b, hg, cur)
                        if not (last and hg >= GROUPS - 2):
                            for k in range(5):
                                if SPLIT_AT[hg][k] == j:
                                    split((hg + 2) % GROUPS, cur if hg < 2 else nxt, g + 2, k)
                        for key in plan.extras[hg][j]:
                            if key[0] == "keys":
                                turn_pairs(b, key[1], nxt, plan)

            turns(pool, pool_turn, POOL_STEPS, s)

        @block.scalar
        def _(act):
            for dst, src in ((w_kqv[:, :, :], io["ca_w"]), (w_o[:, :, :], io["ca_wo"]), (ident[:, :], io["ident"]),
                             (mask[:, :], io["ca_mask"]), (rope[:, :, :, :], io["ca_rope"])):
                act.dma_start(dst, src).then_inc(consts_in, 16)
            act.wait_ge(var_ready, 1)
            act.activation(root[:, :], mv[:, :, 1], ACT.Sqrt, bias=epst[:, 0:1]).then_inc(root_ready, 1)

            def copy(dst, src, signal):
                return act.activation(dst, src, ACT.Identity).then_inc(signal, 1)

            def extra(plan, key, b, where, par):
                if key[0] == "rows":
                    bank, sig = filled(act, plan, key)
                    copy(xT[:, key[1] % 2, :, :], bank[:, 0:D].rearrange("p (c n) -> p c n", c=DC), sig)
                elif key[0] == "keys":
                    t = key[1]
                    wait(act, roped, (b + 1) * TILES + t - 1)
                    bank, sig = filled(act, plan, key)
                    copy(raw[:, t % 2, :], bank[:, :], sig)
                elif key[0] == "values":
                    bank, sig = filled(act, plan, key)
                    t = key[1]
                    dst = v_all[:, where, t, :] if isinstance(where, int) else v_all[:, bass.ds(where, 1), t, :].rearrange("p w n -> p (w n)")
                    if t == 0:
                        wait(act, vg_ready, b * GROUPS)
                    copy(dst, bank[:, 0:D], sig)
                    if t == TILES - 1:
                        wait(act, sig, plan.spot(key)[1] + 1)
                        act.sem_inc(values_in, 1)
                elif key[0] == "terms" and key[2] > 0:
                    _, _, h, side = key
                    bank, sig = filled(act, plan, key)
                    copy((kT, qT)[side][0:KEY_ROWS, par, h, :], bank[0:KEY_ROWS, :].bitcast(BF16), sig)
                elif key[0] == "acts":
                    bank, sig = filled(act, plan, key)
                    copy(aT[:, key[1] % 2, :, :], bank[:, 0:D].rearrange("p (c n) -> p c n", c=DC), sig)

            for key in opening.uses:
                extra(opening, key, -1, 0, 0)

            def act_turn(b, cur, nxt, plan):
                for hg in range(GROUPS):
                    g = b * GROUPS + hg
                    for j in range(TILES):
                        wait(act, pv_done, g * TILES + j - 1)
                        for slot in range(SLOTS):
                            for k in key_slot(j, slot):
                                h, a, e = key_units(j)[k]
                                u = units_before(j) + k
                                wait(act, s2_psum, g * UNITS + u + 1)
                                act.activation(probs[:, j % 2, h, a:e], key_banks[u % 2][:, a % 512:(e - 1) % 512 + 1], ACT.Exp, scale=SCALE).then_inc(exp_ready, 1)
                            if j == 0 and slot in (5, 7) and ("out", hg, 0) in plan.place:
                                copy_sums(g - 1, slot // 7)
                            for key in beside(plan.extras[hg][j], slot):
                                extra(plan, key, b, nxt, (hg + 1) % 2)

            def copy_sums(g, c):
                wait(act, pv_done, (g + 1) * TILES)
                copy(oT[:, c * 512:(c + 1) * 512], O[:, c * 512:(c + 1) * 512], oT_ready)

            turns(act, act_turn, None)
            for c in range(2):
                copy_sums(BATCH * GROUPS - 1, c)
            for t in range(TILES):
                act.wait_ge(closing_turned, t + 1)
                if t >= 2:
                    act.wait_ge(closing_y, t - 1)
                copy(aT[:, t % 2, :, :], narrow[t % 2][:, 0:D].rearrange("p (c n) -> p c n", c=DC), closing_aT)

        @block.vector
        def _(dve):
            s = Steps(dve, dve_step)
            one = lambda i: (s.do(i), s.done())
            one(dve.memset(epst[:, :], EPS))
            one(dve.memset(kT[KEY_ROWS:KEY_ROWS + 3, :, :, :], 1.0))
            one(dve.memset(top[:, :, :, :], -3e38))
            for b in range(BATCH):
                dve.wait_ge(x_loaded[b], 16)
                for n in range(b * TILES, (b + 1) * TILES):
                    s.do(dve.bn_stats(stats[:, n, :], x[:, n, :]))
            s.done()
            for n in range(ALL_TILES):
                s.do(dve.bn_aggr(mv[:, n, :], stats[:, n, :]))
            s.done()
            dve.sem_inc(var_ready, 1)
            dve.wait_ge(consts_in, 16 * N_CONST)
            s.do(dve.tensor_copy(ident16[:, :], ident[:, :]))
            one(dve.tensor_copy(mask16[:, :], mask[:, :]))
            dve.wait_ge(root_ready, 1)
            one(dve.reciprocal(rstd[:, :], root[:, :]))
            dve.wait_ge(zeroed, 1)
            dve.sem_inc(ready, 1)

            def normalise(plan, b, t):
                if t >= 2:
                    filled(dve, plan, ("rows", t - 2))
                n = b * TILES + t
                if isinstance(n, int):
                    src, mean, r = x[:, n, :], mv[:, n, 0:1], rstd[:, n:n + 1]
                else:
                    src, mean, r = x[:, bass.ds(n, 1), :].rearrange("p a d -> p (a d)"), mv[:, bass.ds(n, 1), 0], rstd[:, bass.ds(n, 1)]
                dve.tensor_scalar(xn[:, t % 2, :], src, mean, r, ALU.subtract, ALU.mult).then_inc(xn_ready, 1)

            def place_terms(plan, key, count, side):
                wait(dve, parts_ready, count)
                if key:
                    filled(dve, plan, key)
                to = lambda lo, hi, step: terms[:, side, :, :, :].rearrange("p t h n -> p (t h) n").rearrange("p m (r d) -> p m r d", d=DH)[:, :, lo:hi:step, :]
                of = lambda k, n: parts[:, k, side, :, :].rearrange("p t n -> p (t n)").rearrange("p (m a d) -> p m a d", a=1, d=DH).to_broadcast([P, TILES * GH, n, DH])
                where = (((0, 0, 4, 3), (0, 5, 6, 1), (1, 1, 5, 3), (2, 2, 3, 1)), ((0, 0, 3, 1), (1, 3, 5, 1), (2, 5, 6, 1)))
                for k, lo, hi, step in where[side]:
                    s.do(dve.tensor_copy(to(lo, hi, step), of(k, len(range(lo, hi, step)))))
                if side == 0:
                    s.done()
                    dve.sem_inc(terms_ready, 1)

            def maxima(g, units):
                for u in units:
                    h, i, a, e = query_units()[u]
                    wait(dve, s1_psum, g * UNITS + u + 1)
                    dve.tensor_reduce(top[:, a // 512, h, i:i + 1], query_banks[u % 2][:, 0:e - a], AX.X, ALU.max).then_inc(top_ready, 1)

            def part_tops(g):
                wait(dve, top_ready, g * (UNITS + 1) + UNITS)
                by_tile = top[:, :, :, :].rearrange("p c h t -> p c t h")
                one(dve.tensor_tensor(topl[:, 1, :, :], by_tile[:, 0, :, :], by_tile[:, 1, :, :], ALU.max))
                one(dve.tensor_scalar(topl[:, 0, :, :], topl[:, 1, :, :], -1.0, None, ALU.mult))
                for k in range(3):
                    one(dve.tensor_copy(top3[:, :, :, k], topl[:, k % 2, :, :]))
                    if k < 2:
                        one(dve.tensor_tensor(topl[:, (k + 1) % 2, :, :], topl[:, k % 2, :, :], top3[:, :, :, k], ALU.subtract))
                dve.sem_inc(top_ready, 1)

            def hand_tops(plan, key, par):
                bank, sig = filled(dve, plan, key)
                for h in range(GH):
                    i = dve.tensor_copy(qT[KEY_ROWS:KEY_ROWS + 3, par, h, :], bank[32 * h:32 * h + 3, :].bitcast(BF16))
                i.then_inc(sig, 1)

            def average(bank, sig, hg, c, count):
                half = slice(c * HALF, (c + 1) * HALF)
                o = bank[:, :].rearrange("p (t h d) -> p t h d", h=GH, d=2 * DH)
                dve.reciprocal(rden[:, half, :], o[:, :, :, DH]).then_inc(rden_ready, 1)
                wait(dve, rden_ready, count)
                out = acts[:, half, hg * GH * DH:(hg + 1) * GH * DH].rearrange("p t (h d) -> p t h d", d=DH)
                dve.tensor_tensor(out, o[:, :, :, 0:DH], rden[:, half, :].rearrange("p t (h a) -> p t h a", a=1).to_broadcast([P, HALF, GH, DH]),
                                  ALU.mult).then_inc(sig, 1)

            def copy_terms(plan, key, par):
                bank, sig = filled(dve, plan, key)
                dve.tensor_copy((kT, qT)[key[3]][0:KEY_ROWS, par, 0, :], bank[0:KEY_ROWS, :].bitcast(BF16)).then_inc(sig, 1)

            for t in range(TILES):
                normalise(opening, 0, t)
            for side in (1, 0):
                place_terms(opening, None, 1, side)
            for side in range(2):
                copy_terms(opening, ("terms", -1, 0, side), 0)
            maxima(0, range(UNITS))
            part_tops(0)
            hand_tops(opening, ("tops", -1), 0)
            for side in (1, 0):
                place_terms(opening, ("terms", -1, GH - 1, 1), 2, side)

            def dve_turn(b, cur, nxt, plan):
                last = isinstance(b, int) and b == BATCH - 1
                for hg in range(GROUPS):
                    g = b * GROUPS + hg
                    tiles = [key[1] for j in range(TILES) for key in plan.extras[hg][j] if key[0] == "rows"]
                    for t in tiles[:2]:
                        normalise(plan, b + 1, t)
                    follows, placed = ("tops", hg) in plan.place, not (last and hg >= GROUPS - 2)
                    for j in range(TILES):
                        for slot in range(SLOTS):
                            if follows:
                                maxima(g + 1, query_slot(j, slot))
                            for key in beside(plan.extras[hg][j], slot):
                                if key[0] == "out":
                                    average(*filled(dve, plan, key), (hg - 1) % GROUPS, key[2], 2 * (g - 1) + key[2] + 1)
                                elif key[0] == "rows" and len(tiles) > 2 and key[1] == tiles[0]:
                                    normalise(plan, b + 1, tiles[2])
                                elif key[0] == "terms" and key[2] == 0:
                                    copy_terms(plan, key, (hg + 1) % 2)
                                elif key[0] == "sum":
                                    bank, sig = filled(dve, plan, key)
                                    n = (b - 1) * TILES + key[1]
                                    xs = x[:, n, :] if isinstance(n, int) else x[:, bass.ds(n, 1), :].rearrange("p a d -> p (a d)")
                                    one(dve.tensor_tensor(xs, xs, bank[:, 0:D], ALU.add))
                                    dve.sem_inc(sig, 1)
                                    dve.sem_inc(x_done, 1)
                        if j == TILES - 3 and follows:
                            part_tops(g + 1)
                            if placed:
                                place_terms(plan, ("terms", hg, GH - 1, 1), g + 3, 1)
                        if j == TILES - 2 and follows:
                            hand_tops(plan, ("tops", hg), (hg + 1) % 2)
                            if placed:
                                place_terms(plan, ("terms", hg, GH - 1, 1), g + 3, 0)

            turns(dve, dve_turn, DVE_STEPS, s)
            for c in range(2):
                dve.wait_ge(closing, c + 1)
                average(narrow[c], closing_read, GROUPS - 1, c, 2 * (BATCH * GROUPS - 1) + c + 1)
            for t in range(TILES):
                dve.wait_ge(closing_y, t + 1)
                xs = x[:, (BATCH - 1) * TILES + t, :]
                dve.tensor_tensor(xs, xs, query_banks[t % 2][:, 0:D], ALU.add).then_inc(x_done, 1)

        @block.tensor
        def _(pe):
            pe.wait_ge(ready, 1)

            def fill(plan, key):
                bank, before = plan.spot(key)
                wait(pe, read[bank], before)
                return narrow[bank], full[bank]

            def was_read(plan, key):
                bank, before = plan.spot(key)
                wait(pe, read[bank], before + 1)

            def turn_four(dst, src, n, signal):
                for c in range(n):
                    i = pe.transpose(dst[:, c * P:(c + 1) * P], src(c), ident[:, :])
                i.then_inc(signal, 1)

            def extra(plan, key, b, par):
                if key[0] == "rows":
                    t = key[1]
                    wait(pe, xn_ready, (b + 1) * TILES + t + 1)
                    bank, sig = fill(plan, key)
                    turn_four(bank, lambda c: xn[:, t % 2, c * P:(c + 1) * P], DC, sig)
                elif key[0] in ("keys", "values"):
                    t = key[1]
                    was_read(plan, ("rows", t))
                    bank, sig = fill(plan, key)
                    lo, hi = (0, 2 * D) if key[0] == "keys" else (2 * D, 3 * D)
                    for c in range(DC):
                        i = pe.matmul(bank[:, 0:hi - lo], xT[:, t % 2, c, :], w_kqv[:, c, lo:hi], start=(c == 0), stop=(c == DC - 1))
                    i.then_inc(sig, 1)
                elif key[0] == "terms":
                    _, hg, h, side = key
                    if h == 0 and side == 0:
                        wait(pe, terms_ready, b * GROUPS + hg + 2)
                    bank, sig = fill(plan, key)
                    for t in range(TILES):
                        i = pe.transpose(bank[0:KEY_ROWS, :].bitcast(BF16)[:, t * P:(t + 1) * P], terms[:, side, t, h, :], ident16[:, :])
                    i.then_inc(sig, 1)
                elif key[0] == "out":
                    c = key[2]
                    wait(pe, oT_ready, 2 * (b * GROUPS + key[1] - 1) + c + 1)
                    bank, sig = fill(plan, key)
                    turn_four(bank, lambda k: oT[:, (4 * c + k) * P:(4 * c + k + 1) * P], 4, sig)
                elif key[0] == "acts":
                    t = key[1]
                    if t == 0:
                        for c in range(2):
                            was_read(plan, ("out", 0, c))
                    bank, sig = fill(plan, key)
                    turn_four(bank, lambda c: acts[:, t, c * P:(c + 1) * P], DC, sig)
                elif key[0] == "sum":
                    t = key[1]
                    was_read(plan, ("acts", t))
                    bank, sig = fill(plan, key)
                    for c in range(DC):
                        i = pe.matmul(bank[:, 0:D], aT[:, t % 2, c, :], w_o[:, c, :], start=(c == 0), stop=(c == DC - 1))
                    i.then_inc(sig, 1)

            def query_score(g, u, par, plan, hg):
                h, i, a, e = query_units()[u]
                if i == 0:
                    for side in range(2):
                        was_read(plan, ("terms", hg, h, side))
                wait(pe, top_ready, g * (UNITS + 1) + u - 1)
                on_diagonal = e == (i + 1) * P
                out = query_banks[u % 2]
                last = pe.matmul(out[:, 0:e - a], qT[0:KEY_ROWS, par, h, i * P:(i + 1) * P], kT[0:KEY_ROWS, par, h, a:e], start=True, stop=not on_diagonal)
                if on_diagonal:
                    last = pe.matmul(out[:, e - a - P:e - a], ident16[:, :], mask16[:, :], start=False, stop=True)
                last.then_inc(s1_psum, 1)

            def turn_tops(plan, key, g):
                wait(pe, top_ready, (g + 1) * (UNITS + 1))
                bank, sig = fill(plan, key)
                for t in range(TILES):
                    i = pe.transpose(bank[:, :].bitcast(BF16)[:, t * P:(t + 1) * P], top3[:, t, :, :].rearrange("p h k -> p (h k)"), ident16[:, :])
                i.then_inc(sig, 1)

            def key_score(g, j, k, par):
                h, a, e = key_units(j)[k]
                u = units_before(j) + k
                wait(pe, exp_ready, g * UNITS + u - 1)
                pe.matmul(key_banks[u % 2][:, a % 512:(e - 1) % 512 + 1], kT[0:KEY_ROWS + 3, par, h, j * P:(j + 1) * P],
                          qT[0:KEY_ROWS + 3, par, h, a:e], start=True, stop=True).then_inc(s2_psum, 1)

            def weigh(g, j, n):
                c = j // HALF + n
                if n == 0:
                    wait(pe, cut_ready, (g * TILES + j + 1) * GH)
                    wait(pe, exp_ready, g * UNITS + units_before(j + 1))
                    if j == 0:
                        wait(pe, vg_ready, g + 1)
                        wait(pe, oT_ready, 2 * g)
                lo, hi = max(j * P, c * 512), (c + 1) * 512
                for h in range(GH):
                    i = pe.matmul(O[32 * h:32 * h + 32, lo:hi], vg[:, j, h, :], probs[:, j % 2, h, lo:hi],
                                  start=(j == 0), stop=(hi == (j + 1) * P), tile_position=(0, 32 * h))
                if c == 1:
                    i.then_inc(pv_done, 1)

            for key in opening.uses[:3 * TILES]:
                extra(opening, key, -1, 0)
            for key in opening.uses[3 * TILES:-1]:
                extra(opening, key, 0, 0)
            for u in range(UNITS):
                query_score(0, u, 0, opening, -1)
            turn_tops(opening, ("tops", -1), 0)

            def pe_turn(b, cur, nxt, plan):
                for hg in range(GROUPS):
                    g = b * GROUPS + hg
                    par = hg % 2
                    follows = ("tops", hg) in plan.place
                    if hg:
                        was_read(plan, ("tops", hg - 1))
                    elif isinstance(b, int) and b == 0:
                        was_read(opening, ("tops", -1))
                    else:
                        tops_of_last(b)
                    for j in range(TILES):
                        for slot in range(SLOTS):
                            for k in key_slot(j, slot):
                                key_score(g, j, k, par)
                            if follows:
                                for u in query_slot(j, slot):
                                    query_score(g + 1, u, 1 - par, plan, hg)
                            for key in beside(plan.extras[hg][j], slot):
                                extra(plan, key, b, 1 - par)
                            if j == 0 and slot == 3 and ("out", hg, 0) in plan.place:
                                weigh(g - 1, TILES - 1, 0)
                            if j and slot in WEIGH_AT[2 - (j - 1) // HALF]:
                                weigh(g, j - 1, WEIGH_AT[2 - (j - 1) // HALF].index(slot))
                            if j == TILES - 2 and slot == 7 and follows:
                                turn_tops(plan, ("tops", hg), g + 1)

            def tops_of_last(b):
                k = middle + (MIDDLE_USES * (b - 1)) - 1 if isinstance(b, int) else middle - 1
                bank, before = k % 2, k // 2 + (0 if isinstance(b, int) else (b - 1) * (MIDDLE_USES // 2))
                wait(pe, read[bank], before + 1)

            turns(pe, pe_turn, None)
            g = BATCH * GROUPS - 1
            weigh(g, TILES - 1, 0)
            ends = last_plan_uses()
            for bank in range(2):
                pe.wait_ge(read[bank], ends[bank])
            for c in range(2):
                pe.wait_ge(oT_ready, 2 * g + c + 1)
                turn_four(narrow[c], lambda k: oT[:, (4 * c + k) * P:(4 * c + k + 1) * P], 4, closing)
            pe.wait_ge(closing_read, 2)
            for t in range(TILES + 1):
                if t < TILES:
                    if t >= 2:
                        pe.wait_ge(closing_aT, t - 1)
                    turn_four(narrow[t % 2], lambda c: acts[:, t, c * P:(c + 1) * P], DC, closing_turned)
                if t:
                    pe.wait_ge(closing_aT, t)
                    if t >= 3:
                        pe.wait_ge(x_done, (BATCH - 1) * TILES + t - 2)
                    for c in range(DC):
                        i = pe.matmul(query_banks[(t - 1) % 2][:, 0:D], aT[:, (t - 1) % 2, c, :], w_o[:, c, :], start=(c == 0), stop=(c == DC - 1))
                    i.then_inc(closing_y, 1)


def chunks(a):
    return a.reshape(-1, P, a.shape[-1]).transpose(1, 0, 2)


def on_three(row):
    out = np.zeros((P, row.size), np.float32)
    for p in (0, 32, 64):
        out[p] = row.reshape(-1)
    return out


def rope_tables():
    half = 32
    pos = np.arange(SEQ, dtype=np.float32)
    freq = np.float32(10000.0) ** (-np.arange(half, dtype=np.float32) / np.float32(half))
    angle = pos[:, None] * freq[None, :]
    sin, cos = np.sin(angle), np.cos(angle)
    ga = np.stack([np.concatenate([cos, cos], 1), np.concatenate([-sin, sin], 1)])
    ga = ga.reshape(2, TILES, P, 2 * half).transpose(2, 0, 1, 3)
    d = 16
    freq = np.float32(1.0) / np.float32(10000.0) ** (np.arange(0, d, 2, dtype=np.float32) / np.float32(d))
    angle = pos[:, None] * freq[None, :]
    ca = np.stack([np.cos(angle), np.sin(angle)])
    ca = ca.reshape(2, TILES, P, d // 2).transpose(2, 0, 1, 3)
    return ga.astype(np.float32), ca.astype(np.float32)


def lay(i):
    ga_rope, ca_rope = rope_tables()
    order = [1, 0, 2, 3]
    heads = np.stack([i["L0_attn_gamma"][order], i["L0_attn_beta"][order]])
    tok = np.arange(P)
    dist = np.minimum(np.abs(tok[:, None] - tok[None, :]), 32)
    same = tok[:, None] // 64 == tok[None, :] // 64
    out = {
        "ident": np.eye(P, dtype=np.float32),
        "ga_w": chunks(np.concatenate([i["L0_attn_Wv"], i["L0_attn_Wg"], i["L0_attn_Wqk"]], 0).T),
        "ga_wo": chunks(i["L0_attn_Wo"].T),
        "ga_rope": ga_rope,
        "ga_heads": np.broadcast_to(heads, (P, 2, 4, 64)),
        "ga_bias": np.where(same, i["L0_attn_pos_emb"][dist], np.float32(-1e30)),
        "ga_ln1": np.stack([i["L0_attn_ln1_w"].reshape(2, P).T, i["L0_attn_ln1_b"].reshape(2, P).T], 1),
        "ga_ln2": np.broadcast_to(np.stack([i["L0_attn_ln2_w"], i["L0_attn_ln2_b"]]), (P, 2, 256)),
        "ga_brow": on_three(np.concatenate([i["L0_attn_bv"], i["L0_attn_bg"], i["L0_attn_bqk"], i["L0_attn_bo"]])),
    }
    out.update(lay_rest(i, ca_rope))
    return {k: np.ascontiguousarray(v) for k, v in out.items()}


def lay_rest(i, ca_rope):
    tok = np.arange(P)
    misc = np.concatenate([tok[:, None] < tok[None, :]] + [np.broadcast_to(r, (P, r.size)) for r in
                          (np.arange(EXPERTS), P * np.arange(ALL_TILES), np.arange(ROUTED))], 1).astype(np.float32)
    up0 = np.concatenate([i["L0_ffn_w1"], i["L0_ffn_w3"]], 2)
    up1 = np.concatenate([i["L1_ffn_sWu"][None], i["L1_ffn_Wu"]], 0).transpose(0, 2, 1)
    down1 = np.concatenate([i["L1_ffn_sWd"][None], i["L1_ffn_Wd"]], 0).transpose(0, 2, 1)
    each = lambda w: np.stack([chunks(e) for e in w])
    kqv = i["L1_attn_W_KQV"].T
    return {
        "ca_w": chunks(kqv), "ca_wo": chunks(i["L1_attn_W_O"].T), "ca_rope": ca_rope,
        "ca_mask": np.where(tok[None, :] > tok[:, None], np.float32(-1e30), np.float32(0)),
        "moe_misc": misc,
        "m0_gate": chunks(i["L0_ffn_gate_w"].T), "m0_up": each(up0), "m0_down": each(i["L0_ffn_w2"]),
        "m1_gate": chunks(i["L1_ffn_gate_w"].T), "m1_up": each(up1), "m1_down": each(down1),
        "m1_gbias": np.broadcast_to(i["L1_ffn_gate_bias"], (P, EXPERTS)),
        "m1_bias": np.concatenate([np.concatenate([i["L1_ffn_sbu"][None], i["L1_ffn_bu"]], 0),
                                   np.concatenate([i["L1_ffn_sbd"][None], i["L1_ffn_bd"]], 0)], 1),
    }


def program(nc, io, out):
    at_most = (ROUTED + ALL_TILES) * P
    rows = nc.dram_tensor("expert_rows", [at_most, D], F32).ap()
    results = nc.dram_tensor("expert_results", [at_most, D], F32).ap()
    between = [nc.dram_tensor(f"x_{k}", [BATCH, SEQ, D], F32).ap() for k in range(3)]
    gated_attention(nc, io, io["x"], between[0])
    experts(nc, io, between[0], between[1], rows, results, 0)
    causal_attention(nc, io, between[1], between[2])
    experts(nc, io, between[2], out, rows, results, 1)


def kernel(**inputs):
    import concourse.bacc as bacc
    from concourse.bass_utils import run_bass_kernel_spmd

    nc = bacc.Bacc("TRN2", target_bir_lowering=False, num_devices=1)
    arrays = lay({k: np.asarray(v) for k, v in inputs.items()})
    arrays["x"] = np.ascontiguousarray(inputs["L0_attn_x"])
    io = {k: nc.dram_tensor(f"in_{k}", a.shape, mybir.dt.from_np(a.dtype), kind="ExternalInput").ap() for k, a in arrays.items()}
    out = nc.dram_tensor("out", [BATCH, SEQ, D], F32, kind="ExternalOutput").ap()
    program(nc, io, out)
    r = run_bass_kernel_spmd(nc, [{f"in_{k}": a for k, a in arrays.items()}], core_ids=[0])
    return r.results[0]["out"]
```

```python
from contextlib import ExitStack

import concourse.bass as bass
import numpy as np
from concourse import mybir

F32 = mybir.dt.float32
BF16 = mybir.dt.bfloat16
F32R = mybir.dt.float32r
U32 = mybir.dt.uint32
I32 = mybir.dt.int32
ALU = mybir.AluOpType
ACT = mybir.ActivationFunctionType
AX = mybir.AxisListType

P = 128
BATCH, SEQ, D = 4, 1024, 256
TILES = SEQ // P
ALL_TILES = BATCH * TILES
DC = D // P
EPS = 1e-5


class Steps:

    def __init__(self, engine, semaphore, base=0):
        self.engine, self.semaphore, self.base, self.n = engine, semaphore, base, 0

    def do(self, instruction):
        self.n += 1
        return instruction.then_inc(self.semaphore, 1)

    def done(self):
        self.engine.wait_ge(self.semaphore, self.base + self.n)


class Memory:

    def __init__(self, nc, stack, tag):
        self.nc, self.stack, self.tag, self.sems = nc, stack, tag, []
        stack.callback(self.clear)

    def clear(self):
        self.nc.clear_and_free_semaphores(self.sems)
        self.nc.all_engine_barrier()

    def sb(self, name, shape, dtype=F32):
        return self.stack.enter_context(self.nc.sbuf_tensor(f"{self.tag}_{name}", shape, dtype))

    def banks(self, n):
        return [self.stack.enter_context(self.nc.psum_tensor(f"{self.tag}_bank{i}", [P, 512], F32)) for i in range(n)]

    def sem(self, name):
        self.sems.append(self.nc.alloc_semaphore(f"{self.tag}_{name}"))
        return self.sems[-1]


QK, HID, GROUP = 64, 512, 64
HC = HID // P
NVG = 2 * HID + QK


def gated_attention(nc, io, x_in, x_out, rows):
    with ExitStack() as stack:
        m = Memory(nc, stack, "ga")
        sb, sem = m.sb, m.sem
        x = sb("x", [P, ALL_TILES, D])
        w_vgk = sb("w_vgk", [P, DC, NVG])
        w_high = sb("w_high", [P, DC, 2 * HID], F32R)
        w_low = sb("w_low", [P, DC, 2 * HID], F32R)
        w_o = sb("w_o", [P, HC, D])
        ident = sb("ident", [P, P])
        rope = sb("rope", [P, 2, TILES, QK])
        heads_wb = sb("heads_wb", [P, 2, 4, QK])
        group_bias = sb("group_bias", [P, P])
        ln1 = sb("ln1", [P, 2, DC])
        ln2 = sb("ln2", [P, 2, D])
        BIAS_ROWS = 64
        brow = sb("brow", [BIAS_ROWS, (NVG + D) // BIAS_ROWS])
        bthree = sb("bthree", [BIAS_ROWS, 3, (NVG + D) // BIAS_ROWS], BF16)
        bparts = sb("bparts", [P, NVG + D], BF16)
        bias_rows = nc.dram_tensor("ga_bias_rows", [3, NVG + D], BF16).ap()
        ones = sb("ones", [P, P], BF16)
        zero = sb("zero", [P, 8 * D])
        stats = sb("stats", [P, ALL_TILES, 6])
        mv = sb("mv", [P, ALL_TILES, 2])
        root = sb("root", [P, ALL_TILES])
        r1 = sb("r1", [P, ALL_TILES])
        var2 = sb("var2", [P, ALL_TILES])
        rstd = sb("rstd", [P, ALL_TILES])
        xn = sb("xn", [P, 2, D])
        xT_high = sb("xT_high", [P, 2, DC, P], F32R)
        xT_low = sb("xT_low", [P, 2, DC, P], F32R)
        xT = sb("xT", [P, 2, DC, P])
        v = sb("v", [P, TILES, HID])
        gate = sb("gate", [P, TILES, HID])
        qk = sb("qk", [P, 2, QK])
        hm = sb("hm", [P, 4, QK])
        hb = sb("hb", [P, 4, QK])
        hc = sb("hc", [P, 4, QK])
        hs = sb("hs", [P, 4, QK])
        heads = sb("heads", [P, 2, 5, QK])
        headsT = sb("headsT", [P, TILES, 2, P])
        z = sb("z", [P, P])
        attnT = sb("attnT", [P, TILES, P])
        kv = sb("kv", [P, HID])
        go = sb("go", [P, 2, HID])
        goT = sb("goT", [P, 2, HC, P])
        y = sb("y", [P, TILES, D])
        ystats = sb("ystats", [P, TILES, 6])
        ymv = sb("ymv", [P, TILES, 2])
        yroot = sb("yroot", [P, TILES])
        yrstd = sb("yrstd", [P, TILES])
        epst = sb("epst", [P, 1])

        bT, bR, bV, bG, bQ, bS, bKV, bY = m.banks(8)
        bO = [bV, bG]
        bGT = [bQ, bS]

        consts_in = sem("consts_in")
        x_loaded = [sem(f"x_loaded{b}") for b in range(BATCH)]
        bias_in, bias_split, bias_sent, bias_placed = sem("bias_in"), sem("bias_split"), sem("bias_sent"), sem("bias_placed")
        dve_step = sem("dve_step")
        ready = sem("ready")
        var_ready, root_ready = sem("var_ready"), sem("root_ready")
        xn_ready, xT_psum, xT_ready = sem("xn_ready"), sem("xT_psum"), sem("xT_ready")
        w_split, xT_high_ready, xT_low_ready = sem("w_split"), sem("xT_high_ready"), sem("xT_low_ready")
        v_psum, g_psum, q_psum = sem("v_psum"), sem("g_psum"), sem("q_psum")
        v_ready, g_ready, q_ready = sem("v_ready"), sem("g_ready"), sem("q_ready")
        heads_ready, headsT_psum, headsT_ready = sem("heads_ready"), sem("headsT_psum"), sem("headsT_ready")
        s_psum, attn_ready = sem("s_psum"), sem("attn_ready")
        kv_psum, kv_ready = sem("kv_psum"), sem("kv_ready")
        o_psum, go_ready, goT_psum, goT_ready = sem("o_psum"), sem("go_ready"), sem("goT_psum"), sem("goT_ready")
        y_psum, y_ready = sem("y_psum"), sem("y_ready")
        yvar_ready, yroot_ready = sem("yvar_ready"), sem("yroot_ready")
        POOL_TILES = 6
        last_scaled, dve_last, pool_last, pool_sums = sem("last_scaled"), sem("dve_last"), sem("pool_last"), sem("pool_sums")
        x_done, stored, cleared = sem("x_done"), sem("stored"), sem("cleared")
        waited = sem("waited")
        N_CONST = 8

        def part_columns(part):
            return slice(0, TILES) if part == 0 else slice(TILES, ALL_TILES)

        block = stack.enter_context(nc.Block())

        @block.sync
        def _(sp):
            def load(b):
                sp.dma_start(x[:, b * TILES:(b + 1) * TILES, :], x_in[b].rearrange("(t p) d -> p t d", p=P)).then_inc(x_loaded[b], 16)

            load(0)
            sp.wait_ge(bias_split, 1)
            sp.wait_ge(ready, 4)
            sp.dma_start(bias_rows.rearrange("k (p n) -> p k n", p=BIAS_ROWS), bthree[:, :, :]).then_inc(bias_sent, 16)
            sp.wait_ge(bias_sent, 16)
            for k in range(3):
                sp.dma_start(bparts[32 * k:32 * k + 1, :], bias_rows[k:k + 1, :]).then_inc(bias_placed, 16)
            for b in range(1, BATCH):
                load(b)
            with sp.Fori(0, BATCH - 1) as b:
                sp.wait_ge(x_done, b + 1)
                sp.dma_start(x_out[b].rearrange("(t p) d -> p t d", p=P), x[:, bass.ds(b * TILES, TILES), :]).then_inc(stored, 16)
            last_out, first = x_out[BATCH - 1].rearrange("(t p) d -> p t d", p=P), (BATCH - 1) * TILES
            sp.wait_ge(x_done, BATCH)
            sp.dma_start(last_out[:, 0:POOL_TILES, :], x[:, first:first + POOL_TILES, :]).then_inc(stored, 16)
            sp.wait_ge(pool_sums, 1)
            sp.dma_start(last_out[:, POOL_TILES:TILES, :], x[:, first + POOL_TILES:first + TILES, :]).then_inc(stored, 16)
            sp.wait_ge(stored, 16 * (BATCH + 1))

        def finish_last(eng, tiles, step):
            eng.wait_ge(last_scaled, 1)
            for t in tiles:
                eng.tensor_scalar(y[:, t, :], y[:, t, :], ymv[:, t, 0:1], yrstd[:, t:t + 1], ALU.subtract, ALU.mult).then_inc(step, 1)
            n = len(tiles)
            eng.wait_ge(step, n)
            ys = y[:, tiles[0]:tiles[0] + n, :]
            eng.tensor_tensor(ys, ys, ln2[:, 0, None, :].to_broadcast([P, n, D]), ALU.mult).then_inc(step, 1)
            eng.wait_ge(step, n + 1)
            eng.tensor_tensor(ys, ys, ln2[:, 1, None, :].to_broadcast([P, n, D]), ALU.add).then_inc(step, 1)
            eng.wait_ge(step, n + 2)
            first = (BATCH - 1) * TILES + tiles[0]
            return eng.tensor_tensor(x[:, first:first + n, :], x[:, first:first + n, :], ys, ALU.add)

        @block.gpsimd
        def _(pool):
            pool.memset(ones[:, :], 1.0).then_inc(ready, 1)
            pool.memset(bparts[:, :], 0.0).then_inc(ready, 1)
            pool.memset(kv[:, :], 0.0).then_inc(ready, 1)
            pool.memset(heads[:, :, :, :], 0.0).then_inc(ready, 1)
            pool.memset(zero[:, :], 0.0).then_inc(ready, 1)
            pool.wait_ge(ready, 5)
            pool.wait_ge(x_loaded[BATCH - 1], 16)
            per = P * 8
            for k in range(rows.shape[0] // per):
                pool.dma_start(rows[k * per:(k + 1) * per, :].rearrange("(p r) d -> p (r d)", p=P), zero[:, :]).then_inc(cleared, 16)
            pool.wait_ge(cleared, 16 * (rows.shape[0] // per))
            finish_last(pool, range(POOL_TILES, TILES), pool_last).then_inc(pool_sums, 1)

        @block.scalar
        def _(act):
            act.dma_start(brow[:, :], io["ga_brow"]).then_inc(bias_in, 16)
            for dst, src in ((w_vgk[:, :, :], io["ga_w"]), (w_o[:, :, :], io["ga_wo"]), (ident[:, :], io["ident"]),
                             (rope[:, :, :, :], io["ga_rope"]), (heads_wb[:, :, :, :], io["ga_heads"]),
                             (group_bias[:, :], io["ga_bias"]), (ln1[:, :, :], io["ga_ln1"]), (ln2[:, :, :], io["ga_ln2"])):
                act.dma_start(dst, src).then_inc(consts_in, 16)

            def deviations(part):
                cols = part_columns(part)
                for k, s in enumerate((mv[:, cols, 1], var2[:, cols])):
                    act.wait_ge(var_ready, 2 * part + k + 1)
                    act.activation(root[:, cols], s, ACT.Sqrt, bias=epst[:, 0:1]).then_inc(root_ready, 1)

            deviations(0)
            act.wait_ge(consts_in, 16 * N_CONST)
            act.activation(w_high[:, :, :], w_vgk[:, :, 0:2 * HID], ACT.Identity).then_inc(w_split, 1)

            def sequence(b):
                n0 = b * TILES

                def turned_heads(t):
                    act.wait_ge(headsT_psum, n0 + t + 1)
                    act.activation(headsT[:, t, :, :], bR[:, 0:2 * P].rearrange("p (c n) -> p c n", c=2), ACT.Identity).then_inc(headsT_ready, 1)

                def turned_rows(t):
                    act.wait_ge(xT_psum, n0 + t + 1)
                    for c in range(DC):
                        i = act.activation(xT[:, t % 2, c, :], bT[:, c * P:(c + 1) * P], ACT.Identity,
                                           bias=ln1[:, 1, c:c + 1], scale=ln1[:, 0, c:c + 1])
                    i.then_inc(xT_ready, 1)
                    for c in range(DC):
                        i = act.activation(xT_high[:, t % 2, c, :], bT[:, c * P:(c + 1) * P], ACT.Identity,
                                           bias=ln1[:, 1, c:c + 1], scale=ln1[:, 0, c:c + 1])
                    i.then_inc(xT_high_ready, 1)

                turned_rows(0)
                for t in range(TILES):
                    if t + 1 < TILES:
                        turned_rows(t + 1)
                    act.wait_ge(q_psum, n0 + t + 1)
                    act.activation(qk[:, t % 2, :], bQ[:, 0:QK], ACT.Silu).then_inc(q_ready, 1)
                    if t == 0 and not isinstance(b, int):
                        act.wait_ge(o_psum, n0 + 1)
                    act.wait_ge(v_psum, n0 + t + 1)
                    act.activation(v[:, t, :], bV[:, :], ACT.Silu).then_inc(v_ready, 1)
                    act.wait_ge(g_psum, n0 + t + 1)
                    act.activation(gate[:, t, :], bG[:, :], ACT.Silu).then_inc(g_ready, 1)
                    if t:
                        turned_heads(t - 1)
                turned_heads(TILES - 1)
                act.wait_ge(kv_psum, b + 1)
                act.activation(kv[0:QK, :], bKV[0:QK, :], ACT.Identity, scale=1.0 / SEQ).then_inc(kv_ready, 1)
                for t in range(TILES):
                    act.wait_ge(goT_psum, n0 + t + 1)
                    act.activation(goT[:, t % 2, :, :], bGT[t % 2][:, :].rearrange("p (c n) -> p c n", c=HC), ACT.Identity).then_inc(goT_ready, 1)
                    act.wait_ge(y_psum, n0 + t + 1)
                    act.activation(y[:, t, :], bY[:, 0:D], ACT.Identity).then_inc(y_ready, 1)
                if isinstance(b, int):
                    deviations(1)
                act.wait_ge(yvar_ready, b + 1)
                act.activation(yroot[:, :], ymv[:, :, 1], ACT.Sqrt, bias=epst[:, 0:1]).then_inc(yroot_ready, 1)

            sequence(0)
            with act.Fori(1, BATCH) as b:
                sequence(b)

        @block.vector
        def _(dve):
            s = Steps(dve, dve_step)
            s.do(dve.memset(epst[:, :], EPS))
            dve.wait_ge(bias_in, 16)
            for k in range(3):
                s.do(dve.tensor_copy(bthree[:, k, :], brow[:, :])); s.done()
                if k < 2:
                    s.do(dve.tensor_tensor(brow[:, :], brow[:, :], bthree[:, k, :], ALU.subtract)); s.done()
            dve.sem_inc(bias_split, 1)

            def input_stats(tiles):
                for n in tiles:
                    if n % TILES == 0:
                        dve.wait_ge(x_loaded[n // TILES], 16)
                    s.do(dve.bn_stats(stats[:, n, :], x[:, n, :]))
                s.done()
                for n in tiles:
                    s.do(dve.bn_aggr(mv[:, n, :], stats[:, n, :]))

            def input_scales(part):
                cols = part_columns(part)
                s.done()
                dve.sem_inc(var_ready, 1)
                dve.wait_ge(root_ready, 2 * part + 1)
                s.do(dve.reciprocal(r1[:, cols], root[:, cols])); s.done()
                s.do(dve.tensor_tensor(var2[:, cols], r1[:, cols], r1[:, cols], ALU.mult)); s.done()
                s.do(dve.tensor_tensor(var2[:, cols], var2[:, cols], mv[:, cols, 1], ALU.mult)); s.done()
                dve.sem_inc(var_ready, 1)
                dve.wait_ge(root_ready, 2 * part + 2)
                s.do(dve.reciprocal(rstd[:, cols], root[:, cols])); s.done()
                s.do(dve.tensor_tensor(rstd[:, cols], rstd[:, cols], r1[:, cols], ALU.mult)); s.done()

            input_stats(range(TILES))
            input_scales(0)
            dve.wait_ge(consts_in, 16 * N_CONST)
            dve.wait_ge(ready, 4)

            def normalise(b, t):
                n = b * TILES + t
                if t >= 2:
                    dve.wait_ge(xT_psum, n - 1)
                dve.tensor_scalar(xn[:, t % 2, :], x[:, bass.ds(n, 1), :].rearrange("p a d -> p (a d)"),
                                  mv[:, bass.ds(n, 1), 0], rstd[:, bass.ds(n, 1)],
                                  ALU.subtract, ALU.mult).then_inc(xn_ready, 1)

            def low_rows(b, t):
                dve.wait_ge(xT_high_ready, b * TILES + t + 1)
                dve.tensor_tensor(xT_low[:, t % 2, :, :], xT[:, t % 2, :, :], xT_high[:, t % 2, :, :].bitcast(F32), ALU.subtract).then_inc(xT_low_ready, 1)

            def make_heads(b, t):
                n = b * TILES + t
                dve.wait_ge(q_ready, n + 1)
                if t >= 2:
                    dve.wait_ge(headsT_psum, n - 1)
                    dve.wait_ge(s_psum, n - 1)
                q4 = qk[:, t % 2, None, :].to_broadcast([P, 4, QK])
                s.do(dve.tensor_tensor(hm[:, :, :], q4, heads_wb[:, 0, :, :], ALU.mult)); s.done()
                s.do(dve.tensor_tensor(hb[:, :, :], hm[:, :, :], heads_wb[:, 1, :, :], ALU.add)); s.done()
                cos = rope[:, 0, t, None, :].to_broadcast([P, 4, QK])
                s.do(dve.tensor_tensor(hc[:, :, :], hb[:, :, :], cos, ALU.mult))
                for a, c in ((0, 1), (1, 0)):
                    half = QK // 2
                    sin = rope[:, 1, t, None, a * half:(a + 1) * half].to_broadcast([P, 4, half])
                    s.do(dve.tensor_tensor(hs[:, :, a * half:(a + 1) * half], hb[:, :, c * half:(c + 1) * half], sin, ALU.mult))
                s.done()
                dve.tensor_tensor(heads[:, t % 2, 0:2, :], hc[:, 0:2, :], hs[:, 0:2, :], ALU.add)
                s.do(dve.tensor_tensor(heads[:, t % 2, 3:5, :], hc[:, 2:4, :], hs[:, 2:4, :], ALU.add)); s.done()
                dve.sem_inc(heads_ready, 1)

            def attention(b, t):
                dve.wait_ge(s_psum, b * TILES + t + 1)
                s.do(dve.scalar_tensor_tensor(out=z[:, :], in0=bS[:, 0:P], scalar=1.0 / GROUP, in1=group_bias[:, :],
                                              op0=ALU.mult, op1=ALU.add)); s.done()
                s.do(dve.scalar_tensor_tensor(out=attnT[:, t, :], in0=z[:, :], scalar=0.0, in1=z[:, :],
                                              op0=ALU.max, op1=ALU.mult)); s.done()
                dve.sem_inc(attn_ready, 1)

            def gated(b, t):
                n = b * TILES + t
                dve.wait_ge(o_psum, n + 2)
                if t >= 2:
                    dve.wait_ge(goT_psum, n - 1)
                dve.wait_ge(g_ready, n + 1)
                dve.tensor_tensor(go[:, t % 2, :], bO[t % 2][:, :], gate[:, t, :], ALU.mult).then_inc(go_ready, 1)

            def row_stats(b, t):
                dve.wait_ge(y_ready, b * TILES + t + 1)
                s.do(dve.bn_stats(ystats[:, t, :], y[:, t, :]))

            def moments(b):
                s.done()
                dve.sem_inc(waited, 1)
                for t in range(TILES):
                    s.do(dve.bn_aggr(ymv[:, t, :], ystats[:, t, :]))
                s.done()
                dve.sem_inc(yvar_ready, 1)

            def finish(b, t):
                if t == 0:
                    dve.wait_ge(yroot_ready, b + 1)
                    s.do(dve.reciprocal(yrstd[:, :], yroot[:, :])); s.done()
                n = b * TILES + t
                yt = y[:, t, :]
                s.do(dve.tensor_scalar(yt, yt, ymv[:, t, 0:1], yrstd[:, t:t + 1], ALU.subtract, ALU.mult)); s.done()
                s.do(dve.tensor_tensor(yt, yt, ln2[:, 0, :], ALU.mult)); s.done()
                s.do(dve.tensor_tensor(yt, yt, ln2[:, 1, :], ALU.add)); s.done()
                xs = x[:, n, :] if isinstance(n, int) else x[:, bass.ds(n, 1), :].rearrange("p a d -> p (a d)")
                s.do(dve.tensor_tensor(xs, xs, yt, ALU.add))
                if t == TILES - 1:
                    s.done()
                    dve.sem_inc(x_done, 1)

            def sequence(b, follows):
                normalise(b, 0)
                normalise(b, 1)
                if not follows:
                    dve.wait_ge(w_split, 1)
                    dve.tensor_tensor(w_low[:, :, :], w_vgk[:, :, 0:2 * HID], w_high[:, :, :].bitcast(F32), ALU.subtract).then_inc(w_split, 1)
                low_rows(b, 0)
                for t in range(TILES):
                    if t + 1 < TILES:
                        low_rows(b, t + 1)
                    if t + 2 < TILES:
                        normalise(b, t + 2)
                    make_heads(b, t)
                    if t >= 2:
                        attention(b, t - 2)
                    if follows:
                        finish(b - 1, t)
                    else:
                        others = ALL_TILES - TILES
                        input_stats(range(TILES + others * t // TILES, TILES + others * (t + 1) // TILES))
                attention(b, TILES - 2)
                attention(b, TILES - 1)
                for t in range(TILES):
                    gated(b, t)
                    if t:
                        row_stats(b, t - 1)
                row_stats(b, TILES - 1)
                if not follows:
                    input_scales(1)
                moments(b)

            sequence(0, False)
            once, PER = s.n, TILES * (6 + 2 + 1 + 1 + 4) + 1
            with dve.Fori(1, BATCH) as b:
                s.base, s.n = once + (b - 1) * PER, 0
                sequence(b, True)
                assert s.n == PER
            s.base, s.n = once + (BATCH - 1) * PER, 0
            dve.wait_ge(yroot_ready, BATCH)
            dve.reciprocal(yrstd[:, :], yroot[:, :]).then_inc(last_scaled, 1)
            finish_last(dve, range(0, POOL_TILES), dve_last).then_inc(x_done, 1)

        @block.tensor
        def _(pe):
            pe.wait_ge(ready, 4)
            pe.wait_ge(bias_placed, 16 * 3)
            pe.wait_ge(w_split, 2)
            pe.wait_ge(consts_in, 16 * N_CONST)
            pe.sem_inc(o_psum, 1)

            def turn_rows(b, t):
                n = b * TILES + t
                pe.wait_ge(xn_ready, n + 1)
                if t:
                    pe.wait_ge(xT_high_ready, n)
                for c in range(DC):
                    i = pe.transpose(bT[:, c * P:(c + 1) * P], xn[:, t % 2, c * P:(c + 1) * P], ident[:, :])
                i.then_inc(xT_psum, 1)

            def project(b, t):
                n = b * TILES + t
                pe.wait_ge(xT_ready, n + 1)
                pe.wait_ge(xT_low_ready, n + 1)
                if t:
                    pe.wait_ge(g_ready, n)
                for bank, at, width, signal in ((bQ, 2 * HID, QK, q_psum), (bV, 0, HID, v_psum), (bG, HID, HID, g_psum)):
                    for c in range(DC):
                        if bank is bQ:
                            pe.matmul(bank[:, 0:width], xT[:, t % 2, c, :], w_vgk[:, c, at:at + width], start=(c == 0), stop=False)
                            continue
                        for turned, weights in ((xT_high, w_high), (xT_high, w_low), (xT_low, w_high)):
                            pe.matmul(bank[:, 0:width], turned[:, t % 2, c, :], weights[:, c, at:at + width],
                                      start=(c == 0 and weights is w_high and turned is xT_high), stop=False)
                    pe.matmul(bank[:, 0:width], ones[:, :], bparts[:, at:at + width], start=False, stop=True).then_inc(signal, 1)

            def turn_heads(b, t):
                n = b * TILES + t
                pe.wait_ge(heads_ready, n + 1)
                if t:
                    pe.wait_ge(headsT_ready, n)
                for c in range(2):
                    i = pe.transpose(bR[:, c * P:(c + 1) * P], heads[:, t % 2, 2 * c:2 * c + 2, :].rearrange("p a d -> p (a d)"), ident[:, :])
                i.then_inc(headsT_psum, 1)

            def scores(b, t):
                n = b * TILES + t
                pe.wait_ge(v_ready, n + 1)
                i = pe.matmul(bKV[0:QK, :], heads[:, t % 2, 4, :], v[:, t, :], start=(t == 0), stop=(t == TILES - 1))
                if t == TILES - 1:
                    i.then_inc(kv_psum, 1)
                pe.wait_ge(headsT_ready, n + 1)
                if t:
                    pe.wait_ge(attn_ready, n)
                pe.matmul(bS[:, 0:P], headsT[:, t, 1, :], headsT[:, t, 0, :], start=True, stop=True).then_inc(s_psum, 1)

            def outputs(b, t):
                n = b * TILES + t
                if t == 0:
                    pe.wait_ge(kv_ready, b + 1)
                    pe.wait_ge(g_ready, (b + 1) * TILES)
                    pe.wait_ge(attn_ready, (b + 1) * TILES)
                if t >= 2:
                    pe.wait_ge(go_ready, n - 1)
                pe.matmul(bO[t % 2][:, :], attnT[:, t, :], v[:, t, :], start=True, stop=False)
                pe.matmul(bO[t % 2][:, :], headsT[:, t, 0, :], kv[:, :], start=False, stop=True).then_inc(o_psum, 1)

            def turn_gated(b, t):
                n = b * TILES + t
                pe.wait_ge(go_ready, n + 1)
                if t >= 2:
                    pe.wait_ge(goT_ready, n - 1)
                for c in range(HC):
                    i = pe.transpose(bGT[t % 2][:, c * P:(c + 1) * P], go[:, t % 2, c * P:(c + 1) * P], ident[:, :])
                i.then_inc(goT_psum, 1)

            def project_out(b, t):
                n = b * TILES + t
                pe.wait_ge(goT_ready, n + 1)
                if t:
                    pe.wait_ge(y_ready, n)
                for c in range(HC):
                    pe.matmul(bY[:, 0:D], goT[:, t % 2, c, :], w_o[:, c, :], start=(c == 0), stop=False)
                pe.matmul(bY[:, 0:D], ones[:, :], bparts[:, NVG:NVG + D], start=False, stop=True).then_inc(y_psum, 1)

            with pe.Fori(0, BATCH) as b:
                turn_rows(b, 0)
                for t in range(TILES):
                    if t + 1 < TILES:
                        turn_rows(b, t + 1)
                    project(b, t)
                    if t:
                        turn_heads(b, t - 1)
                    if t >= 2:
                        scores(b, t - 2)
                turn_heads(b, TILES - 1)
                scores(b, TILES - 2)
                scores(b, TILES - 1)
                for t in range(TILES + 2):
                    if t < TILES:
                        outputs(b, t)
                    if 1 <= t <= TILES:
                        turn_gated(b, t - 1)
                    if t >= 2:
                        project_out(b, t - 2)


EXPERTS, TOPK, UP = 8, 2, 1024
ASSIGNED = TOPK * BATCH * SEQ
ROUTED = (ASSIGNED + EXPERTS * (P - 1)) // P
ROUTED += ROUTED % 2


def experts(nc, io, x_in, x_out, rows, results, layer):
    gated = layer == 0
    shared = 0 if gated else 1
    n_exp = EXPERTS + shared
    hidden = UP // 2 if gated else UP
    hc = hidden // P
    QUARTER = ALL_TILES // 4
    SH = shared * ALL_TILES // 2
    LAST = SH + ROUTED
    BLOCKS = LAST + SH
    with ExitStack() as stack:
        m = Memory(nc, stack, f"moe{layer}")
        sb, sem = m.sb, m.sem
        w_up = sb("w_up", [P, EXPERTS, DC, UP])
        act_out = sb("act_out", [P, 2, hidden])
        if shared:
            low_shared = sb("low_shared", [P, 1, DC, UP], F32R)

        def first_weights(e):
            return act_out[:, :, :] if shared and e == 0 else w_up[:, e - shared, :, :]

        def low_weights(e):
            return low_shared[:, 0, :, :] if shared else w_up[:, e, :, :].bitcast(F32R)

        w_down = sb("w_down", [P, n_exp, hc, D])
        if gated:
            high = sb("high", [P, n_exp, DC, UP], F32R)
            LATE = n_exp
            HIGH_LATE = n_exp - ALL_TILES * D // (DC * UP)
            xn_all = high[:, HIGH_LATE:n_exp, :, :].bitcast(F32).rearrange("p e c n -> p (e c n)").rearrange("p (t d) -> p t d", d=D)
        else:
            high = sb("high", [P, 1, DC, UP], F32R)
            LATE = n_exp - ALL_TILES * D // (DC * UP)
            xn_all = w_up[:, LATE - 1:, :, :].rearrange("p e c n -> p (e c n)").rearrange("p (t d) -> p t d", d=D)
        spare = None if gated else w_down[:, LATE:n_exp, :, :].rearrange("p e c n -> p (e c n)")
        used = [0]

        def early(name, shape, dtype=F32):
            if gated:
                return sb(name, shape, dtype)
            n = int(np.prod(shape[1:])) * (2 if dtype == BF16 else 4) // 4
            view = spare[0:shape[0], used[0]:used[0] + n]
            used[0] += n
            if dtype != F32:
                view = view.bitcast(dtype)
            if len(shape) == 3:
                view = view.rearrange("p (a b) -> p a b", b=shape[2])
            if len(shape) == 4:
                view = view.rearrange("p (a b c) -> p a b c", b=shape[2], c=shape[3])
            return view

        ident = sb("ident", [P, P])
        misc = early("misc", [P, P + EXPERTS + ALL_TILES + ROUTED])
        if gated:
            slots = sb("slots", [P, P + ALL_TILES])
            slot_int = sb("slot_int", [P, TOPK, ALL_TILES], U32)
            slot = sb("slot", [P, TOPK, ALL_TILES])
            blk = sb("blk", [P, TOPK, ALL_TILES])
            RING = 4
            at_slot = sb("at_slot", [P, RING, P])
            in_block = sb("in_block", [P, RING, ROUTED])
            token = sb("token", [P, ROUTED], U32)
        w_gate = early("w_gate", [P, DC, EXPERTS])
        gbias = early("gbias", [P, EXPERTS])
        before = early("before", [P, P], BF16)
        ones = sb("ones", [P, P], BF16)
        if not gated:
            b_row = early("b_row", [n_exp, UP + D])
            b_parts = early("b_parts", [n_exp, 3, UP + D], BF16)
            b_dram = nc.dram_tensor("moe_bias_parts", [n_exp, 3, UP + D], BF16).ap()
            b_table = sb("b_table", [P, n_exp, UP + D], BF16)
        stats = early("stats", [P, ALL_TILES, 6])
        mv = early("mv", [P, ALL_TILES, 2])
        root = early("root", [P, ALL_TILES])
        rstd = early("rstd", [P, ALL_TILES])
        epst = sb("epst", [P, 1])
        te = [P, ALL_TILES, EXPERTS]
        logit = early("logit", te)
        prob = early("prob", te)
        top = early("top", te)
        small = early("small", [P, ALL_TILES])
        hot = early("hot", [P, TOPK, ALL_TILES, EXPERTS])
        both = early("both", te)
        both16 = early("both16", te, BF16)
        upto = early("upto", te)
        place = early("place", te)
        picked = early("picked", te)
        over = early("over", [P, EXPERTS, ALL_TILES])
        nblk = early("nblk", [P, EXPERTS])
        blk_end = sb("blk_end", [P, EXPERTS])
        blk_start = early("blk_start", [P, EXPERTS])
        one8 = early("one8", [P, ALL_TILES])
        posf = early("posf", [P, TOPK, ALL_TILES])
        pos = sb("pos", [P, TOPK, ALL_TILES], U32)
        weight = sb("weight", [P, TOPK, ALL_TILES])
        passed = early("passed", [P, ROUTED, EXPERTS])
        ownerf = early("ownerf", [P, BLOCKS])
        if gated:
            owner = sb("owner", [P, BLOCKS], I32)
        else:
            rest = sb("rest", [P, 2, 4, D])
            owner = rest[:, 1, TOPK, 0:BLOCKS].bitcast(I32)
        xb = sb("xb", [P, 2, D])
        xT = sb("xT", [P, 2, DC, P], F32R)
        xT_low = sb("xT_low", [P, 2, DC, P], F32R)
        xT_whole = None if gated else rest[:, 0, 0:TOPK, :].rearrange("p q (c n) -> p q c n", c=DC)
        h = sb("h", [P, 2, hidden]) if gated else act_out
        hT = sb("hT", [P, 2, hc, P])
        gT = hT[:, :, 0:2 * DC, :]
        yb = sb("yb", [P, 2, D])
        if gated:
            SLOTS = 8
            free = high[:, :, :, :].bitcast(F32).rearrange("p e c n -> p (e c n)")
            rest = free[:, 0:SLOTS * 4 * D].rearrange("p (q k d) -> p q k d", q=SLOTS, d=D)
            part = free[:, SLOTS * 4 * D:SLOTS * 5 * D].rearrange("p (q d) -> p q d", d=D)
        else:
            SLOTS = 2
            part = yb
        y_in, x_res = rest[:, :, 0:TOPK + shared, :], rest[:, :, 3, :]

        bX, bU0, bU1, bU2, bU3, bH0, bH1, bY = m.banks(8)
        bU = [(bU0, bU1), (bU2, bU3)]

        consts_in, w_in, x_loaded = sem("consts_in"), sem("w_in"), [sem(f"x_loaded{q}") for q in range(4)]
        late_in, high_ready, low_ready, xT_low_ready = sem("late_in"), sem("high_ready"), sem("low_ready"), sem("xT_low_ready")
        marks_ready, marks_used, token_ready = sem("marks_ready"), sem("marks_used"), sem("token_ready")
        ready, dve_step = sem("ready"), sem("dve_step")
        var_ready, root_ready, xn_ready = sem("var_ready"), sem("root_ready"), sem("xn_ready")
        gT_psum, gT_ready, logit_psum = sem("gT_psum"), sem("gT_ready"), sem("logit_psum")
        exp_in, exp_ready = sem("exp_in"), sem("exp_ready")
        both_ready, rank_psum, routed = sem("both_ready"), sem("rank_psum"), sem("routed")
        sent, copied = [sem(f"sent{q}") for q in range(4)], sem("copied")
        bias_in, b_ready, b_sent, b_in = sem("bias_in"), sem("b_ready"), sem("b_sent"), sem("b_in")
        xb_in, xT_psum, xT_ready = [sem("xb_in0"), sem("xb_in1")], sem("xT_psum"), sem("xT_ready")
        u_psum, a_ready, h_ready = sem("u_psum"), sem("a_ready"), sem("h_ready")
        hT_psum, hT_ready, y_psum, yb_ready, yb_out = sem("hT_psum"), sem("hT_ready"), sem("y_psum"), sem("yb_ready"), [sem("yb_out0"), sem("yb_out1")]
        hT_ready2 = sem("hT_ready2")
        out_ready = sem("out_ready")
        gathered, res_in, stored = [[sem(f"{x}{q}") for q in range(SLOTS)] for x in ("gathered", "res_in", "stored")]
        sh_in = sem("sh_in")
        N_CONST = 4
        HALF_TILES = ALL_TILES // 2

        SPLIT = n_exp if gated else 1
        runs = [(1, 0, BLOCKS)] if gated else [(0, 0, SH), (1, SH, LAST), (2, LAST, BLOCKS)]

        def in_parts(t):
            return gated or (not SH <= t.j < LAST if isinstance(t.j, int) else t.run != 1)

        def low_count(t):
            last = t.j >= LAST if isinstance(t.j, int) else t.run == 2
            return t.j + 1 - (ROUTED if last and not gated else 0)

        SHARED_ROWS = ROUTED * P
        routed_rows, routed_results = rows[0:SHARED_ROWS, :], results[0:SHARED_ROWS, :]
        x_tiles = x_in.rearrange("b (t p) d -> p (b t) d", p=P)
        block = stack.enter_context(nc.Block())

        @block.sync
        def _(sp):
            for out in yb_out:
                sp.sem_inc(out, 16)
            for q in range(4):
                n = ALL_TILES // 4
                sp.dma_start(xn_all[:, q * n:(q + 1) * n, :], x_tiles[:, q * n:(q + 1) * n, :]).then_inc(x_loaded[q], 16)
            for q in range(4):
                sp.wait_ge(x_loaded[q], 16)
            for e in range(LATE):
                sp.dma_start(first_weights(e), io[f"m{layer}_up"][e]).then_inc(w_in, 16)
                sp.dma_start(w_down[:, e, :, :], io[f"m{layer}_down"][e]).then_inc(w_in, 16)
            plain = 0 if gated else SHARED_ROWS
            sp.wait_ge(xn_ready, ALL_TILES)
            sp.dma_start(rows[plain:plain + ALL_TILES * P, :].rearrange("(t p) d -> p t d", p=P), xn_all[:, :, :]).then_inc(copied, 16)
            sp.wait_ge(copied, 16)

            def load_block(t, origin):
                if t.n >= 2:
                    sp.wait_ge(xT_psum, t.j - 1)
                sp.dma_start(xb[:, t.side, :], rows[bass.ds(t.j * P + origin, P), :]).then_inc(xb_in[t.side], 16)

            def store_block(t, origin):
                sp.wait_ge(yb_ready, t.j + 1)
                sp.dma_start(results[bass.ds(t.j * P + origin, P), :], yb[:, t.side, :]).then_inc(yb_out[t.side], 16)

            def pass_blocks(first, end, origin):
                for j in range(first, first + 4):
                    load_block(Turn(j // 2, j % 2, j), origin)
                    if j >= 3:
                        store_block(at(j - 3), origin if j - 3 >= first else SHARED_ROWS)
                with sp.Fori(first // 2 + 2, end // 2) as pair:
                    load_block(Turn(pair, 0, 2), origin)
                    store_block(Turn(pair - 2, 1, 3), origin)
                    load_block(Turn(pair, 1, 3), origin)
                    store_block(Turn(pair - 1, 0, 2), origin)

            if SH:
                pass_blocks(0, SH, SHARED_ROWS)
            if gated:
                with sp.Fori(0, BLOCKS // 2) as pair:
                    for side in range(2):
                        store_block(Turn(pair, side, 2 + side), 0)
            else:
                for q in range(4):
                    sp.wait_ge(sent[q], 16 * TOPK * QUARTER)
                pass_blocks(SH, LAST, -SH * P)
            if gated:
                for out in yb_out:
                    sp.wait_ge(out, 8 * LAST + 16)
                with sp.Fori(0, ALL_TILES // SLOTS) as i:
                    for q in range(SLOTS):
                        n = SLOTS * i + q
                        sp.wait_ge(out_ready, n + 1)
                        sp.dma_start(x_res[:, q, :], x_tiles[:, bass.ds(n, 1), :].rearrange("p a d -> p (a d)")).then_inc(res_in[q], 16)
            else:
                def load_rest(i, q):
                    sp.dma_start(x_res[:, q, :], x_tiles[:, bass.ds(q * SH + i, 1), :].rearrange("p a d -> p (a d)")).then_inc(res_in[q], 16)
                    if q == 0:
                        sp.dma_start(y_in[:, 0, TOPK, :], results[bass.ds(i * P + SHARED_ROWS, P), :]).then_inc(res_in[0], 16)

                def store_sum(i, q):
                    sp.wait_ge(out_ready, 2 * i + q + 1)
                    sp.dma_start(x_out.rearrange("b (t p) d -> p (b t) d", p=P)[:, bass.ds(q * SH + i, 1), :].rearrange("p a d -> p (a d)"), part[:, q, :]).then_inc(stored[q], 16)

                origin = SHARED_ROWS - ROUTED * P
                for side in range(2):
                    load_block(Turn(LAST // 2, side, 2 + side), origin)
                for j in range(LAST - 3, LAST):
                    store_block(at(j), -SH * P)
                for q in range(2):
                    sp.sem_inc(stored[q], 16)
                    load_rest(0, q)
                with sp.Fori(LAST // 2 + 1, BLOCKS // 2) as pair:
                    for side in range(2):
                        load_block(Turn(pair, side, 2 + side), origin)
                        i = 2 * pair + side - LAST
                        for q in range(2):
                            store_sum(i - 2, q)
                            load_rest(i - 1, q)
                for q in range(2):
                    store_sum(SH - 2, q)
                    load_rest(SH - 1, q)
                for q in range(2):
                    store_sum(SH - 1, q)
                for q in range(2):
                    sp.wait_ge(stored[q], 16 * (SH + 1))

        @block.gpsimd
        def _(pool):
            pool.memset(ones[:, :], 1.0).then_inc(ready, 1)
            if not gated:
                pool.memset(b_table[:, :, :], 0.0).then_inc(ready, 1)
            for e in range(SPLIT):
                pool.wait_ge(high_ready, e + 1)
                pool.tensor_tensor(low_weights(e), first_weights(e), high[:, e, :, :].bitcast(F32), ALU.subtract).then_inc(low_ready, 1)
            if gated:
                pool.wait_ge(token_ready, 1)
                pool.wait_ge(copied, 16)
                for j in range(ROUTED):
                    if j >= 2:
                        pool.wait_ge(xT_psum, j - 1)
                    pool.indirect_dma_start(xb[:, j % 2, :], None, rows[0:ALL_TILES * P, :],
                                            bass.IndirectOffsetOnAxis(ap=token[:, j:j + 1], axis=0)).then_inc(xb_in[j % 2], 16)
            else:
                pool.wait_ge(routed, 1)
                pool.wait_ge(xn_ready, ALL_TILES)
                if LATE < n_exp:
                    pool.wait_ge(copied, 16)
                    pool.wait_ge(gT_psum, ALL_TILES // 2)
                    pool.wait_ge(b_in, 16)
                    for e in range(LATE, n_exp):
                        pool.dma_start(w_down[:, e, :, :], io[f"m{layer}_down"][e]).then_inc(late_in, 16)
                for q in range(4 + 1):
                    for n in range(q * QUARTER, min((q + 1) * QUARTER, ALL_TILES)):
                        for k in range(TOPK):
                            pool.indirect_dma_start(routed_rows, bass.IndirectOffsetOnAxis(ap=pos_slot(pos, k, n), axis=0),
                                                    xn_all[:, n, :], None).then_inc(sent[q], 16)
                    if q and LATE < n_exp:
                        pool.wait_ge(sent[q - 1], 16 * TOPK * QUARTER)
                        pool.dma_start(first_weights(LATE + q - 1), io[f"m{layer}_up"][LATE + q - 1]).then_inc(late_in, 16)
            for out in yb_out:
                pool.wait_ge(out, 8 * LAST + 16)
            for m in range(ALL_TILES):
                n = m if gated else m % 2 * SH + m // 2
                if m >= SLOTS:
                    pool.wait_ge(out_ready, m + 1 if gated else m - 1)
                for k in range(TOPK):
                    pool.indirect_dma_start(y_in[:, m % SLOTS, k, :], None, routed_results,
                                            bass.IndirectOffsetOnAxis(ap=pos_slot(pos, k, n), axis=0)).then_inc(gathered[m % SLOTS], 16)

        @block.scalar
        def _(act):
            consts = [(slots[:, :], io["moe_slots"])] if gated else []
            consts += [(ident[:, :], io["ident"]), (misc[:, :], io["moe_misc"]), (w_gate[:, :, :], io[f"m{layer}_gate"])]
            if not gated:
                act.dma_start(b_row[:, :], io["m1_bias"]).then_inc(bias_in, 16)
                consts += [(gbias[:, :], io["m1_gbias"])]
            for dst, src in consts:
                act.dma_start(dst, src).then_inc(consts_in, 16)
            if not gated:
                act.wait_ge(b_ready, 1)
                act.wait_ge(ready, 2)
                act.dma_start(b_dram, b_parts[:, :, :]).then_inc(b_sent, 16)
                act.wait_ge(b_sent, 16)
                act.dma_start(b_table[0:3, :, :], b_dram.rearrange("e k n -> k e n")).then_inc(b_in, 16)

            def deviations(q):
                cols = slice(q * QUARTER, (q + 1) * QUARTER)
                act.wait_ge(var_ready, q + 1)
                act.activation(root[:, cols], mv[:, cols, 1], ACT.Sqrt, bias=epst[:, 0:1]).then_inc(root_ready, 1)

            deviations(0)
            for t in range(ALL_TILES // 2):
                act.wait_ge(gT_psum, t + 1)
                if t >= 2:
                    act.wait_ge(logit_psum, 2 * (t - 1))
                act.activation(gT[:, t % 2, :, :], bU[t % 2][0][:, :].rearrange("p (c n) -> p c n", c=2 * DC), ACT.Identity).then_inc(gT_ready, 1)
                if t % 4 == 1 and t // 4 + 1 < 4:
                    deviations(t // 4 + 1)
            act.wait_ge(exp_in, 1)
            act.activation(prob[:, :, :], logit[:, :, :], ACT.Exp if gated else ACT.Sigmoid).then_inc(exp_ready, 1)

            act.wait_ge(w_in, 16 * 2 * LATE)
            for e in range(SPLIT):
                if gated and e == HIGH_LATE:
                    act.wait_ge(copied, 16)
                    act.wait_ge(gT_psum, ALL_TILES // 2)
                act.activation(high[:, e, :, :], first_weights(e), ACT.Identity).then_inc(high_ready, 1)

            def turned(t):
                j, n = t.j, t.n
                act.wait_ge(xT_psum, j + 1)
                dst = xT if in_parts(t) else xT_whole
                act.activation(dst[:, n % 2, :, :], bX[:, 0:DC * P].rearrange("p (c n) -> p c n", c=DC), ACT.Identity).then_inc(xT_ready, 1)

            def nonlinear(t):
                j, n = t.j, t.n
                act.wait_ge(u_psum, j + 1)
                if n >= 2:
                    act.wait_ge(h_ready if gated else hT_psum, j - 1)
                if gated:
                    act.activation(act_out[:, n % 2, :], bU[n % 2][0][:, :], ACT.Silu).then_inc(a_ready, 1)
                else:
                    for k in range(2):
                        i = act.activation(act_out[:, n % 2, k * 512:(k + 1) * 512], bU[n % 2][k][:, :], ACT.Gelu)
                    i.then_inc(a_ready, 1)

            def turned_hidden(t):
                j, n = t.j, t.n
                act.wait_ge(hT_psum, j + 1)
                if n >= 2:
                    act.wait_ge(y_psum, j - 1)
                act.activation(hT[:, n % 2, 0:4, :], bH0[:, :].rearrange("p (c n) -> p c n", c=4), ACT.Identity).then_inc(hT_ready, 1)

            turned(at(0))

            def act_block(t):
                j, n = t.j, t.n
                nonlinear(t)
                if n + 1 < BLOCKS:
                    turned(t.after())
                turned_hidden(t)
            for_blocks(act, runs, act_block)
            if gated:
                for q in range(SLOTS):
                    act.sem_inc(stored[q], 16)
                with act.Fori(0, ALL_TILES // SLOTS) as i:
                    for q in range(SLOTS):
                        n = SLOTS * i + q
                        act.wait_ge(out_ready, n + 1 + SLOTS)
                        act.dma_start(x_out.rearrange("b (t p) d -> p (b t) d", p=P)[:, bass.ds(n, 1), :].rearrange("p a d -> p (a d)"), part[:, q, :]).then_inc(stored[q], 16)
                for q in range(SLOTS):
                    act.wait_ge(stored[q], 16 * (ALL_TILES // SLOTS + 1))

        @block.vector
        def _(dve):
            s = Steps(dve, dve_step)
            one = lambda i: (s.do(i), s.done())
            one(dve.memset(epst[:, :], EPS))
            one(dve.memset(one8[:, :], 1.0))
            if not gated:
                dve.wait_ge(bias_in, 16)
                for k in range(3):
                    one(dve.tensor_copy(b_parts[:, k, :], b_row[:, :]))
                    if k < 2:
                        one(dve.tensor_tensor(b_row[:, :], b_row[:, :], b_parts[:, k, :], ALU.subtract))
                dve.sem_inc(b_ready, 1)
            for q in range(4):
                part_q = range(q * QUARTER, (q + 1) * QUARTER)
                cols = slice(q * QUARTER, (q + 1) * QUARTER)
                dve.wait_ge(x_loaded[q], 16)
                for n in part_q:
                    s.do(dve.bn_stats(stats[:, n, :], xn_all[:, n, :]))
                s.done()
                for n in part_q:
                    s.do(dve.bn_aggr(mv[:, n, :], stats[:, n, :]))
                s.done()
                dve.sem_inc(var_ready, 1)
                dve.wait_ge(root_ready, q + 1)
                one(dve.reciprocal(rstd[:, cols], root[:, cols]))
                for n in part_q:
                    dve.tensor_scalar(xn_all[:, n, :], xn_all[:, n, :], mv[:, n, 0:1], rstd[:, n:n + 1],
                                      ALU.subtract, ALU.mult).then_inc(xn_ready, 1)
            dve.wait_ge(consts_in, 16 * N_CONST)
            one(dve.tensor_copy(before[:, :], misc[:, 0:P]))
            dve.wait_ge(logit_psum, ALL_TILES)
            in_bank = bH0[:, 0:ALL_TILES * EXPERTS].rearrange("p (t e) -> p t e", e=EXPERTS)
            if gated:
                one(dve.tensor_copy(logit[:, :, :], in_bank))
            else:
                one(dve.tensor_tensor(logit[:, :, :], in_bank, gbias[:, None, :].to_broadcast(te), ALU.add))
            wide = lambda a: a.rearrange("p (t a) -> p t a", a=1).to_broadcast(te)
            if gated:
                one(dve.tensor_reduce(small[:, :], logit[:, :, :], AX.X, ALU.max))
                one(dve.tensor_tensor(logit[:, :, :], logit[:, :, :], wide(small[:, :]), ALU.subtract))
            dve.sem_inc(exp_in, 1)
            dve.wait_ge(exp_ready, 1)
            if gated:
                one(dve.tensor_reduce(small[:, :], prob[:, :, :], AX.X, ALU.add))
                one(dve.reciprocal(small[:, :], small[:, :]))
                one(dve.tensor_tensor(prob[:, :, :], prob[:, :, :], wide(small[:, :]), ALU.mult))
            iota8 = misc[:, None, P:P + EXPERTS].to_broadcast(te)
            left = prob
            for k in range(TOPK):
                one(dve.tensor_reduce(weight[:, k, :], left[:, :, :], AX.X, ALU.max))
                one(dve.tensor_tensor(picked[:, :, :], left[:, :, :], wide(weight[:, k, :]), ALU.is_equal))
                one(dve.scalar_tensor_tensor(out=picked[:, :, :], in0=iota8, scalar=-float(EXPERTS), in1=picked[:, :, :], op0=ALU.add, op1=ALU.mult))
                one(dve.tensor_reduce(small[:, :], picked[:, :, :], AX.X, ALU.min))
                one(dve.scalar_tensor_tensor(out=hot[:, k, :, :], in0=iota8, scalar=-float(EXPERTS), in1=wide(small[:, :]), op0=ALU.add, op1=ALU.is_equal))
                if k == 0:
                    one(dve.scalar_tensor_tensor(out=top[:, :, :], in0=hot[:, 0, :, :], scalar=-2.0, in1=prob[:, :, :], op0=ALU.mult, op1=ALU.add))
                    left = top
            one(dve.tensor_tensor(both[:, :, :], hot[:, 0, :, :], hot[:, 1, :, :], ALU.add))
            one(dve.tensor_copy(both16[:, :, :], both[:, :, :]))
            dve.sem_inc(both_ready, 1)
            if not gated:
                one(dve.tensor_tensor(small[:, :], weight[:, 0, :], weight[:, 1, :], ALU.add))
                one(dve.tensor_scalar(small[:, :], small[:, :], 1e-6, None, ALU.add))
                one(dve.reciprocal(small[:, :], small[:, :]))
                for k in range(TOPK):
                    s.do(dve.tensor_tensor(weight[:, k, :], weight[:, k, :], small[:, :], ALU.mult))
                s.done()
            dve.wait_ge(rank_psum, 1)
            te_of = lambda bank: bank[:, 0:ALL_TILES * EXPERTS].rearrange("p (t e) -> p t e", e=EXPERTS)
            for e in range(EXPERTS):
                s.do(dve.tensor_tensor_scan(upto[:, :, e], one8[:, :], te_of(bU1)[:, :, e], 0.0, ALU.mult, ALU.add))
            s.done()
            one(dve.tensor_tensor(place[:, :, :], upto[:, :, :], te_of(bU1), ALU.subtract))
            one(dve.tensor_tensor(place[:, :, :], place[:, :, :], te_of(bU0), ALU.add))
            et = [P, EXPERTS, ALL_TILES]
            total = upto[:, ALL_TILES - 1, :].rearrange("p (e a) -> p e a", a=1).to_broadcast(et)
            mult128 = misc[:, None, P + EXPERTS:P + EXPERTS + ALL_TILES].to_broadcast(et)
            one(dve.tensor_tensor(over[:, :, :], total, mult128, ALU.is_gt))
            one(dve.tensor_reduce(nblk[:, :], over[:, :, :], AX.X, ALU.add))
            one(dve.tensor_tensor_scan(blk_end[:, :], one8[:, 0:EXPERTS], nblk[:, :], 0.0, ALU.mult, ALU.add))
            one(dve.tensor_tensor(blk_start[:, :], blk_end[:, :], nblk[:, :], ALU.subtract))
            one(dve.tensor_scalar(blk_start[:, :], blk_start[:, :], float(P), None, ALU.mult))
            one(dve.tensor_tensor(place[:, :, :], place[:, :, :], blk_start[:, None, :].to_broadcast(te), ALU.add))
            for k in range(TOPK):
                one(dve.tensor_tensor(picked[:, :, :], place[:, :, :], hot[:, k, :, :], ALU.mult))
                one(dve.tensor_reduce(posf[:, k, :], picked[:, :, :], AX.X, ALU.add))
            one(dve.tensor_copy(pos[:, :, :], posf[:, :, :]))
            if gated:
                one(dve.tensor_scalar(slot_int[:, :, :], pos[:, :, :], P - 1, None, ALU.bitwise_and))
                one(dve.tensor_copy(slot[:, :, :], slot_int[:, :, :]))
                one(dve.tensor_tensor(blk[:, :, :], posf[:, :, :], slot[:, :, :], ALU.subtract))
                one(dve.tensor_scalar(blk[:, :, :], blk[:, :, :], 1.0 / P, None, ALU.mult))
                iota_row = misc[:, P + EXPERTS + ALL_TILES:]
                for m in range(TOPK * ALL_TILES):
                    n, k = m // TOPK, m % TOPK
                    if m >= RING:
                        dve.wait_ge(marks_used, m - RING + 1)
                    s.do(dve.tensor_scalar(at_slot[:, m % RING, :], slots[:, 0:P], slot[:, k, n:n + 1], None, ALU.is_equal))
                    dve.tensor_scalar(in_block[:, m % RING, :], iota_row, blk[:, k, n:n + 1], slots[:, P + n:P + n + 1], ALU.is_equal, ALU.mult).then_inc(marks_ready, 1)
                dve.wait_ge(marks_used, TOPK * ALL_TILES)
                dve.tensor_copy(token[:, :], bY[:, 0:ROUTED]).then_inc(token_ready, 1)
            be = [P, ROUTED, EXPERTS]
            iota_b = misc[:, P + EXPERTS + ALL_TILES:].rearrange("p (j a) -> p j a", a=1).to_broadcast(be)
            one(dve.tensor_tensor(passed[:, :, :], blk_end[:, None, :].to_broadcast(be), iota_b, ALU.is_le))
            if SH:
                one(dve.memset(ownerf[:, :], 0.0))
            one(dve.tensor_reduce(ownerf[:, SH:LAST], passed[:, :, :], AX.X, ALU.add))
            one(dve.tensor_scalar(ownerf[:, SH:LAST], ownerf[:, SH:LAST], float(EXPERTS - 1), float(shared), ALU.min, ALU.add))
            one(dve.tensor_copy(owner[:, :], ownerf[:, :]))
            dve.sem_inc(routed, 2)

            def turned_low(t):
                j, n = t.j, t.n
                dve.wait_ge(xT_ready, j + 1)
                dve.tensor_tensor(xT_low[:, n % 2, :, :], bX[:, 0:DC * P].rearrange("p (c n) -> p c n", c=DC), xT[:, n % 2, :, :].bitcast(F32),
                                  ALU.subtract).then_inc(xT_low_ready, 1)

            def gate_hidden(t):
                j, n = t.j, t.n
                dve.wait_ge(a_ready, j + 1)
                if n >= 2:
                    dve.wait_ge(hT_psum, j - 1)
                dve.tensor_tensor(h[:, n % 2, :], act_out[:, n % 2, :], bU[n % 2][1][:, :], ALU.mult).then_inc(h_ready, 1)

            def turned_hidden(t):
                j, n = t.j, t.n
                dve.wait_ge(hT_psum, j + 1)
                if n >= 2:
                    dve.wait_ge(y_psum, j - 1)
                dve.tensor_copy(hT[:, n % 2, 4:8, :], bH1[:, :].rearrange("p (c n) -> p c n", c=4)).then_inc(hT_ready2, 1)

            def result(t):
                j, n = t.j, t.n
                dve.wait_ge(y_psum, j + 1)
                dve.wait_ge(yb_out[t.side], 16 * (t.pair + 1))
                dve.tensor_copy(yb[:, n % 2, :], bY[:, 0:D]).then_inc(yb_ready, 1)

            def dve_block(t):
                j, n = t.j, t.n
                if n == 0:
                    turned_low(t)
                if gated:
                    gate_hidden(t)
                if n + 1 < BLOCKS and in_parts(t.after()):
                    turned_low(t.after())
                if n:
                    result(t.before())
                if not gated:
                    turned_hidden(t)
            for_blocks(dve, runs[:2], dve_block)
            result(at(LAST - 1))

            def add_weighed(acc, out, q, k, n):
                return dve.scalar_tensor_tensor(out=out, in0=y_in[:, q, k, :], scalar=weight[:, k, bass.ds(n, 1)], in1=acc, op0=ALU.mult, op1=ALU.add)

            once = s.n
            if gated:
                dve.sem_inc(out_ready, SLOTS)
                with dve.Fori(0, ALL_TILES // SLOTS) as i:
                    s.base, s.n = once + i * SLOTS, 0
                    for q in range(SLOTS):
                        n = SLOTS * i + q
                        dve.wait_ge(gathered[q], 16 * TOPK * (i + 1))
                        dve.wait_ge(res_in[q], 16 * (i + 1))
                        dve.wait_ge(stored[q], 16 * (i + 1))
                        acc = x_res[:, q, :]
                        one(add_weighed(acc, acc, q, 0, n))
                        add_weighed(acc, part[:, q, :], q, 1, n).then_inc(out_ready, 1)
            else:
                def last_block(t):
                    i = t.j - LAST
                    s.base, s.n = once + i * 4, 0
                    if t.n + 1 < BLOCKS:
                        turned_low(t.after())
                    turned_hidden(t)
                    for q in range(2):
                        dve.wait_ge(gathered[q], 16 * TOPK * (i + 1))
                        dve.wait_ge(res_in[q], 16 * (2 - q) * (i + 1))
                        acc = x_res[:, q, :]
                        if q == 0:
                            one(dve.scalar_tensor_tensor(out=acc, in0=y_in[:, 0, TOPK, :], scalar=0.1, in1=acc, op0=ALU.mult, op1=ALU.add))
                        one(add_weighed(acc, acc, q, 0, q * SH + i))
                        if q == 0:
                            dve.wait_ge(stored[0], 16 * (i + 1))
                            add_weighed(acc, part[:, 0, :], 0, 1, i).then_inc(out_ready, 1)
                        else:
                            one(add_weighed(acc, acc, q, 1, SH + i))
                    dve.wait_ge(y_psum, t.j + 1)
                    dve.wait_ge(stored[1], 16 * (i + 1))
                    dve.scalar_tensor_tensor(out=part[:, 1, :], in0=bY[:, 0:D], scalar=0.1, in1=x_res[:, 1, :], op0=ALU.mult, op1=ALU.add).then_inc(yb_ready, 1)
                    dve.wait_ge(yb_ready, t.j + 1)
                    dve.sem_inc(out_ready, 1)
                for_blocks(dve, runs[2:], last_block)

        @block.tensor
        def _(pe):
            pe.wait_ge(consts_in, 16 * N_CONST)
            for t in range(ALL_TILES // 2 + 1):
                if t < ALL_TILES // 2:
                    pe.wait_ge(xn_ready, 2 * t + 2)
                    if t >= 2:
                        pe.wait_ge(gT_ready, t - 1)
                    for q in range(2):
                        for c in range(DC):
                            col = (q * DC + c) * P
                            i = pe.transpose(bU[t % 2][0][:, col:col + P], xn_all[:, 2 * t + q, c * P:(c + 1) * P], ident[:, :])
                    i.then_inc(gT_psum, 1)
                if t:
                    pe.wait_ge(gT_ready, t)
                    for q in range(2):
                        n = 2 * (t - 1) + q
                        for c in range(DC):
                            i = pe.matmul(bH0[:, n * EXPERTS:(n + 1) * EXPERTS], gT[:, (t - 1) % 2, q * DC + c, :], w_gate[:, c, :], start=(c == 0), stop=(c == DC - 1))
                        i.then_inc(logit_psum, 1)
            pe.wait_ge(both_ready, 1)
            pe.wait_ge(ready, 1 if gated else 2)
            flat = both16[:, :, :].rearrange("p t e -> p (t e)")
            pe.matmul(bU0[:, 0:ALL_TILES * EXPERTS], before[:, :], flat, start=True, stop=True)
            pe.matmul(bU1[:, 0:ALL_TILES * EXPERTS], ones[:, :], flat, start=True, stop=True).then_inc(rank_psum, 1)
            if gated:
                marks = TOPK * ALL_TILES
                for k in range(marks):
                    pe.wait_ge(marks_ready, k + 1)
                    pe.matmul(bY[:, 0:ROUTED], at_slot[:, k % RING, :], in_block[:, k % RING, :], start=(k == 0), stop=(k == marks - 1)).then_inc(marks_used, 1)
                pe.wait_ge(token_ready, 1)
            pe.wait_ge(w_in, 16 * 2 * LATE)
            pe.wait_ge(low_ready, SPLIT)
            pe.wait_ge(routed, 2)
            if not gated:
                pe.wait_ge(b_in, 16)

            def turn(t):
                j, n = t.j, t.n
                pe.wait_ge(xb_in[t.side], 16 * (t.pair + 1))
                if n:
                    if in_parts(t.before()):
                        pe.wait_ge(xT_low_ready, low_count(t.before()))
                    else:
                        pe.wait_ge(xT_ready, j)
                for c in range(DC):
                    i = pe.transpose(bX[:, c * P:(c + 1) * P], xb[:, n % 2, c * P:(c + 1) * P], ident[:, :])
                i.then_inc(xT_psum, 1)

            def owner_of(t):
                if not gated and in_parts(t):
                    return 0
                return pe.value_load(owner[0:1, bass.ds(t.j, 1)], min_val=shared, max_val=n_exp - 1)

            def of_expert(w, e, c, cols):
                if isinstance(e, int):
                    return w[:, e, cols] if c is None else w[:, e, c, cols]
                part = w[:, bass.ds(e, 1), cols] if c is None else w[:, bass.ds(e, 1), c, cols]
                return part.rearrange("p a n -> p (a n)")

            def up(t):
                j, n = t.j, t.n
                e = owner_of(t)
                if in_parts(t):
                    pe.wait_ge(xT_low_ready, low_count(t))
                else:
                    pe.wait_ge(xT_ready, j + 1)
                if n >= 2:
                    pe.wait_ge(h_ready if gated else a_ready, j - 1)
                for k in range(2):
                    out, cols = bU[n % 2][k][:, :], slice(k * 512, (k + 1) * 512)
                    for c in range(DC):
                        if in_parts(t):
                            x_high, w_high = xT[:, n % 2, c, :], of_expert(high, e, c, cols)
                            pe.matmul(out, x_high, w_high, start=(c == 0), stop=False)
                            pe.matmul(out, x_high, of_expert(w_up, e, c, cols).bitcast(F32R) if gated else low_shared[:, e, c, cols], start=False, stop=False)
                            i = pe.matmul(out, xT_low[:, n % 2, c, :], w_high, start=False, stop=(gated and c == DC - 1))
                        else:
                            pe.matmul(out, xT_whole[:, n % 2, c, :], of_expert(w_up, e - shared, c, cols), start=(c == 0), stop=False)
                    if not gated:
                        i = pe.matmul(out, ones[:, :], of_expert(b_table, e, None, cols), start=False, stop=True)
                i.then_inc(u_psum, 1)

            def turn_hidden(t):
                j, n = t.j, t.n
                pe.wait_ge(h_ready if gated else a_ready, j + 1)
                if n:
                    pe.wait_ge(hT_ready, j)
                    if not gated:
                        pe.wait_ge(hT_ready2, j)
                for c in range(hc):
                    i = pe.transpose((bH0, bH1)[c // 4][:, (c % 4) * P:(c % 4 + 1) * P], h[:, n % 2, c * P:(c + 1) * P], ident[:, :])
                i.then_inc(hT_psum, 1)

            def down(t, e):
                j, n = t.j, t.n
                pe.wait_ge(hT_ready, j + 1)
                if not gated:
                    pe.wait_ge(hT_ready2, j + 1)
                if n:
                    pe.wait_ge(yb_ready, j)
                for c in range(hc):
                    i = pe.matmul(bY[:, 0:D], hT[:, n % 2, c, :], of_expert(w_down, e, c, slice(0, D)), start=(c == 0), stop=(gated and c == hc - 1))
                if not gated:
                    i = pe.matmul(bY[:, 0:D], ones[:, :], of_expert(b_table, e, None, slice(UP, UP + D)), start=False, stop=True)
                i.then_inc(y_psum, 1)

            def pe_block(t):
                j, n = t.j, t.n
                if not gated and isinstance(j, int) and j == SH:
                    pe.wait_ge(late_in, 16 * 2 * (n_exp - LATE))
                up(t)
                if n:
                    e = owner_of(t.before())
                if n + 1 < BLOCKS:
                    turn(t.after())
                if n:
                    down(t.before(), e)
                turn_hidden(t)

            turn(at(0))
            for_blocks(pe, runs, pe_block)
            down(at(BLOCKS - 1), owner_of(at(BLOCKS - 1)))


def pos_slot(pos, k, n):
    return pos[:, k, n:n + 1]


class Turn:

    def __init__(self, pair, side, n, run=None):
        self.pair, self.side, self.n, self.run = pair, side, n, run
        self.j = 2 * pair + side

    def before(self):
        return Turn(self.pair - 1 if self.side == 0 else self.pair, 1 - self.side, self.n - 1, self.run)

    def after(self):
        return Turn(self.pair + 1 if self.side == 1 else self.pair, 1 - self.side, self.n + 1, self.run)


def at(j):
    return Turn(j // 2, j % 2, j)


def for_blocks(engine, runs, step):
    for number, first, end in runs:
        step(at(first))
        step(at(first + 1))
        with engine.Fori(first // 2 + 1, end // 2 - 1) as pair:
            for side in range(2):
                step(Turn(pair, side, 2 + side, number))
        step(at(end - 2))
        step(at(end - 1))


HEADS, DH = 16, 16
GH = 4
GROUPS = HEADS // GH
TERMS = 6
KEY_ROWS = TERMS * DH
Q_PART = (0, 0, 0, 1, 1, 2)
K_PART = (0, 1, 2, 0, 1, 0)
POOL_STEPS = (TILES * 6 + GROUPS * 6,) * 2
DVE_STEPS = (GROUPS * 14, GROUPS * 14 + TILES)


UNITS = 3 * TILES // 2 * GH
HALF = 4


def query_units():
    return [(h, i, c * 512, min((i + 1) * P, (c + 1) * 512)) for h in range(GH) for i in range(TILES) for c in range(i // HALF + 1)]


def key_units(j):
    return [(h, max(j * P, c * 512), (c + 1) * 512) for h in range(GH) for c in range(j // HALF, 2)]


SLOTS = 8
QUERIES_AT = (0, 5, 8, 11, 12, 12, 0, 0)
WEIGH_AT = {2: (4, 7), 1: (6,)}
ROWS_AT = (3, 3, 0, 0)
SPLIT_AT = ((1, 2, 2, 3, 4),) * 2 + ((3, 3, 4, 4, 5), (1, 2, 2, 3, 4))


def key_slot(j, slot):
    n = len(key_units(j))
    return (slot * n // SLOTS,) if slot * n % SLOTS == 0 else ()


def query_slot(j, slot):
    before, n = sum(QUERIES_AT[:j]), QUERIES_AT[j]
    return range(before + n * slot // SLOTS, before + n * (slot + 1) // SLOTS)


def beside(extras, slot):
    n = len(extras)
    return extras[n * slot // SLOTS:n * (slot + 1) // SLOTS]


def units_before(j):
    return sum(len(key_units(k)) for k in range(j))


class Plan:

    def __init__(self, first, last, start=0, later=0):
        self.start, self.later, self.uses, self.extras = start, later, [], {}
        for hg in range(GROUPS):
            follows = not (last and hg == GROUPS - 1)
            steps = [[] for _ in range(TILES)]
            if follows:
                for h in range(GH):
                    steps[h] += [("terms", hg, h, side) for side in range(2)]
            if not (first and hg == 0):
                steps[1] += [("out", hg, c) for c in range(2)]
            if not last:
                tiles = (range(0, 3), range(3, 6), range(6, 8), ())[hg]
                for k, t in enumerate(tiles):
                    at_step = ROWS_AT[hg] + k
                    steps[at_step] += [("rows", t)]
                    steps[at_step + 1] = [("keys", t), ("values", t)] + steps[at_step + 1]
            if hg == 0 and not first:
                for t in range(TILES):
                    steps[2 + t // 2] += [("acts", t)]
                for t in range(TILES):
                    at_step = 3 + t // 2
                    steps[at_step].insert(t % 2, ("sum", t))
            self.extras[hg] = steps
            for step in steps:
                self.uses += step
            if follows:
                self.uses.append(("tops", hg))
        self.place = {key: k for k, key in enumerate(self.uses)}

    def spot(self, key):
        k = self.start + self.place[key]
        return k % 2, self.later + k // 2


class Opening(Plan):

    def __init__(self):
        self.start, self.later = 0, 0
        self.uses = [(kind, t) for t in range(TILES) for kind in ("rows", "keys", "values")]
        self.uses += [("terms", -1, h, side) for h in range(GH) for side in range(2)] + [("tops", -1)]
        self.place = {key: k for k, key in enumerate(self.uses)}


def causal_attention(nc, io, x_in, x_out):
    with ExitStack() as stack:
        m = Memory(nc, stack, "ca")
        sb, sem = m.sb, m.sem
        x = sb("x", [P, ALL_TILES, D])
        w_kqv = sb("w_kqv", [P, DC, 3 * D])
        w_o = sb("w_o", [P, DC, D])
        ident = sb("ident", [P, P])
        ident16 = sb("ident16", [P, P], BF16)
        mask = sb("mask", [P, P])
        mask16 = sb("mask16", [P, P], BF16)
        rope = sb("rope", [P, 2, TILES, DH // 2])
        stats = sb("stats", [P, ALL_TILES, 6])
        mv = sb("mv", [P, ALL_TILES, 2])
        root = sb("root", [P, ALL_TILES])
        rstd = sb("rstd", [P, ALL_TILES])
        epst = sb("epst", [P, 1])
        xn = sb("xn", [P, 2, D])
        xT = sb("xT", [P, 2, DC, P])
        raw = sb("raw", [P, 2, 2 * D])
        scratch = sb("scratch", [P, 4 * D])
        left = scratch[:, :].rearrange("p (s t n) -> p s t n", t=TILES, s=2)
        kq = sb("kq", [P, 2, TILES, 2, D])
        v_all = sb("v_all", [P, 2, TILES, D])
        vg = sb("vg", [P, TILES, GH, 2 * DH])
        parts = sb("parts", [P, 3, 2, TILES, GH * DH], BF16)
        terms = sb("terms", [P, 2, TILES, GH, KEY_ROWS], BF16)
        kT = sb("kT", [P, 2, GH, SEQ], BF16)
        qT = sb("qT", [P, 2, GH, SEQ], BF16)
        top = sb("top", [P, 2, GH, TILES])
        topl = sb("topl", [P, 2, TILES, GH])
        top3 = sb("top3", [P, TILES, GH, 32], BF16)
        probs = sb("probs", [P, 2, GH, SEQ])
        oT = sb("oT", [P, SEQ])
        rden = sb("rden", [P, TILES, GH])
        acts = sb("acts", [P, TILES, D])
        aT = sb("aT", [P, 2, DC, P])

        O = stack.enter_context(nc.psum_tensor("ca_wide", [P, 1024], F32))
        banks = m.banks(6)
        key_banks, query_banks, narrow = banks[0:2], banks[2:4], banks[4:6]

        consts_in = sem("consts_in")
        x_loaded = [sem(f"x_loaded{b}") for b in range(BATCH)]
        ready, zeroed, dve_step, pool_step = sem("ready"), sem("zeroed"), sem("dve_step"), sem("pool_step")
        var_ready, root_ready, xn_ready = sem("var_ready"), sem("root_ready"), sem("xn_ready")
        full, read = [sem("full0"), sem("full1")], [sem("read0"), sem("read1")]
        roped, parts_ready, terms_ready, vg_ready = [sem("roped0"), sem("roped1")], sem("parts_ready"), sem("terms_ready"), sem("vg_ready")
        s1_psum, top_ready = sem("s1_psum"), sem("top_ready")
        s2_psum, exp_ready, cut_ready, pv_done = sem("s2_psum"), sem("exp_ready"), sem("cut_ready"), sem("pv_done")
        oT_ready, rden_ready = sem("oT_ready"), sem("rden_ready")
        x_done, stored, values_in = sem("x_done"), sem("stored"), sem("values_in")
        closing, closing_read, closing_turned, closing_aT, closing_y = [sem(f"closing{k}") for k in range(5)]
        waited = sem("waited")
        N_CONST = 5
        SCALE = DH ** -0.5

        opening = Opening()
        first_plan = Plan(True, False, len(opening.uses))
        middle = len(opening.uses) + len(first_plan.uses)
        MIDDLE_USES = len(Plan(False, False).uses)
        assert MIDDLE_USES % 2 == 0

        def last_plan_uses():
            n = middle + (BATCH - 2) * MIDDLE_USES + len(Plan(False, True).uses)
            return (n + 1) // 2, n // 2

        def wait(engine, semaphore, value):
            if isinstance(value, int):
                if value > 0:
                    engine.wait_ge(semaphore, value)
            else:
                engine.wait_ge(semaphore, value)
                if engine is nc.gpsimd:
                    engine.sem_inc(waited, 1)

        def turns(engine, turn_of, steps_of, steps=None):
            start = steps.n if steps else 0

            def based(b, base):
                if steps:
                    steps.base, steps.n = base, 0
                return b

            turn_of(based(0, start), 0, 1, first_plan)
            start += steps_of[0] if steps else 0
            assert not steps or steps.n == steps_of[0], (steps.n, steps_of)
            engine.sem_inc(waited, 1)
            with engine.Fori(1, BATCH - 1) as b:
                turn_of(based(b, start + (b - 1) * (steps_of[1] if steps else 0)), 2 - b, b - 1, Plan(False, False, middle, (b - 1) * (MIDDLE_USES // 2)))
                assert not steps or steps.n == steps_of[1], (steps.n, steps_of)
                engine.sem_inc(waited, 1)
            start += (BATCH - 2) * (steps_of[1] if steps else 0)
            turn_of(based(BATCH - 1, start), 1, 0, Plan(False, True, middle + (BATCH - 2) * MIDDLE_USES))

        def filled(engine, plan, key):
            bank, before = plan.spot(key)
            wait(engine, full[bank], before + 1)
            return narrow[bank], read[bank]

        def query_bank(g, u):
            first = isinstance(g, int) and g == 0
            return (query_banks + key_banks)[u % 4] if first else query_banks[u % 2]

        def settle(s):
            wait(s.engine, s.semaphore, s.base + s.n)

        def turn_pairs(s, t, where, plan, scratch=scratch):
            engine = s.engine
            bank, before = plan.spot(("keys", t))
            wait(engine, read[bank], before + 1)
            half = 2 * HEADS
            pairs = raw[:, t % 2, :].rearrange("p (h f a) -> p h f a", f=DH // 2, a=2)
            even, odd = pairs[:, :, :, 0], pairs[:, :, :, 1]
            cos = rope[:, 0, t, None, :].to_broadcast([P, half, DH // 2])
            sin = rope[:, 1, t, None, :].to_broadcast([P, half, DH // 2])
            tmp = [scratch[:, k * D:(k + 1) * D].rearrange("p (h f) -> p h f", f=DH // 2) for k in range(4)]
            for k, (a, w) in enumerate(((even, cos), (odd, sin), (even, sin), (odd, cos))):
                s.do(engine.tensor_tensor(tmp[k], a, w, ALU.mult))
            settle(s)
            out = kq[:, where, t, :, :].rearrange("p s (h a f) -> p (s h) a f", a=2, f=DH // 2) if isinstance(where, int) else \
                kq[:, bass.ds(where, 1), t, :, :].rearrange("p w s (h a f) -> p (w s h) a f", a=2, f=DH // 2)
            s.do(engine.tensor_tensor(out[:, :, 0, :], tmp[0], tmp[1], ALU.subtract))
            s.do(engine.tensor_tensor(out[:, :, 1, :], tmp[2], tmp[3], ALU.add))
            settle(s)
            engine.sem_inc(roped[t % 2], 1)

        def split(s, hg, where, before, k):
            engine = s.engine
            lo, hi = hg * GH * DH, (hg + 1) * GH * DH
            src = kq[:, where, :, :, lo:hi].rearrange("p t s n -> p s t n") if isinstance(where, int) else \
                kq[:, bass.ds(where, 1), :, :, lo:hi].rearrange("p w t s n -> p s (w t) n")
            if k == 0:
                wait(engine, terms_ready, before)
            rest = src if k < 2 else left[:, :, :, :]
            if k % 2 == 0:
                s.do(engine.tensor_copy(parts[:, k // 2, :, :, :], rest))
            else:
                s.do(engine.tensor_tensor(left[:, :, :, :], rest, parts[:, k // 2, :, :, :], ALU.subtract))
            settle(s)
            if k == 4:
                engine.sem_inc(parts_ready, 1)

        block = stack.enter_context(nc.Block())

        @block.sync
        def _(sp):
            for b in range(BATCH):
                if b == 1:
                    sp.wait_ge(x_loaded[0], 16)
                    sp.wait_ge(consts_in, 16 * N_CONST)
                sp.dma_start(x[:, b * TILES:(b + 1) * TILES, :], x_in[b].rearrange("(t p) d -> p t d", p=P)).then_inc(x_loaded[b], 16)
            with sp.Fori(0, BATCH) as b:
                sp.wait_ge(x_done, (b + 1) * TILES)
                sp.dma_start(x_out[b].rearrange("(t p) d -> p t d", p=P), x[:, bass.ds(b * TILES, TILES), :]).then_inc(stored, 16)
            sp.wait_ge(stored, 16 * BATCH)

        @block.gpsimd
        def _(pool):
            s = Steps(pool, pool_step)

            def one(instruction):
                s.do(instruction)
                wait(pool, pool_step, s.base + s.n)

            one(pool.memset(vg[:, :, :, :], 0.0))
            one(pool.memset(vg[:, :, :, DH:DH + 1], 1.0))
            one(pool.memset(top3[:, :, :, :], 0.0))
            one(pool.memset(kT[KEY_ROWS:KEY_ROWS + 3, :, :, :], 1.0))
            pool.memset(top[:, :, :, :], -3e38).then_inc(zeroed, 1)
            pool.wait_ge(consts_in, 16 * N_CONST)

            for t in range(1, TILES, 2):
                turn_pairs(s, t, 0, opening, probs[:, 0, 0, :])
            for k in range(5):
                split(s, 1, 0, 1, k)

            def copy_values(b, hg, cur):
                wait(pool, pv_done, (b * GROUPS + hg) * TILES)
                if hg == 0:
                    wait(pool, values_in, b + 1)
                lo, hi = hg * GH * DH, (hg + 1) * GH * DH
                src = v_all[:, cur, :, lo:hi] if isinstance(cur, int) else v_all[:, bass.ds(cur, 1), :, lo:hi].rearrange("p w t n -> p (w t) n")
                one(pool.tensor_copy(vg[:, :, :, 0:DH], src.rearrange("p t (h d) -> p t h d", d=DH)))
                pool.sem_inc(vg_ready, 1)

            def pool_turn(b, cur, nxt, plan):
                last = isinstance(b, int) and b == BATCH - 1
                for hg in range(GROUPS):
                    g = b * GROUPS + hg
                    for j in range(TILES):
                        u = g * UNITS + units_before(j)
                        for k, (h, a, e) in enumerate(key_units(j)):
                            if a == j * P:
                                wait(pool, exp_ready, u + k + 1)
                                on = probs[:, j % 2, h, a:a + P]
                                pool.affine_select(out=on, in_=on, compare_op=ALU.is_ge, fill=0.0, base=0,
                                                   pattern=[[1, P]], channel_multiplier=-1).then_inc(cut_ready, 1)
                        if j == 0:
                            copy_values(b, hg, cur)
                        if not (last and hg >= GROUPS - 2):
                            for k in range(5):
                                if SPLIT_AT[hg][k] == j:
                                    split(s, (hg + 2) % GROUPS, cur if hg < 2 else nxt, g + 2, k)
                        for key in plan.extras[hg][j]:
                            if key[0] == "keys":
                                turn_pairs(s, key[1], nxt, plan)

            turns(pool, pool_turn, POOL_STEPS, s)

        @block.scalar
        def _(act):
            for dst, src in ((w_kqv[:, :, :], io["ca_w"]), (w_o[:, :, :], io["ca_wo"]), (ident[:, :], io["ident"]),
                             (mask[:, :], io["ca_mask"]), (rope[:, :, :, :], io["ca_rope"])):
                act.dma_start(dst, src).then_inc(consts_in, 16)

            def deviations(k):
                act.wait_ge(var_ready, k + 1)
                cols = slice(0, TILES) if k == 0 else slice(TILES, ALL_TILES)
                act.activation(root[:, cols], mv[:, cols, 1], ACT.Sqrt, bias=epst[:, 0:1]).then_inc(root_ready, 1)

            deviations(0)

            def copy(dst, src, signal):
                return act.activation(dst, src, ACT.Identity).then_inc(signal, 1)

            def extra(plan, key, b, where, par):
                if key[0] == "rows":
                    bank, sig = filled(act, plan, key)
                    copy(xT[:, key[1] % 2, :, :], bank[:, 0:D].rearrange("p (c n) -> p c n", c=DC), sig)
                elif key[0] == "keys":
                    t = key[1]
                    wait(act, roped[t % 2], (b + 1) * (TILES // 2) + t // 2)
                    bank, sig = filled(act, plan, key)
                    copy(raw[:, t % 2, :], bank[:, :], sig)
                elif key[0] == "values":
                    bank, sig = filled(act, plan, key)
                    t = key[1]
                    dst = v_all[:, where, t, :] if isinstance(where, int) else v_all[:, bass.ds(where, 1), t, :].rearrange("p w n -> p (w n)")
                    if t == 0:
                        wait(act, vg_ready, b * GROUPS)
                    copy(dst, bank[:, 0:D], sig)
                    if t == TILES - 1:
                        wait(act, sig, plan.spot(key)[1] + 1)
                        act.sem_inc(values_in, 1)
                elif key[0] == "terms" and key[2] > 0:
                    _, _, h, side = key
                    bank, sig = filled(act, plan, key)
                    copy((kT, qT)[side][0:KEY_ROWS, par, h, :], bank[0:KEY_ROWS, :].bitcast(BF16), sig)
                elif key[0] == "acts":
                    bank, sig = filled(act, plan, key)
                    copy(aT[:, key[1] % 2, :, :], bank[:, 0:D].rearrange("p (c n) -> p c n", c=DC), sig)

            for key in opening.uses[:3 * TILES]:
                extra(opening, key, -1, 0, 0)
            deviations(1)
            for key in opening.uses[3 * TILES:]:
                extra(opening, key, -1, 0, 0)

            def act_turn(b, cur, nxt, plan):
                for hg in range(GROUPS):
                    g = b * GROUPS + hg
                    for j in range(TILES):
                        wait(act, pv_done, g * TILES + j - 1)
                        for slot in range(SLOTS):
                            for k in key_slot(j, slot):
                                h, a, e = key_units(j)[k]
                                u = units_before(j) + k
                                wait(act, s2_psum, g * UNITS + u + 1)
                                act.activation(probs[:, j % 2, h, a:e], key_banks[u % 2][:, a % 512:(e - 1) % 512 + 1], ACT.Exp, scale=SCALE).then_inc(exp_ready, 1)
                            if j == 0 and slot in (5, 7) and ("out", hg, 0) in plan.place:
                                copy_sums(g - 1, slot // 7)
                            for key in beside(plan.extras[hg][j], slot):
                                extra(plan, key, b, nxt, (hg + 1) % 2)

            def copy_sums(g, c):
                wait(act, pv_done, (g + 1) * TILES)
                copy(oT[:, c * 512:(c + 1) * 512], O[:, c * 512:(c + 1) * 512], oT_ready)

            turns(act, act_turn, None)
            for c in range(2):
                copy_sums(BATCH * GROUPS - 1, c)
            for t in range(TILES):
                act.wait_ge(closing_turned, t + 1)
                if t >= 2:
                    act.wait_ge(closing_y, t - 1)
                copy(aT[:, t % 2, :, :], narrow[t % 2][:, 0:D].rearrange("p (c n) -> p c n", c=DC), closing_aT)

        @block.vector
        def _(dve):
            s = Steps(dve, dve_step)
            one = lambda i: (s.do(i), s.done())
            one(dve.memset(epst[:, :], EPS))

            def row_stats(tiles):
                for n in tiles:
                    s.do(dve.bn_stats(stats[:, n, :], x[:, n, :]))
                s.done()
                for n in tiles:
                    s.do(dve.bn_aggr(mv[:, n, :], stats[:, n, :]))

            dve.wait_ge(x_loaded[0], 16)
            row_stats(range(TILES))
            s.done()
            dve.sem_inc(var_ready, 1)
            dve.wait_ge(consts_in, 16 * N_CONST)
            s.do(dve.tensor_copy(ident16[:, :], ident[:, :]))
            one(dve.tensor_copy(mask16[:, :], mask[:, :]))
            dve.wait_ge(root_ready, 1)
            one(dve.reciprocal(rstd[:, 0:TILES], root[:, 0:TILES]))
            dve.sem_inc(ready, 1)

            def normalise(plan, b, t):
                if t >= 2:
                    filled(dve, plan, ("rows", t - 2))
                n = b * TILES + t
                if isinstance(n, int):
                    src, mean, r = x[:, n, :], mv[:, n, 0:1], rstd[:, n:n + 1]
                else:
                    src, mean, r = x[:, bass.ds(n, 1), :].rearrange("p a d -> p (a d)"), mv[:, bass.ds(n, 1), 0], rstd[:, bass.ds(n, 1)]
                dve.tensor_scalar(xn[:, t % 2, :], src, mean, r, ALU.subtract, ALU.mult).then_inc(xn_ready, 1)

            def place_terms(plan, key, count, side):
                wait(dve, parts_ready, count)
                if key:
                    filled(dve, plan, key)
                to = lambda lo, hi, step: terms[:, side, :, :, :].rearrange("p t h n -> p (t h) n").rearrange("p m (r d) -> p m r d", d=DH)[:, :, lo:hi:step, :]
                of = lambda k, n: parts[:, k, side, :, :].rearrange("p t n -> p (t n)").rearrange("p (m a d) -> p m a d", a=1, d=DH).to_broadcast([P, TILES * GH, n, DH])
                where = (((0, 0, 4, 3), (0, 5, 6, 1), (1, 1, 5, 3), (2, 2, 3, 1)), ((0, 0, 3, 1), (1, 3, 5, 1), (2, 5, 6, 1)))
                for k, lo, hi, step in where[side]:
                    s.do(dve.tensor_copy(to(lo, hi, step), of(k, len(range(lo, hi, step)))))
                if side == 0:
                    s.done()
                    dve.sem_inc(terms_ready, 1)

            def maxima(g, units):
                for u in units:
                    h, i, a, e = query_units()[u]
                    wait(dve, s1_psum, g * UNITS + u + 1)
                    dve.tensor_reduce(top[:, a // 512, h, i:i + 1], query_bank(g, u)[:, 0:e - a], AX.X, ALU.max).then_inc(top_ready, 1)

            def part_tops(g):
                wait(dve, top_ready, g * (UNITS + 1) + UNITS)
                by_tile = top[:, :, :, :].rearrange("p c h t -> p c t h")
                one(dve.tensor_tensor(topl[:, 1, :, :], by_tile[:, 0, :, :], by_tile[:, 1, :, :], ALU.max))
                one(dve.tensor_scalar(topl[:, 0, :, :], topl[:, 1, :, :], -1.0, None, ALU.mult))
                for k in range(3):
                    one(dve.tensor_copy(top3[:, :, :, k], topl[:, k % 2, :, :]))
                    if k < 2:
                        one(dve.tensor_tensor(topl[:, (k + 1) % 2, :, :], topl[:, k % 2, :, :], top3[:, :, :, k], ALU.subtract))
                dve.sem_inc(top_ready, 1)

            def hand_tops(plan, key, par):
                bank, sig = filled(dve, plan, key)
                for h in range(GH):
                    i = dve.tensor_copy(qT[KEY_ROWS:KEY_ROWS + 3, par, h, :], bank[32 * h:32 * h + 3, :].bitcast(BF16))
                i.then_inc(sig, 1)

            def average(bank, sig, hg, c, count):
                half = slice(c * HALF, (c + 1) * HALF)
                o = bank[:, :].rearrange("p (t h d) -> p t h d", h=GH, d=2 * DH)
                dve.reciprocal(rden[:, half, :], o[:, :, :, DH]).then_inc(rden_ready, 1)
                wait(dve, rden_ready, count)
                out = acts[:, half, hg * GH * DH:(hg + 1) * GH * DH].rearrange("p t (h d) -> p t h d", d=DH)
                dve.tensor_tensor(out, o[:, :, :, 0:DH], rden[:, half, :].rearrange("p t (h a) -> p t h a", a=1).to_broadcast([P, HALF, GH, DH]),
                                  ALU.mult).then_inc(sig, 1)

            def copy_terms(plan, key, par):
                bank, sig = filled(dve, plan, key)
                dve.tensor_copy((kT, qT)[key[3]][0:KEY_ROWS, par, 0, :], bank[0:KEY_ROWS, :].bitcast(BF16)).then_inc(sig, 1)

            normalise(opening, 0, 0)
            normalise(opening, 0, 1)
            others = ALL_TILES - TILES
            for t in range(TILES):
                if t + 2 < TILES:
                    normalise(opening, 0, t + 2)
                if t % 2 == 0:
                    turn_pairs(s, t, 0, opening)
                mine = range(TILES + others * t // TILES, TILES + others * (t + 1) // TILES)
                for n in mine:
                    if n % TILES == 0:
                        dve.wait_ge(x_loaded[n // TILES], 16)
                row_stats(mine)
            s.done()
            dve.sem_inc(var_ready, 1)
            dve.wait_ge(roped[1], TILES // 2)
            for k in range(5):
                split(s, 0, 0, 0, k)
            for side in (1, 0):
                place_terms(opening, None, 1, side)
            for side in range(2):
                copy_terms(opening, ("terms", -1, 0, side), 0)
            dve.wait_ge(root_ready, 2)
            one(dve.reciprocal(rstd[:, TILES:ALL_TILES], root[:, TILES:ALL_TILES]))
            dve.wait_ge(zeroed, 1)
            maxima(0, range(UNITS))
            part_tops(0)
            hand_tops(opening, ("tops", -1), 0)
            for side in (1, 0):
                place_terms(opening, ("terms", -1, GH - 1, 1), 2, side)

            def dve_turn(b, cur, nxt, plan):
                last = isinstance(b, int) and b == BATCH - 1
                for hg in range(GROUPS):
                    g = b * GROUPS + hg
                    tiles = [key[1] for j in range(TILES) for key in plan.extras[hg][j] if key[0] == "rows"]
                    for t in tiles[:2]:
                        normalise(plan, b + 1, t)
                    follows, placed = ("tops", hg) in plan.place, not (last and hg >= GROUPS - 2)
                    for j in range(TILES):
                        for slot in range(SLOTS):
                            if follows:
                                maxima(g + 1, query_slot(j, slot))
                            for key in beside(plan.extras[hg][j], slot):
                                if key[0] == "out":
                                    average(*filled(dve, plan, key), (hg - 1) % GROUPS, key[2], 2 * (g - 1) + key[2] + 1)
                                elif key[0] == "rows" and len(tiles) > 2 and key[1] == tiles[0]:
                                    normalise(plan, b + 1, tiles[2])
                                elif key[0] == "terms" and key[2] == 0:
                                    copy_terms(plan, key, (hg + 1) % 2)
                                elif key[0] == "sum":
                                    bank, sig = filled(dve, plan, key)
                                    n = (b - 1) * TILES + key[1]
                                    xs = x[:, n, :] if isinstance(n, int) else x[:, bass.ds(n, 1), :].rearrange("p a d -> p (a d)")
                                    one(dve.tensor_tensor(xs, xs, bank[:, 0:D], ALU.add))
                                    dve.sem_inc(sig, 1)
                                    dve.sem_inc(x_done, 1)
                        if j == TILES - 3 and follows:
                            part_tops(g + 1)
                            if placed:
                                place_terms(plan, ("terms", hg, GH - 1, 1), g + 3, 1)
                        if j == TILES - 2 and follows:
                            hand_tops(plan, ("tops", hg), (hg + 1) % 2)
                            if placed:
                                place_terms(plan, ("terms", hg, GH - 1, 1), g + 3, 0)

            turns(dve, dve_turn, DVE_STEPS, s)
            for c in range(2):
                dve.wait_ge(closing, c + 1)
                average(narrow[c], closing_read, GROUPS - 1, c, 2 * (BATCH * GROUPS - 1) + c + 1)
            for t in range(TILES):
                dve.wait_ge(closing_y, t + 1)
                xs = x[:, (BATCH - 1) * TILES + t, :]
                dve.tensor_tensor(xs, xs, query_banks[t % 2][:, 0:D], ALU.add).then_inc(x_done, 1)

        @block.tensor
        def _(pe):
            pe.wait_ge(ready, 1)

            def fill(plan, key):
                bank, before = plan.spot(key)
                wait(pe, read[bank], before)
                return narrow[bank], full[bank]

            def was_read(plan, key):
                bank, before = plan.spot(key)
                wait(pe, read[bank], before + 1)

            def turn_four(dst, src, n, signal):
                for c in range(n):
                    i = pe.transpose(dst[:, c * P:(c + 1) * P], src(c), ident[:, :])
                i.then_inc(signal, 1)

            def extra(plan, key, b, par):
                if key[0] == "rows":
                    t = key[1]
                    wait(pe, xn_ready, (b + 1) * TILES + t + 1)
                    bank, sig = fill(plan, key)
                    turn_four(bank, lambda c: xn[:, t % 2, c * P:(c + 1) * P], DC, sig)
                elif key[0] in ("keys", "values"):
                    t = key[1]
                    was_read(plan, ("rows", t))
                    bank, sig = fill(plan, key)
                    lo, hi = (0, 2 * D) if key[0] == "keys" else (2 * D, 3 * D)
                    for c in range(DC):
                        i = pe.matmul(bank[:, 0:hi - lo], xT[:, t % 2, c, :], w_kqv[:, c, lo:hi], start=(c == 0), stop=(c == DC - 1))
                    i.then_inc(sig, 1)
                elif key[0] == "terms":
                    _, hg, h, side = key
                    if h == 0 and side == 0:
                        wait(pe, terms_ready, b * GROUPS + hg + 2)
                    bank, sig = fill(plan, key)
                    for t in range(TILES):
                        i = pe.transpose(bank[0:KEY_ROWS, :].bitcast(BF16)[:, t * P:(t + 1) * P], terms[:, side, t, h, :], ident16[:, :])
                    i.then_inc(sig, 1)
                elif key[0] == "out":
                    c = key[2]
                    wait(pe, oT_ready, 2 * (b * GROUPS + key[1] - 1) + c + 1)
                    bank, sig = fill(plan, key)
                    turn_four(bank, lambda k: oT[:, (4 * c + k) * P:(4 * c + k + 1) * P], 4, sig)
                elif key[0] == "acts":
                    t = key[1]
                    if t == 0:
                        for c in range(2):
                            was_read(plan, ("out", 0, c))
                    bank, sig = fill(plan, key)
                    turn_four(bank, lambda c: acts[:, t, c * P:(c + 1) * P], DC, sig)
                elif key[0] == "sum":
                    t = key[1]
                    was_read(plan, ("acts", t))
                    bank, sig = fill(plan, key)
                    for c in range(DC):
                        i = pe.matmul(bank[:, 0:D], aT[:, t % 2, c, :], w_o[:, c, :], start=(c == 0), stop=(c == DC - 1))
                    i.then_inc(sig, 1)

            def query_score(g, u, par, plan, hg):
                h, i, a, e = query_units()[u]
                if i == 0:
                    for side in range(2):
                        was_read(plan, ("terms", hg, h, side))
                first = isinstance(g, int) and g == 0
                wait(pe, top_ready, u - 3 if first else g * (UNITS + 1) + u - 1)
                on_diagonal = e == (i + 1) * P
                out = query_bank(g, u)
                last = pe.matmul(out[:, 0:e - a], qT[0:KEY_ROWS, par, h, i * P:(i + 1) * P], kT[0:KEY_ROWS, par, h, a:e], start=True, stop=not on_diagonal)
                if on_diagonal:
                    last = pe.matmul(out[:, e - a - P:e - a], ident16[:, :], mask16[:, :], start=False, stop=True)
                last.then_inc(s1_psum, 1)

            def turn_tops(plan, key, g):
                wait(pe, top_ready, (g + 1) * (UNITS + 1))
                bank, sig = fill(plan, key)
                for t in range(TILES):
                    i = pe.transpose(bank[:, :].bitcast(BF16)[:, t * P:(t + 1) * P], top3[:, t, :, :].rearrange("p h k -> p (h k)"), ident16[:, :])
                i.then_inc(sig, 1)

            def key_score(g, j, k, par):
                h, a, e = key_units(j)[k]
                u = units_before(j) + k
                wait(pe, exp_ready, g * UNITS + u - 1)
                pe.matmul(key_banks[u % 2][:, a % 512:(e - 1) % 512 + 1], kT[0:KEY_ROWS + 3, par, h, j * P:(j + 1) * P],
                          qT[0:KEY_ROWS + 3, par, h, a:e], start=True, stop=True).then_inc(s2_psum, 1)

            def weigh(g, j, n):
                c = j // HALF + n
                if n == 0:
                    wait(pe, cut_ready, (g * TILES + j + 1) * GH)
                    wait(pe, exp_ready, g * UNITS + units_before(j + 1))
                    if j == 0:
                        wait(pe, vg_ready, g + 1)
                        wait(pe, oT_ready, 2 * g)
                lo, hi = max(j * P, c * 512), (c + 1) * 512
                for h in range(GH):
                    i = pe.matmul(O[32 * h:32 * h + 32, lo:hi], vg[:, j, h, :], probs[:, j % 2, h, lo:hi],
                                  start=(j == 0), stop=(hi == (j + 1) * P), tile_position=(0, 32 * h))
                if c == 1:
                    i.then_inc(pv_done, 1)

            for key in opening.uses[:3 * TILES]:
                extra(opening, key, -1, 0)
            for key in opening.uses[3 * TILES:-1]:
                extra(opening, key, 0, 0)
            for u in range(UNITS):
                query_score(0, u, 0, opening, -1)
            turn_tops(opening, ("tops", -1), 0)

            def pe_turn(b, cur, nxt, plan):
                for hg in range(GROUPS):
                    g = b * GROUPS + hg
                    par = hg % 2
                    follows = ("tops", hg) in plan.place
                    if hg:
                        was_read(plan, ("tops", hg - 1))
                    elif isinstance(b, int) and b == 0:
                        was_read(opening, ("tops", -1))
                    else:
                        tops_of_last(b)
                    for j in range(TILES):
                        for slot in range(SLOTS):
                            for k in key_slot(j, slot):
                                key_score(g, j, k, par)
                            if follows:
                                for u in query_slot(j, slot):
                                    query_score(g + 1, u, 1 - par, plan, hg)
                            for key in beside(plan.extras[hg][j], slot):
                                extra(plan, key, b, 1 - par)
                            if j == 0 and slot == 3 and ("out", hg, 0) in plan.place:
                                weigh(g - 1, TILES - 1, 0)
                            if j and slot in WEIGH_AT[2 - (j - 1) // HALF]:
                                weigh(g, j - 1, WEIGH_AT[2 - (j - 1) // HALF].index(slot))
                            if j == TILES - 2 and slot == 7 and follows:
                                turn_tops(plan, ("tops", hg), g + 1)

            def tops_of_last(b):
                k = middle + (MIDDLE_USES * (b - 1)) - 1 if isinstance(b, int) else middle - 1
                bank, before = k % 2, k // 2 + (0 if isinstance(b, int) else (b - 1) * (MIDDLE_USES // 2))
                wait(pe, read[bank], before + 1)

            turns(pe, pe_turn, None)
            g = BATCH * GROUPS - 1
            weigh(g, TILES - 1, 0)
            ends = last_plan_uses()
            for bank in range(2):
                pe.wait_ge(read[bank], ends[bank])
            for c in range(2):
                pe.wait_ge(oT_ready, 2 * g + c + 1)
                turn_four(narrow[c], lambda k: oT[:, (4 * c + k) * P:(4 * c + k + 1) * P], 4, closing)
            pe.wait_ge(closing_read, 2)
            for t in range(TILES + 1):
                if t < TILES:
                    if t >= 2:
                        pe.wait_ge(closing_aT, t - 1)
                    turn_four(narrow[t % 2], lambda c: acts[:, t, c * P:(c + 1) * P], DC, closing_turned)
                if t:
                    pe.wait_ge(closing_aT, t)
                    if t >= 3:
                        pe.wait_ge(x_done, (BATCH - 1) * TILES + t - 2)
                    for c in range(DC):
                        i = pe.matmul(query_banks[(t - 1) % 2][:, 0:D], aT[:, (t - 1) % 2, c, :], w_o[:, c, :], start=(c == 0), stop=(c == DC - 1))
                    i.then_inc(closing_y, 1)


def chunks(a):
    return a.reshape(-1, P, a.shape[-1]).transpose(1, 0, 2)


def rope_tables():
    half = 32
    pos = np.arange(SEQ, dtype=np.float32)
    freq = np.float32(10000.0) ** (-np.arange(half, dtype=np.float32) / np.float32(half))
    angle = pos[:, None] * freq[None, :]
    sin, cos = np.sin(angle), np.cos(angle)
    ga = np.stack([np.concatenate([cos, cos], 1), np.concatenate([-sin, sin], 1)])
    ga = ga.reshape(2, TILES, P, 2 * half).transpose(2, 0, 1, 3)
    d = 16
    freq = np.float32(1.0) / np.float32(10000.0) ** (np.arange(0, d, 2, dtype=np.float32) / np.float32(d))
    angle = pos[:, None] * freq[None, :]
    ca = np.stack([np.cos(angle), np.sin(angle)])
    ca = ca.reshape(2, TILES, P, d // 2).transpose(2, 0, 1, 3)
    return ga.astype(np.float32), ca.astype(np.float32)


def lay(i):
    ga_rope, ca_rope = rope_tables()
    order = [1, 0, 2, 3]
    heads = np.stack([i["L0_attn_gamma"][order], i["L0_attn_beta"][order]])
    tok = np.arange(P)
    dist = np.minimum(np.abs(tok[:, None] - tok[None, :]), 32)
    same = tok[:, None] // 64 == tok[None, :] // 64
    out = {
        "ident": np.eye(P, dtype=np.float32),
        "ga_w": chunks(np.concatenate([i["L0_attn_Wv"], i["L0_attn_Wg"], i["L0_attn_Wqk"]], 0).T),
        "ga_wo": chunks(i["L0_attn_Wo"].T),
        "ga_rope": ga_rope,
        "ga_heads": np.broadcast_to(heads, (P, 2, 4, 64)),
        "ga_bias": np.where(same, i["L0_attn_pos_emb"][dist], np.float32(-1e30)),
        "ga_ln1": np.stack([i["L0_attn_ln1_w"].reshape(2, P).T, i["L0_attn_ln1_b"].reshape(2, P).T], 1),
        "ga_ln2": np.broadcast_to(np.stack([i["L0_attn_ln2_w"], i["L0_attn_ln2_b"]]), (P, 2, 256)),
        "ga_brow": np.concatenate([i["L0_attn_bv"], i["L0_attn_bg"], i["L0_attn_bqk"], i["L0_attn_bo"]]).reshape(64, -1),
    }
    out.update(lay_rest(i, ca_rope))
    return {k: np.ascontiguousarray(v) for k, v in out.items()}


def lay_rest(i, ca_rope):
    tok = np.arange(P)
    misc = np.concatenate([tok[:, None] < tok[None, :]] + [np.broadcast_to(r, (P, r.size)) for r in
                          (np.arange(EXPERTS), P * np.arange(ALL_TILES), np.arange(ROUTED))], 1).astype(np.float32)
    up0 = np.concatenate([i["L0_ffn_w1"], i["L0_ffn_w3"]], 2)
    up1 = np.concatenate([i["L1_ffn_sWu"][None], i["L1_ffn_Wu"]], 0).transpose(0, 2, 1)
    down1 = np.concatenate([i["L1_ffn_sWd"][None], i["L1_ffn_Wd"]], 0).transpose(0, 2, 1)
    each = lambda w: np.stack([chunks(e) for e in w])
    kqv = i["L1_attn_W_KQV"].T
    return {
        "ca_w": chunks(kqv), "ca_wo": chunks(i["L1_attn_W_O"].T), "ca_rope": ca_rope,
        "ca_mask": np.where(tok[None, :] > tok[:, None], np.float32(-1e30), np.float32(0)),
        "moe_misc": misc,
        "moe_slots": np.concatenate([np.broadcast_to(tok, (P, P)), P * np.arange(ALL_TILES) + tok[:, None]], 1).astype(np.float32),
        "m0_gate": chunks(i["L0_ffn_gate_w"].T), "m0_up": each(up0), "m0_down": each(i["L0_ffn_w2"]),
        "m1_gate": chunks(i["L1_ffn_gate_w"].T), "m1_up": each(up1), "m1_down": each(down1),
        "m1_gbias": np.broadcast_to(i["L1_ffn_gate_bias"], (P, EXPERTS)),
        "m1_bias": np.concatenate([np.concatenate([i["L1_ffn_sbu"][None], i["L1_ffn_bu"]], 0),
                                   np.concatenate([i["L1_ffn_sbd"][None], i["L1_ffn_bd"]], 0)], 1),
    }


def program(nc, io, out):
    at_most = (ROUTED + ALL_TILES) * P
    rows = nc.dram_tensor("expert_rows", [at_most, D], F32).ap()
    results = nc.dram_tensor("expert_results", [at_most, D], F32).ap()
    between = [nc.dram_tensor(f"x_{k}", [BATCH, SEQ, D], F32).ap() for k in range(3)]
    gated_attention(nc, io, io["x"], between[0], rows[0:ROUTED * P, :])
    experts(nc, io, between[0], between[1], rows, results, 0)
    causal_attention(nc, io, between[1], between[2])
    experts(nc, io, between[2], out, rows, results, 1)


def kernel(**inputs):
    import concourse.bacc as bacc
    from concourse.bass_utils import run_bass_kernel_spmd

    nc = bacc.Bacc("TRN2", target_bir_lowering=False, num_devices=1)
    arrays = lay({k: np.asarray(v) for k, v in inputs.items()})
    arrays["x"] = np.ascontiguousarray(inputs["L0_attn_x"])
    io = {k: nc.dram_tensor(f"in_{k}", a.shape, mybir.dt.from_np(a.dtype), kind="ExternalInput").ap() for k, a in arrays.items()}
    out = nc.dram_tensor("out", [BATCH, SEQ, D], F32, kind="ExternalOutput").ap()
    program(nc, io, out)
    r = run_bass_kernel_spmd(nc, [{f"in_{k}": a for k, a in arrays.items()}], core_ids=[0])
    return r.results[0]["out"]
```
